# Optimizing a Trainium2 kernel written in Bass

```python
import numpy as np
import jax
import jax.numpy as jnp

def _softmax(x, axis=-1):
    return jax.nn.softmax(x, axis=axis)

def _gelu(x):
    return jax.nn.gelu(x, approximate=True)

def _silu(x):
    return jax.nn.silu(x)

def _sigmoid(x):
    return jax.nn.sigmoid(x)

def _layernorm(x, axis=-1, eps=1e-05):
    m = jnp.mean(x, axis=axis, keepdims=True)
    v = jnp.var(x, axis=axis, keepdims=True)
    return (x - m) / jnp.sqrt(v + eps)

def _scatter_add(tgt, idx, src, axis=0):
    return tgt.at[idx].add(src)

def _segment_sum(src, seg, n):
    return jax.ops.segment_sum(src, seg, n)
kernel_name = 'mk_flamingo_gated_d2_seqx_r4_53ba38'

def setup_inputs(seed: int=0):
    np.random.seed(seed)
    _w = jnp.asarray

    def _rec_inputs():
        import jax
        import jax.numpy as jnp
        _rk = jax.random.key(seed)
        x = -0.0002928 + 1 * jax.random.normal(jax.random.fold_in(_rk, 1), (8, 256, 512), jnp.float32)
        _lenS = 256 - jax.random.randint(jax.random.fold_in(_rk, 7), (8,), 0, max(1, 256 // 4) + 1, jnp.int32)
        _lenS2 = 256 - jax.random.randint(jax.random.fold_in(_rk, 8), (8,), 0, max(1, 256 // 4) + 1, jnp.int32)
        _ctx_2048P = jax.random.normal(jax.random.fold_in(_rk, 11), (8, 16, 512), jnp.float32)
        _ctx_2048c = jax.random.dirichlet(jax.random.fold_in(_rk, 511), 0.3 * jnp.ones((16,), jnp.float32), (8, 256))
        _ctx_2048t = jnp.einsum('bsk,bkd->bsd', _ctx_2048c, _ctx_2048P)
        _ctx_2048t = _ctx_2048t * jax.lax.rsqrt(jnp.mean(jnp.square(_ctx_2048t)) + 1e-12) * 0.953939
        ctx_2048 = -1.39393e-06 + 0.999914 * (_ctx_2048t + 0.3 * jax.random.normal(jax.random.fold_in(_rk, 611), (8, 256, 512), jnp.float32))
        _validS = jnp.arange(256)[None, :] < _lenS[:, None]
        _validS2 = jnp.arange(256)[None, :] < _lenS2[:, None]
        _causal = jnp.tril(jnp.ones((256, 256), dtype=bool))
        mask_Bx1x2048_fk1 = jnp.where(jnp.ones((8, 1, 512), dtype=bool), 1.0, 0.0).astype(jnp.float32)
        _g = jax.random.normal(jax.random.fold_in(_rk, 9001), (2, 2), jnp.float32)
        _g = jnp.sign(_g) * jnp.maximum(jnp.abs(_g), 1.0) + (_g == 0) * 1.0
        g_xattn = _g[0]
        g_ffn = _g[1]
        return (x, ctx_2048, mask_Bx1x2048_fk1, g_xattn, g_ffn)
    x, ctx_2048, mask_Bx1x2048_fk1, g_xattn, g_ffn = _rec_inputs()

    def _L0_xattn_setup():
        import math
        import jax, jax.numpy as jnp
        import numpy as np
        SIZE = 256
        HEADS = 16
        HEAD_DIM = SIZE // HEADS
        B, T, S = (2, 512, 512)
        NEG = 1000000.0
        key = jax.random.key(seed)
        ks = jax.random.split(key, 10)
        target = jax.random.normal(ks[0], (B, SIZE, T), dtype=jnp.float32)
        source = jax.random.normal(ks[1], (B, SIZE, S), dtype=jnp.float32)
        target_mask = (jax.random.uniform(ks[2], (B, 1, T)) > 0.1).astype(jnp.float32)
        source_mask = (jax.random.uniform(ks[3], (B, 1, S)) > 0.1).astype(jnp.float32)
        scale = 1.0 / math.sqrt(SIZE)
        Wq = jax.random.normal(ks[4], (SIZE, SIZE), dtype=jnp.float32) * scale
        Wk = jax.random.normal(ks[5], (SIZE, SIZE), dtype=jnp.float32) * scale
        Wv = jax.random.normal(ks[6], (SIZE, SIZE), dtype=jnp.float32) * scale
        bq = jax.random.normal(ks[7], (SIZE,), dtype=jnp.float32) * 0.01
        bk = jax.random.normal(ks[8], (SIZE,), dtype=jnp.float32) * 0.01
        bv = jax.random.normal(ks[9], (SIZE,), dtype=jnp.float32) * 0.01
        return {'target': target, 'source': source, 'target_mask': target_mask, 'source_mask': source_mask, 'Wq': Wq, 'bq': bq, 'Wk': Wk, 'bk': bk, 'Wv': Wv, 'bv': bv}
    _L0_xattn_all = _L0_xattn_setup()
    _L0_xattn_in = {k: v for k, v in _L0_xattn_all.items() if k in ('Wq', 'bq', 'Wk', 'bk', 'Wv', 'bv')}
    del _L0_xattn_all

    def _L0_ffn_setup():
        import jax, jax.numpy as jnp
        import numpy as np
        E = 64
        K = 8
        H = 512
        I = 192
        CAP = 128

        def _moe(hidden_states, gate_w, wg, wu, wd):
            B, S, Hd = hidden_states.shape
            x = hidden_states.reshape(-1, Hd)
            T = x.shape[0]
            logits = x @ gate_w.T
            probs = jax.nn.softmax(logits.astype(jnp.float32), axis=-1)
            w, sel = jax.lax.top_k(probs, K)
            w = w / jnp.sum(w, axis=-1, keepdims=True)
            w = w.astype(x.dtype)
            eid = sel.reshape(-1)
            tok = jnp.repeat(jnp.arange(T), K)
            oh = jax.nn.one_hot(eid, E, dtype=jnp.int32)
            pos = jnp.sum(jnp.cumsum(oh, axis=0) * oh, axis=-1) - 1
            valid = pos < CAP
            slot = jnp.where(valid, pos, CAP)
            xin = jnp.zeros((E, CAP + 1, Hd), x.dtype).at[eid, slot].set(x[tok])
            inp = xin[:, :CAP]
            h = jax.nn.silu(jnp.einsum('ech,ehi->eci', inp, wg)) * jnp.einsum('ech,ehi->eci', inp, wu)
            out = jnp.einsum('eci,eih->ech', h, wd)
            out_pad = jnp.concatenate([out, jnp.zeros((E, 1, Hd), out.dtype)], axis=1)
            g = out_pad[eid, slot] * (w.reshape(-1) * valid.astype(w.dtype))[:, None]
            y = jnp.zeros((T, Hd), x.dtype).at[tok].add(g)
            return y.reshape(B, S, Hd)
        key = jax.random.key(seed)
        k1, k2, k3, k4, k5 = jax.random.split(key, 5)
        hidden_states = jax.random.normal(k1, (1, 512, H), dtype=jnp.float32)
        gate_w = jax.random.normal(k2, (E, H), dtype=jnp.float32) * 0.02
        wg = jax.random.normal(k3, (E, H, I), dtype=jnp.float32) * 0.02
        wu = jax.random.normal(k4, (E, H, I), dtype=jnp.float32) * 0.02
        wd = jax.random.normal(k5, (E, I, H), dtype=jnp.float32) * 0.02
        return {'hidden_states': hidden_states, 'gate_w': gate_w, 'wg': wg, 'wu': wu, 'wd': wd}
    _L0_ffn_all = _L0_ffn_setup()
    _L0_ffn_in = {k: v for k, v in _L0_ffn_all.items() if k in ('gate_w', 'wg', 'wu', 'wd')}
    del _L0_ffn_all

    def _L1_xattn_setup():
        import jax, jax.numpy as jnp
        import numpy as np
        B, S, E, NH = (2, 256, 512, 16)
        DH = E // NH
        EPS = 1e-06

        def _mlstm_forward(q, k, v, Wi, bi, Wf, bf, ln_scale):
            b, s, e = q.shape
            nh = Wi.shape[1]
            dh = e // nh
            x = jnp.concatenate([q, k, v], axis=-1)
            ig = (x @ Wi + bi).transpose(0, 2, 1)[..., None]
            fg = (x @ Wf + bf).transpose(0, 2, 1)[..., None]
            split = lambda t: t.reshape(b, s, nh, dh).transpose(0, 2, 1, 3)
            qh, kh, vh = (split(q), split(k), split(v))
            log_f = jax.nn.log_sigmoid(fg)
            log_f_cum = jnp.concatenate([jnp.zeros((b, nh, 1, 1), q.dtype), jnp.cumsum(log_f, axis=2)], axis=2)
            fg_mat = log_f_cum - jnp.transpose(log_f_cum, (0, 1, 3, 2))
            ltr = jnp.tril(jnp.ones((s, s), dtype=bool))
            log_fg = jnp.where(ltr, fg_mat[:, :, 1:, 1:], -jnp.inf)
            log_D = log_fg + jnp.transpose(ig, (0, 1, 3, 2))
            max_log_D = jnp.max(log_D, axis=-1, keepdims=True)
            D = jnp.exp(log_D - max_log_D)
            qk = jnp.einsum('bhsd,bhtd->bhst', qh, kh) / jnp.sqrt(jnp.asarray(dh, q.dtype))
            C = qk * D
            normalizer = jnp.maximum(jnp.abs(C.sum(-1, keepdims=True)), jnp.exp(-max_log_D))
            Cn = C / (normalizer + EPS)
            h = jnp.einsum('bhst,bhtd->bhsd', Cn, vh)
            mu = h.mean(-1, keepdims=True)
            var = ((h - mu) ** 2).mean(-1, keepdims=True)
            hn = (h - mu) * jax.lax.rsqrt(var + EPS)
            hn = hn * ln_scale.reshape(1, nh, 1, dh)
            return hn.transpose(0, 2, 1, 3).reshape(b, s, e)
        key = jax.random.key(seed)
        ks = jax.random.split(key, 6)
        q = jax.random.normal(ks[0], (B, S, E), dtype=jnp.float32)
        k = jax.random.normal(ks[1], (B, S, E), dtype=jnp.float32)
        v = jax.random.normal(ks[2], (B, S, E), dtype=jnp.float32)
        Wi = jax.random.normal(ks[3], (3 * E, NH), dtype=jnp.float32) * 0.02
        bi = jax.random.normal(ks[4], (NH,), dtype=jnp.float32) * 0.1
        Wf = jax.random.normal(ks[5], (3 * E, NH), dtype=jnp.float32) * 0.02
        bf = jnp.linspace(3.0, 6.0, NH, dtype=jnp.float32)
        ln_scale = jnp.ones((E,), dtype=jnp.float32)
        return {'q': q, 'k': k, 'v': v, 'Wi': Wi, 'bi': bi, 'Wf': Wf, 'bf': bf, 'ln_scale': ln_scale}
    _L1_xattn_all = _L1_xattn_setup()
    _L1_xattn_in = {k: v for k, v in _L1_xattn_all.items() if k in ('Wi', 'bi', 'Wf', 'bf', 'ln_scale')}
    del _L1_xattn_all

    def _L1_ffn_setup():
        import jax, jax.numpy as jnp
        import numpy as np
        H = 512
        I = 2048
        MI = 256
        E = 8
        K = 2
        B, S = (2, 256)
        EPS = 1e-06
        ROOT = H ** (-0.5)

        def _rms(x, w=None, eps=EPS):
            ms = jnp.mean(x * x, axis=-1, keepdims=True) + eps
            y = x * jax.lax.rsqrt(ms)
            return y * w if w is not None else y

        def _gelu_tanh(x):
            return jax.nn.gelu(x, approximate=True)
        key = jax.random.key(seed)
        ks = jax.random.split(key, 10)
        s = 0.02
        return {'hidden_states': jax.random.normal(ks[0], (B, S, H), jnp.float32), 'rn_pre1': jnp.ones((H,), jnp.float32), 'rn_pre2': jnp.ones((H,), jnp.float32), 'rn_post1': jnp.ones((H,), jnp.float32), 'rn_post2': jnp.ones((H,), jnp.float32), 'rn_post': jnp.ones((H,), jnp.float32), 'w_gate': jax.random.normal(ks[1], (H, I), jnp.float32) * s, 'w_up': jax.random.normal(ks[2], (H, I), jnp.float32) * s, 'w_down': jax.random.normal(ks[3], (I, H), jnp.float32) * s, 'router_w': jax.random.normal(ks[4], (H, E), jnp.float32) * s, 'router_scale': jnp.ones((H,), jnp.float32), 'per_expert_scale': jnp.ones((E,), jnp.float32), 'we_gate': jax.random.normal(ks[5], (E, H, MI), jnp.float32) * s, 'we_up': jax.random.normal(ks[6], (E, H, MI), jnp.float32) * s, 'we_down': jax.random.normal(ks[7], (E, MI, H), jnp.float32) * s}
    _L1_ffn_all = _L1_ffn_setup()
    _L1_ffn_in = {k: v for k, v in _L1_ffn_all.items() if k in ('rn_pre1', 'rn_pre2', 'rn_post1', 'rn_post2', 'rn_post', 'w_gate', 'w_up', 'w_down', 'router_w', 'router_scale', 'per_expert_scale', 'we_gate', 'we_up', 'we_down')}
    del _L1_ffn_all
    return {'x': x, 'ctx_2048': ctx_2048, 'mask_Bx1x2048_fk1': mask_Bx1x2048_fk1, 'g_xattn': g_xattn, 'g_ffn': g_ffn, 'L0_xattn_Wq': _L0_xattn_in['Wq'], 'L0_xattn_bq': _L0_xattn_in['bq'], 'L0_xattn_Wk': _L0_xattn_in['Wk'], 'L0_xattn_bk': _L0_xattn_in['bk'], 'L0_xattn_Wv': _L0_xattn_in['Wv'], 'L0_xattn_bv': _L0_xattn_in['bv'], 'L0_ffn_gate_w': _L0_ffn_in['gate_w'], 'L0_ffn_wg': _L0_ffn_in['wg'], 'L0_ffn_wu': _L0_ffn_in['wu'], 'L0_ffn_wd': _L0_ffn_in['wd'], 'L1_xattn_Wi': _L1_xattn_in['Wi'], 'L1_xattn_bi': _L1_xattn_in['bi'], 'L1_xattn_Wf': _L1_xattn_in['Wf'], 'L1_xattn_bf': _L1_xattn_in['bf'], 'L1_xattn_ln_scale': _L1_xattn_in['ln_scale'], 'L1_ffn_rn_pre1': _L1_ffn_in['rn_pre1'], 'L1_ffn_rn_pre2': _L1_ffn_in['rn_pre2'], 'L1_ffn_rn_post1': _L1_ffn_in['rn_post1'], 'L1_ffn_rn_post2': _L1_ffn_in['rn_post2'], 'L1_ffn_rn_post': _L1_ffn_in['rn_post'], 'L1_ffn_w_gate': _L1_ffn_in['w_gate'], 'L1_ffn_w_up': _L1_ffn_in['w_up'], 'L1_ffn_w_down': _L1_ffn_in['w_down'], 'L1_ffn_router_w': _L1_ffn_in['router_w'], 'L1_ffn_router_scale': _L1_ffn_in['router_scale'], 'L1_ffn_per_expert_scale': _L1_ffn_in['per_expert_scale'], 'L1_ffn_we_gate': _L1_ffn_in['we_gate'], 'L1_ffn_we_up': _L1_ffn_in['we_up'], 'L1_ffn_we_down': _L1_ffn_in['we_down']}

def reference(x, ctx_2048, mask_Bx1x2048_fk1, g_xattn, g_ffn, L0_xattn_Wq, L0_xattn_bq, L0_xattn_Wk, L0_xattn_bk, L0_xattn_Wv, L0_xattn_bv, L0_ffn_gate_w, L0_ffn_wg, L0_ffn_wu, L0_ffn_wd, L1_xattn_Wi, L1_xattn_bi, L1_xattn_Wf, L1_xattn_bf, L1_xattn_ln_scale, L1_ffn_rn_pre1, L1_ffn_rn_pre2, L1_ffn_rn_post1, L1_ffn_rn_post2, L1_ffn_rn_post, L1_ffn_w_gate, L1_ffn_w_up, L1_ffn_w_down, L1_ffn_router_w, L1_ffn_router_scale, L1_ffn_per_expert_scale, L1_ffn_we_gate, L1_ffn_we_up, L1_ffn_we_down):
    import jax
    import jax.numpy as jnp

    def _L0_xattn_ref(target, source, target_mask, source_mask, Wq, bq, Wk, bk, Wv, bv):
        import math
        import jax, jax.numpy as jnp
        import numpy as np
        SIZE = 256
        HEADS = 16
        HEAD_DIM = SIZE // HEADS
        B, T, S = (2, 512, 512)
        NEG = 1000000.0
        b, _, t = target.shape
        s = source.shape[-1]
        q = jnp.einsum('oc,bct->bot', Wq, target) + bq[None, :, None]
        k = jnp.einsum('oc,bcs->bos', Wk, source) + bk[None, :, None]
        v = jnp.einsum('oc,bcs->bos', Wv, source) + bv[None, :, None]
        q = q.reshape(b, HEADS, HEAD_DIM, t)
        k = k.reshape(b, HEADS, HEAD_DIM, s)
        v = v.reshape(b, HEADS, HEAD_DIM, s)
        dot = jnp.einsum('bhdt,bhds->bhts', q, k) / math.sqrt(HEAD_DIM)
        mask = target_mask[:, :, :, None] * source_mask[:, :, None, :]
        dot = mask * dot - (1.0 - mask) * NEG
        amap = jax.nn.softmax(dot, axis=-1) * mask
        out = jnp.einsum('bhts,bhds->bhdt', amap, v)
        return out.reshape(b, HEADS * HEAD_DIM, t)

    def _L0_ffn_ref(hidden_states, gate_w, wg, wu, wd):
        import jax, jax.numpy as jnp
        import numpy as np
        E = 64
        K = 8
        H = 512
        I = 192
        CAP = 128

        def _moe(hidden_states, gate_w, wg, wu, wd):
            B, S, Hd = hidden_states.shape
            x = hidden_states.reshape(-1, Hd)
            T = x.shape[0]
            logits = x @ gate_w.T
            probs = jax.nn.softmax(logits.astype(jnp.float32), axis=-1)
            w, sel = jax.lax.top_k(probs, K)
            w = w / jnp.sum(w, axis=-1, keepdims=True)
            w = w.astype(x.dtype)
            eid = sel.reshape(-1)
            tok = jnp.repeat(jnp.arange(T), K)
            oh = jax.nn.one_hot(eid, E, dtype=jnp.int32)
            pos = jnp.sum(jnp.cumsum(oh, axis=0) * oh, axis=-1) - 1
            valid = pos < CAP
            slot = jnp.where(valid, pos, CAP)
            xin = jnp.zeros((E, CAP + 1, Hd), x.dtype).at[eid, slot].set(x[tok])
            inp = xin[:, :CAP]
            h = jax.nn.silu(jnp.einsum('ech,ehi->eci', inp, wg)) * jnp.einsum('ech,ehi->eci', inp, wu)
            out = jnp.einsum('eci,eih->ech', h, wd)
            out_pad = jnp.concatenate([out, jnp.zeros((E, 1, Hd), out.dtype)], axis=1)
            g = out_pad[eid, slot] * (w.reshape(-1) * valid.astype(w.dtype))[:, None]
            y = jnp.zeros((T, Hd), x.dtype).at[tok].add(g)
            return y.reshape(B, S, Hd)
        return _moe(hidden_states, gate_w, wg, wu, wd)

    def _L1_xattn_ref(q, k, v, Wi, bi, Wf, bf, ln_scale):
        import jax, jax.numpy as jnp
        import numpy as np
        B, S, E, NH = (2, 256, 512, 16)
        DH = E // NH
        EPS = 1e-06

        def _mlstm_forward(q, k, v, Wi, bi, Wf, bf, ln_scale):
            b, s, e = q.shape
            nh = Wi.shape[1]
            dh = e // nh
            x = jnp.concatenate([q, k, v], axis=-1)
            ig = (x @ Wi + bi).transpose(0, 2, 1)[..., None]
            fg = (x @ Wf + bf).transpose(0, 2, 1)[..., None]
            split = lambda t: t.reshape(b, s, nh, dh).transpose(0, 2, 1, 3)
            qh, kh, vh = (split(q), split(k), split(v))
            log_f = jax.nn.log_sigmoid(fg)
            log_f_cum = jnp.concatenate([jnp.zeros((b, nh, 1, 1), q.dtype), jnp.cumsum(log_f, axis=2)], axis=2)
            fg_mat = log_f_cum - jnp.transpose(log_f_cum, (0, 1, 3, 2))
            ltr = jnp.tril(jnp.ones((s, s), dtype=bool))
            log_fg = jnp.where(ltr, fg_mat[:, :, 1:, 1:], -jnp.inf)
            log_D = log_fg + jnp.transpose(ig, (0, 1, 3, 2))
            max_log_D = jnp.max(log_D, axis=-1, keepdims=True)
            D = jnp.exp(log_D - max_log_D)
            qk = jnp.einsum('bhsd,bhtd->bhst', qh, kh) / jnp.sqrt(jnp.asarray(dh, q.dtype))
            C = qk * D
            normalizer = jnp.maximum(jnp.abs(C.sum(-1, keepdims=True)), jnp.exp(-max_log_D))
            Cn = C / (normalizer + EPS)
            h = jnp.einsum('bhst,bhtd->bhsd', Cn, vh)
            mu = h.mean(-1, keepdims=True)
            var = ((h - mu) ** 2).mean(-1, keepdims=True)
            hn = (h - mu) * jax.lax.rsqrt(var + EPS)
            hn = hn * ln_scale.reshape(1, nh, 1, dh)
            return hn.transpose(0, 2, 1, 3).reshape(b, s, e)
        return _mlstm_forward(q, k, v, Wi, bi, Wf, bf, ln_scale)

    def _L1_ffn_ref(hidden_states, rn_pre1, rn_pre2, rn_post1, rn_post2, rn_post, w_gate, w_up, w_down, router_w, router_scale, per_expert_scale, we_gate, we_up, we_down):
        import jax, jax.numpy as jnp
        import numpy as np
        H = 512
        I = 2048
        MI = 256
        E = 8
        K = 2
        B, S = (2, 256)
        EPS = 1e-06
        ROOT = H ** (-0.5)

        def _rms(x, w=None, eps=EPS):
            ms = jnp.mean(x * x, axis=-1, keepdims=True) + eps
            y = x * jax.lax.rsqrt(ms)
            return y * w if w is not None else y

        def _gelu_tanh(x):
            return jax.nn.gelu(x, approximate=True)
        b, s, h = hidden_states.shape
        T = b * s
        dense_in = _rms(hidden_states, rn_pre1)
        dense_out = _gelu_tanh(dense_in @ w_gate) * (dense_in @ w_up) @ w_down
        dense_out = _rms(dense_out, rn_post1)
        x = hidden_states.reshape(T, h)
        xr = _rms(x) * router_scale * ROOT
        router_logits = xr @ router_w
        probs = jax.nn.softmax(router_logits, axis=-1)
        top_w, top_i = jax.lax.top_k(probs, K)
        top_w = top_w / jnp.sum(top_w, axis=-1, keepdims=True)
        top_w = top_w * per_expert_scale[top_i]
        aff = jnp.zeros((T, E), x.dtype).at[jnp.arange(T)[:, None], top_i].set(top_w)
        moe_in = _rms(hidden_states, rn_pre2).reshape(T, h)
        g = jnp.einsum('th,ehm->tem', moe_in, we_gate)
        u = jnp.einsum('th,ehm->tem', moe_in, we_up)
        eo = jnp.einsum('tem,emh->teh', _gelu_tanh(g) * u, we_down)
        moe_out = jnp.einsum('te,teh->th', aff, eo).reshape(b, s, h)
        moe_out = _rms(moe_out, rn_post2)
        return _rms(dense_out + moe_out, rn_post)
    x = x + jnp.tanh(g_xattn[0]) * _L0_xattn_ref(_layernorm(x, axis=-1), ctx_2048, mask_Bx1x2048_fk1, mask_Bx1x2048_fk1, L0_xattn_Wq, L0_xattn_bq, L0_xattn_Wk, L0_xattn_bk, L0_xattn_Wv, L0_xattn_bv)
    x = x + jnp.tanh(g_ffn[0]) * _L0_ffn_ref(_layernorm(x, axis=-1), L0_ffn_gate_w, L0_ffn_wg, L0_ffn_wu, L0_ffn_wd)
    x = x + jnp.tanh(g_xattn[1]) * _L1_xattn_ref(_layernorm(x, axis=-1), ctx_2048, ctx_2048, L1_xattn_Wi, L1_xattn_bi, L1_xattn_Wf, L1_xattn_bf, L1_xattn_ln_scale)
    x = x + jnp.tanh(g_ffn[1]) * _L1_ffn_ref(_layernorm(x, axis=-1), L1_ffn_rn_pre1, L1_ffn_rn_pre2, L1_ffn_rn_post1, L1_ffn_rn_post2, L1_ffn_rn_post, L1_ffn_w_gate, L1_ffn_w_up, L1_ffn_w_down, L1_ffn_router_w, L1_ffn_router_scale, L1_ffn_per_expert_scale, L1_ffn_we_gate, L1_ffn_we_up, L1_ffn_we_down)
    return x

_drawn_inputs = setup_inputs


def setup_inputs(seed=0):
    import zlib

    import numpy as np

    out = dict(_drawn_inputs(seed))
    spreads = {'g_ffn': (-1.0, 0.2),
     'L1_xattn_ln_scale': (1.0, 0.2),
     'L1_ffn_rn_pre1': (1.0, 0.2),
     'L1_ffn_rn_pre2': (1.0, 0.2),
     'L1_ffn_rn_post1': (1.0, 0.2),
     'L1_ffn_rn_post2': (1.0, 0.2),
     'L1_ffn_rn_post': (1.0, 0.2),
     'L1_ffn_router_scale': (1.0, 0.2),
     'L1_ffn_per_expert_scale': (1.0, 0.2)}
    factors = {'L0_xattn_bq': 5.238, 'L0_xattn_bk': 64.0, 'L0_xattn_bv': 8.0, 'L1_xattn_bi': 59.447}
    for name, (base, spread) in spreads.items():
        noise = np.random.default_rng([zlib.crc32(name.encode()), seed]).standard_normal(out[name].shape)
        drawn = base * np.exp(spread * noise) if base else spread * noise
        out[name] = jnp.asarray(drawn.astype(out[name].dtype))
    for name, factor in factors.items():
        out[name] = (out[name] * factor).astype(out[name].dtype)
    return out
```

```python
import numpy as np
import concourse.bass as bass
from concourse import mybir
from contextlib import ExitStack

F32 = mybir.dt.float32
BF16 = mybir.dt.bfloat16
I32 = mybir.dt.int32
U32 = mybir.dt.uint32
ALU = mybir.AluOpType
ACT = mybir.ActivationFunctionType
AX = mybir.AxisListType

P = 128
B, C, T = 8, 256, 512
CT = C // P
NT = B * CT
NTOK = B * C
HC = T // P
NH = 16


class Chain:

    def __init__(self, eng, sem, base=0):
        self.eng, self.sem, self.base, self.n = eng, sem, base, 0

    def __call__(self, ins):
        self.n += 1
        ins.then_inc(self.sem, 1)
        self.eng.wait_ge(self.sem, self.base + self.n)


class Room:

    def __init__(self, nc, ctx, tag):
        self.nc, self.ctx, self.tag, self.sems = nc, ctx, tag, []
        ctx.callback(self.clear)

    def clear(self):
        if self.sems:
            self.nc.clear_and_free_semaphores(self.sems)
            self.nc.all_engine_barrier()

    def sb(self, name, shape, dt=F32):
        return self.ctx.enter_context(self.nc.sbuf_tensor(f"{self.tag}_{name}", shape, dt))

    def ps(self, name, shape, dt=F32):
        return self.ctx.enter_context(self.nc.psum_tensor(f"{self.tag}_{name}", shape, dt))

    def sem(self, name):
        self.sems.append(self.nc.alloc_semaphore(f"{self.tag}_{name}"))
        return self.sems[-1]

    def block(self):
        return self.ctx.enter_context(self.nc.Block())


def row_of(vector):
    n = vector.shape[0]
    return vector.rearrange("(a n) -> a n", a=1).broadcast_to([P, n])


def load_x(nc, x_dram, X):
    with ExitStack() as ctx:
        r = Room(nc, ctx, "ld")
        loaded = r.sem("loaded")
        block = r.block()

        @block.sync
        def _(sp):
            for i in range(NT):
                sp.dma_start(X[:, i, :], x_dram[i]).then_inc(loaded, 16)
            sp.wait_ge(loaded, 16 * NT)


def store_x(nc, out_dram, X):
    with ExitStack() as ctx:
        r = Room(nc, ctx, "st")
        stored = r.sem("stored")
        block = r.block()

        @block.sync
        def _(sp):
            for i in range(NT):
                sp.dma_start(out_dram[i], X[:, i, :]).then_inc(stored, 16)
            sp.wait_ge(stored, 16 * NT)


def constants(nc, K):
    with ExitStack() as ctx:
        r = Room(nc, ctx, "cst")
        filled = r.sem("filled")
        graw = r.sb("graw", [P, 4])
        gload = r.sem("gload")
        block = r.block()

        @block.gpsimd
        def _(pool):
            nc.gpsimd.memset(K["ident"][:], 0.0).then_inc(filled, 1)
            pool.wait_ge(filled, 1)
            nc.gpsimd.affine_select(out=K["ident"][:], in_=K["ident"][:], compare_op=ALU.not_equal, fill=1.0,
                                    base=0, pattern=[[-1, P]], channel_multiplier=1).then_inc(filled, 1)
            pool.wait_ge(filled, 2)

        @block.sync
        def _(sp):
            sp.dma_start(graw[:, 0:2], row_of(K["g_xattn"])).then_inc(gload, 16)
            sp.dma_start(graw[:, 2:4], row_of(K["g_ffn"])).then_inc(gload, 16)

        @block.scalar
        def _(act):
            act.wait_ge(gload, 32)
            nc.scalar.activation(K["gate"][:], graw[:], ACT.Tanh)


def row_stats(nc, X, tag, eps, rms, mean, rstd, second=None):
    with ExitStack() as ctx:
        r = Room(nc, ctx, tag)
        st = r.sb("bn", [P, NT, 6])
        ag = r.sb("ag", [P, NT, 2])
        v = r.sb("v", [P, NT])
        dv = r.sem("dv")
        root = r.sem("root")
        ready = r.sem("ready")
        block = r.block()

        @block.vector
        def _(dve):
            with dve.Fori(0, NT) as i:
                ins = nc.vector.bn_stats(st[:, i, :], X[:, i, :])
                ins.then_inc(dv, 1)
            dve.wait_ge(dv, NT)
            c = Chain(dve, dv, NT)
            for i in range(NT):
                ins = nc.vector.bn_aggr(ag[:, i, :], st[:, i, :])
            c(ins)
            c(nc.vector.tensor_copy(mean[:], ag[:, :, 0]))
            if rms:
                c(nc.vector.tensor_tensor(v[:], mean[:], mean[:], ALU.mult))
                c(nc.vector.scalar_tensor_tensor(out=v[:], in0=v[:], scalar=eps, in1=ag[:, :, 1],
                                                 op0=ALU.add, op1=ALU.add))
            elif second is not None:
                c(nc.vector.tensor_scalar(v[:], ag[:, :, 1], 1.0 + second, eps * second, ALU.mult, ALU.add))
            else:
                c(nc.vector.tensor_scalar(v[:], ag[:, :, 1], eps, None, ALU.add))
            dve.sem_inc(ready, 1)
            dve.wait_ge(root, 1)
            c(nc.vector.reciprocal(rstd[:], v[:]))

        @block.scalar
        def _(act):
            act.wait_ge(ready, 1)
            nc.scalar.activation(v[:], v[:], ACT.Sqrt).then_inc(root, 1)



HD = 16
GH = 4
NG = NH // GH
NN = B * NG
QROWS = ("h", "h", "m", "h", "l", "m")
KROWS = ("h", "m", "h", "l", "h", "m")
NEG = 1000000.0
MROW = 6 * HD
MAXROW = MROW + 9
NROW = MAXROW + 3
VW = HD + 1


def split3(dve, nc, chain, parts, rest, src):
    chain(nc.vector.tensor_copy(parts[0], src))
    chain(nc.vector.tensor_tensor(rest, src, parts[0], ALU.subtract))
    chain(nc.vector.tensor_copy(parts[1], rest))
    chain(nc.vector.tensor_tensor(rest, rest, parts[1], ALU.subtract))
    chain(nc.vector.tensor_copy(parts[2], rest))


def attention(nc, io, X, K, S):
    ident, gate = K["ident"], K["gate"]
    mask8 = io["mask"].rearrange("b a t -> (b a) t")
    with ExitStack() as outer:
        o = Room(nc, outer, "at")
        mean = o.sb("mean", [P, NT])
        rstd = o.sb("rstd", [P, NT])
        V = o.sb("V", [P, NN, HC * GH * VW])
        row_stats(nc, X, "at_st", 1e-5, False, mean, rstd)

        with ExitStack() as ctx:
            r = Room(nc, ctx, "mk")
            m = r.sb("m", [B, T])
            a = r.sb("a", [B, T])
            rest = r.sb("rest", [B, T])
            mp = r.sb("mp", [B, 3, T], BF16)
            ap = r.sb("ap", [B, 3, T], BF16)
            one = r.sb("one", [B, 3, T], BF16)
            loaded = r.sem("loaded")
            dv = r.sem("dv")
            split = r.sem("split")
            stored = r.sem("stored")
            block = r.block()

            @block.vector
            def _(dve):
                c = Chain(dve, dv)
                c(nc.vector.memset(one[:], 1.0))
                dve.wait_ge(loaded, 16)
                c(nc.vector.tensor_scalar(a[:], m[:], -1.0, NEG, ALU.add, ALU.mult))
                split3(dve, nc, c, [mp[:, j, :] for j in range(3)], rest[:], m[:])
                split3(dve, nc, c, [ap[:, j, :] for j in range(3)], rest[:], a[:])
                dve.sem_inc(split, 1)

            @block.sync
            def _(sp):
                sp.dma_start(m[:], mask8).then_inc(loaded, 16)
                sp.wait_ge(split, 1)
                n = 0
                part = {"h": 0, "m": 1, "l": 2}
                for rows, dst, src in ((QROWS, S["mq"], ap), (KROWS, S["mk"], mp)):
                    view = dst.rearrange("(b g) r t -> b g r t", g=NG)
                    for g in range(NG):
                        for k, w in enumerate(rows):
                            sp.dma_start(view[:, g, k, :], src[:, part[w], :]).then_inc(stored, 16)
                            n += 1
                        tail = one if dst is S["mq"] else ap
                        sp.dma_start(view[:, g, 6:9, :], tail[:]).then_inc(stored, 16)
                        n += 1
                        if dst is S["mk"]:
                            sp.dma_start(view[:, g, 9:12, :], one[:]).then_inc(stored, 16)
                            n += 1
                view = S["mrep"].rearrange("(b c) t -> b c t", c=CT)
                for ct in range(CT):
                    sp.dma_start(view[:, ct, :], m[:]).then_inc(stored, 16)
                    n += 1
                sp.wait_ge(stored, 16 * n)

        with ExitStack() as ctx:
            r = Room(nc, ctx, "pj")
            wraw = r.sb("wraw", [P, 3, CT, C])
            wT = r.sb("wT", [P, 3, CT, C])
            bcol = r.sb("bcol", [P, 2, CT])
            bvb = r.sb("bvb", [P, C])
            smc = r.sb("smc", [P, B, HC])
            tmb = r.sb("tmb", [P, 2, T])
            src = r.sb("src", [P, 2, CT, T])
            xn = r.sb("xn", [P, 2, CT, T])
            full = r.sb("full", [P, 2, T])
            rest = r.sb("rest", [P, 2, T])
            parts = r.sb("parts", [P, 2, 2, 3, T], BF16)
            vt = r.sb("vt", [P, 2, C])
            pt = r.ps("pt", [P, 2, 512])
            pq = r.ps("pq", [P, 2, 512])
            pv = r.ps("pv", [P, 2, 512])
            wload = r.sem("wload")
            transposed = r.sem("transposed")
            evacuated = r.sem("evacuated")
            in_loaded = [r.sem(f"in_loaded{u}") for u in range(2)]
            in_free = [r.sem(f"in_free{u}") for u in range(2)]
            src_free = [r.sem(f"src_free{u}") for u in range(2)]
            normed = r.sem("normed")
            projected = r.sem("projected")
            proj_free = r.sem("proj_free")
            vproj = r.sem("vproj")
            vfree = r.sem("vfree")
            vpart = r.sem("vpart")
            dv = r.sem("dv")
            split_done = [r.sem(f"split_done{u}") for u in range(2)]
            split_stored = [r.sem(f"split_stored{u}") for u in range(2)]
            block = r.block()
            ctx_v = io["ctx"].rearrange("b (c p) t -> b p c t", p=P)

            @block.sync
            def _(sp):
                for k, w in enumerate(("Wq", "Wk", "Wv")):
                    sp.dma_start(wraw[:, k, :, :], io[w].rearrange("(c p) n -> p c n", p=P)).then_inc(wload, 16)
                for k, w in enumerate(("bq", "bk")):
                    for c in range(CT):
                        sp.dma_start(bcol[:, k, c:c + 1], io[w].rearrange("(c p a) -> c p a", p=P, a=1)[c])\
                          .then_inc(wload, 16)
                sp.dma_start(bvb[:], row_of(io["bv"])).then_inc(wload, 16)
                for b in range(B):
                    for c in range(HC):
                        sp.dma_start(smc[:, b, c:c + 1],
                                     io["mask"][b, 0].rearrange("(c p a) -> c p a", p=P, a=1)[c]).then_inc(wload, 16)
                with sp.Fori(0, B // 2) as i:
                    for u in range(2):
                        b = 2 * i + u
                        sp.wait_ge(in_free[u], i + 1)
                        sp.wait_ge(src_free[u], i + 1)
                        sp.dma_start(src[:, u, :, :], ctx_v[b]).then_inc(in_loaded[u], 16)
                        sp.dma_start(tmb[:, u, :], mask8[bass.ds(b, 1)].broadcast_to([P, T])).then_inc(in_loaded[u], 16)

            @block.gpsimd
            def _(pool):
                for u in range(2):
                    pool.sem_inc(in_free[u], 1)
                    pool.sem_inc(src_free[u], 1)
                    pool.sem_inc(split_stored[u], 16)
                pool.sem_inc(proj_free, 2)
                pool.sem_inc(vfree, 2)

            qs_v = [S[k].rearrange("n j d h t -> n h d j t") for k in ("qs", "ks")]

            @block.scalar
            def _(act):
                with act.Fori(0, B) as b:
                    for ct in range(CT):
                        act.wait_ge(split_done[ct], b + 1)
                        for k in range(2):
                            for hh in range(8):
                                n = 4 * b + (ct * 8 + hh) // GH
                                act.dma_start(qs_v[k][n, hh % GH], parts[HD * hh:HD * hh + HD, ct, k, :, :])\
                                   .then_inc(split_stored[ct], 16)
                for ct in range(CT):
                    act.wait_ge(split_stored[ct], 256 * B + 16)

            @block.tensor
            def _(pe):
                pe.wait_ge(wload, 16 * (3 + 4 + 1 + B * HC))
                n = 0
                for k in range(3):
                    for co in range(CT):
                        if n >= 2:
                            pe.wait_ge(evacuated, n - 1)
                        for ci in range(CT):
                            last = nc.tensor.transpose(pt[:, n % 2, ci * P:ci * P + P],
                                                       wraw[:, k, co, ci * P:ci * P + P], ident[:])
                        last.then_inc(transposed, 1)
                        n += 1
                pe.wait_ge(evacuated, n)
                with pe.Fori(0, B // 2) as i:
                    for u in range(2):
                        b = 2 * i + u
                        pe.wait_ge(in_loaded[u], 32 * i + 32)
                        pe.wait_ge(normed, b + 1)
                        for ct in range(CT):
                            for k, rhs in enumerate((xn, src)):
                                pe.wait_ge(proj_free, 4 * b + 2 * ct + k + 1)
                                for c in range(CT):
                                    last = nc.tensor.matmul(pq[:, k, :], wT[:, k, c, ct * P:ct * P + P],
                                                            rhs[:, u, c, :], start=(c == 0), stop=(c == CT - 1))
                                last.then_inc(projected, 1)
                        for s in range(HC):
                            pe.wait_ge(vfree, 4 * b + s + 1)
                            for c in range(CT):
                                last = nc.tensor.matmul(pv[:, s % 2, 0:C], src[:, u, c, s * P:s * P + P],
                                                        wT[:, 2, c, :], start=(c == 0), stop=(c == CT - 1))
                            last.then_inc(vproj, 1)
                        pe.wait_ge(vfree, 4 * b + HC + 2)
                        pe.sem_inc(src_free[u], 1)

            @block.vector
            def _(dve):
                n = 0
                for k in range(3):
                    for co in range(CT):
                        dve.wait_ge(transposed, n + 1)
                        nc.vector.tensor_copy(wT[:, k, :, co * P:co * P + P],
                                              pt[:, n % 2, 0:CT * P].rearrange("p (c n) -> p c n", c=CT))\
                          .then_inc(evacuated, 1)
                        n += 1
                per = CT + CT * 2 * (2 + 5) + HC * 2
                first = Chain(dve, dv)
                first(nc.vector.memset(V[:], 1.0))
                with dve.Fori(0, B // 2) as i:
                    c = Chain(dve, dv, 1 + i * (2 * per))
                    for u in range(2):
                        b = 2 * i + u
                        for ct in range(CT):
                            tile = CT * b + ct
                            c(nc.vector.tensor_scalar(xn[:, u, ct, :], X[:, tile, :],
                                                      mean[:, bass.ds(tile, 1)], rstd[:, bass.ds(tile, 1)],
                                                      ALU.subtract, ALU.mult))
                        dve.sem_inc(normed, 1)
                        dve.wait_ge(in_loaded[u], 32 * i + 32)
                        for ct in range(CT):
                            dve.wait_ge(split_stored[ct], 256 * b + 16)
                            for k in range(2):
                                dve.wait_ge(projected, 4 * b + 2 * ct + k + 1)
                                c(nc.vector.tensor_scalar(full[:, k, :], pq[:, k, :], bcol[:, k, ct:ct + 1],
                                                          HD ** -0.5 if k == 0 else 1.0, ALU.add, ALU.mult))
                                dve.sem_inc(proj_free, 1)
                                c(nc.vector.tensor_tensor(full[:, k, :], full[:, k, :], tmb[:, u, :], ALU.mult))
                                split3(dve, nc, c, [parts[:, ct, k, j, :] for j in range(3)],
                                       rest[:, k, :], full[:, k, :])
                            dve.sem_inc(split_done[ct], 1)
                        dve.sem_inc(in_free[u], 1)
                        for s in range(HC):
                            dve.wait_ge(vproj, 4 * b + s + 1)
                            c(nc.vector.tensor_tensor(vt[:, s % 2, :], pv[:, s % 2, 0:C], bvb[:], ALU.add))
                            dve.sem_inc(vfree, 1)
                            dst = V[:, bass.ds(4 * b, NG), s * GH * VW:(s + 1) * GH * VW]\
                                .rearrange("p g (h w) -> p g h w", h=GH)[:, :, :, 0:HD]
                            c(nc.vector.tensor_scalar(
                                dst, vt[:, s % 2, :].rearrange("p (g h w) -> p g h w", g=NG, h=GH),
                                smc[:, bass.ds(b, 1), s:s + 1].rearrange("p a b -> p (a b)"), None, ALU.mult))
                    assert c.n == 2 * per

        attend(nc, io, X, K, S, V)


def attend(nc, io, X, K, S, V):
    ident, gate = K["ident"], K["gate"]
    with ExitStack() as ctx:
        r = Room(nc, ctx, "sm")
        Q = r.sb("Q", [P, 2, GH, T], BF16)
        Kk = r.sb("K", [P, 2, GH, T], BF16)
        negm = r.sb("negm", [P, 2, GH * HC])
        mrow = r.sb("mrow", [GH * HC, P])
        mrest = r.sb("mrest", [GH * HC, P])
        mparts = r.sb("mparts", [GH * HC, 2, 3, P], BF16)
        Pe = r.sb("P", [P, 4, 2, T])
        Vg = r.sb("Vg", [P, 2, HC, GH, 32])
        O = r.sb("O", [P, 2, T])
        rden = r.sb("rden", [P, T])
        On = r.sb("On", [P, 2, T])
        tmb = r.sb("tmb", [P, T])
        res = r.sb("res", [P, T])
        dsel = r.sb("dsel", [P, P])
        sel = r.sb("sel", [P, 2, P])
        ps_m = r.ps("ps_m", [P, 2, 512])
        ps_s = r.ps("ps_s", [P, 2, 2, 512])
        ps_o = r.ps("ps_o", [P, 512])
        ps_x = r.ps("ps_x", [P, 512])
        made = r.sem("made")
        stacked = [r.sem(f"stacked{u}") for u in range(2)]
        stack_free = [r.sem(f"stack_free{u}") for u in range(2)]
        m_scored = r.sem("m_scored")
        m_read = r.sem("m_read")
        m_turned = r.sem("m_turned")
        m_split = r.sem("m_split")
        m_stored = r.sem("m_stored")
        m_sent = r.sem("m_sent")
        m_rows = [r.sem(f"m_rows{u}") for u in range(2)]
        scored = r.sem("scored")
        exped = r.sem("exped")
        v_ready = r.sem("v_ready")
        valued = r.sem("valued")
        o_copied = r.sem("o_copied")
        den_out = r.sem("den_out")
        x_read = r.sem("x_read")
        o_normed = r.sem("o_normed")
        picked = r.sem("picked")
        tm_loaded = r.sem("tm_loaded")
        tm_free = r.sem("tm_free")
        added = r.sem("added")
        dv = r.sem("dv")
        apart = r.sem("apart")
        block = r.block()

        def schedule(eng, maxima, rest):
            maxima(0, 0, 0)
            with eng.Fori(0, NN // 2 - 1) as i:
                maxima(2 * i + 1, 1, i)
                rest(2 * i, 0, i)
                maxima(2 * i + 2, 0, i + 1)
                rest(2 * i + 1, 1, i)
            maxima(NN - 1, 1, NN // 2 - 1)
            rest(NN - 2, 0, NN // 2 - 1)
            rest(NN - 1, 1, NN // 2 - 1)

        @block.gpsimd
        def _(pool):
            nc.gpsimd.memset(dsel[:], 0.0).then_inc(made, 1)
            nc.gpsimd.memset(sel[:], 0.0).then_inc(made, 1)
            nc.gpsimd.memset(Vg[:], 0.0).then_inc(made, 1)
            pool.wait_ge(made, 3)
            v = dsel[:].rearrange("p (j d) -> p j d", j=GH)
            nc.gpsimd.affine_select(out=v, in_=v, compare_op=ALU.not_equal, fill=1.0, base=-HD,
                                    pattern=[[-32, GH], [0, 32]], channel_multiplier=1).then_inc(made, 1)
            for q in range(2):
                v = sel[:, q, 64 * q:64 * q + 64].rearrange("p (j d) -> p j d", j=GH)
                nc.gpsimd.affine_select(out=v, in_=v, compare_op=ALU.not_equal, fill=1.0, base=0,
                                        pattern=[[-32, GH], [-1, HD]], channel_multiplier=1).then_inc(made, 1)
            for u in range(2):
                pool.sem_inc(stack_free[u], 1)
            for s, k in ((m_read, 1), (m_sent, 2), (exped, 2), (valued, 2), (o_copied, 1), (x_read, 1),
                         (o_normed, 2), (tm_free, 1)):
                pool.sem_inc(s, k)

            def maxima(n, u, i):
                pool.wait_ge(m_split, n + 1)
                pool.sem_inc(apart, 1)
                pool.dma_start(S["mx"][u].rearrange("j k p -> k j p"), mparts[:, u, :, :]).then_inc(m_stored, 16)
                pool.wait_ge(m_stored, 16 * n + 16)
                pool.sem_inc(m_sent, 1)
                pool.dma_start(Q[MAXROW:NROW, u, :, :].rearrange("p h t -> p (h t)"),
                               S["mx"][u].rearrange("j k p -> j (k p)")).then_inc(m_rows[u], 16)

            def rest(n, u, i):
                if u == 0:
                    pool.wait_ge(tm_free, i + 1)
                    pool.sem_inc(apart, 1)
                    pool.dma_start(tmb[:], S["mrep"][bass.ds(i, 1)].broadcast_to([P, T])).then_inc(tm_loaded, 16)

            schedule(pool, maxima, rest)

        @block.sync
        def _(sp):
            with sp.Fori(0, NN // 2) as i:
                for u in range(2):
                    n = 2 * i + u
                    sp.wait_ge(stack_free[u], i + 1)
                    for j in range(6):
                        for dst, name, rows in ((Q, "qs", QROWS), (Kk, "ks", KROWS)):
                            part = {"h": 0, "m": 1, "l": 2}[rows[j]]
                            sp.dma_start(dst[HD * j:HD * j + HD, u, :, :], S[name][n, part]).then_inc(stacked[u], 16)
                    for h in range(GH):
                        sp.dma_start(Q[MROW:MROW + 9, u, h, :], S["mq"][n]).then_inc(stacked[u], 16)
                        sp.dma_start(Kk[MROW:MROW + 12, u, h, :], S["mk"][n]).then_inc(stacked[u], 16)

        STACK = 16 * (12 + 2 * GH)
        READS = GH * HC + 1

        @block.tensor
        def _(pe):
            pe.wait_ge(made, 6)

            def maxima(n, u, i):
                pe.wait_ge(stacked[u], STACK * i + STACK)
                for h in range(GH):
                    for t in range(HC):
                        k = h * HC + t
                        pe.wait_ge(m_read, READS * n + max(k - 1, 0) + 1)
                        nc.tensor.matmul(ps_m[:, k % 2, :], Q[0:MAXROW, u, h, t * P:t * P + P],
                                         Kk[0:MAXROW, u, h, :], start=True, stop=True).then_inc(m_scored, 1)
                pe.wait_ge(m_read, READS * n + GH * HC + 1)
                nc.tensor.transpose(ps_m[0:GH * HC, 0, 0:P], negm[:, u, :], ident[:]).then_inc(m_turned, 1)

            def values(n, u, s):
                pe.wait_ge(exped, 8 * n + 2 * s + 4)
                for h in range(GH):
                    last = nc.tensor.matmul(ps_o[32 * h:32 * h + 32, :], Vg[:, u, s, h, :],
                                            Pe[:, 2 * (s % 2) + h // 2, h % 2, :],
                                            start=(s == 0), stop=(s == HC - 1), skip_group_check=True)
                last.then_inc(valued, 1)

            def rest(n, u, i):
                pe.wait_ge(m_rows[u], 16 * i + 16)
                pe.wait_ge(v_ready, n + 1)
                for s in range(HC):
                    for hp in range(2):
                        pe.wait_ge(exped, 8 * n + 2 * s + hp + 1)
                        for h in range(2):
                            last = nc.tensor.matmul(ps_s[:, hp, h, :],
                                                    Kk[0:NROW, u, 2 * hp + h, s * P:s * P + P],
                                                    Q[0:NROW, u, 2 * hp + h, :], start=True, stop=True)
                        last.then_inc(scored, 1)
                    if s == 0:
                        pe.wait_ge(o_copied, n + 1)
                    else:
                        values(n, u, s - 1)
                values(n, u, HC - 1)
                pe.sem_inc(stack_free[u], 1)
                pe.wait_ge(o_copied, n + 2)
                pe.wait_ge(x_read, 3 * i + u + 1)
                nc.tensor.matmul(ps_x[:], dsel[:], O[:, u, :], start=True, stop=True).then_inc(den_out, 1)
                if u == 1:
                    pe.wait_ge(o_normed, n + 3)
                    nc.tensor.matmul(ps_x[:], sel[:, 0, :], On[:, 0, :], start=True, stop=False)
                    nc.tensor.matmul(ps_x[:], sel[:, 1, :], On[:, 1, :], start=False, stop=True).then_inc(picked, 1)

            schedule(pe, maxima, rest)

        @block.scalar
        def _(act):
            def maxima(n, u, i):
                return

            def rest(n, u, i):
                for s in range(HC):
                    act.wait_ge(valued, 4 * n + s + 1)
                    for hp in range(2):
                        act.wait_ge(scored, 8 * n + 2 * s + hp + 1)
                        nc.scalar.activation(Pe[:, 2 * (s % 2) + hp, :, :], ps_s[:, hp, :, :], ACT.Exp)\
                          .then_inc(exped, 1)
                act.wait_ge(valued, 4 * n + HC + 2)
                act.wait_ge(o_normed, n + 1)
                nc.scalar.activation(O[:, u, :], ps_o[:], ACT.Copy).then_inc(o_copied, 1)

            schedule(act, maxima, rest)

        @block.vector
        def _(dve):
            dve.wait_ge(made, 6)

            def maxima(n, u, i):
                for k in range(GH * HC):
                    dve.wait_ge(m_scored, GH * HC * n + k + 1)
                    nc.vector.tensor_reduce(negm[:, u, k:k + 1], ps_m[:, k % 2, :], AX.X, ALU.max, negate=True)\
                      .then_inc(m_read, 1)
                nc.vector.tensor_copy(Vg[:, u, :, :, 0:VW],
                                      V[:, bass.ds(n, 1), :].rearrange("p a (s h w) -> p (a s) h w", s=HC, h=GH))\
                  .then_inc(v_ready, 1)
                dve.wait_ge(m_turned, n + 1)
                nc.vector.tensor_copy(mrow[:], ps_m[0:GH * HC, 0, 0:P]).then_inc(m_read, 1)
                dve.wait_ge(m_read, READS * n + READS + 1)
                dve.wait_ge(m_sent, n + 1)
                c = Chain(dve, dv, 4 * n)
                mp = [mparts[:, u, j, :] for j in range(3)]
                c(nc.vector.tensor_copy(mp[0], mrow[:]))
                c(nc.vector.tensor_tensor(mrest[:], mrow[:], mp[0], ALU.subtract))
                c(nc.vector.tensor_copy(mp[1], mrest[:]))
                c(nc.vector.tensor_tensor(mp[2], mrest[:], mp[1], ALU.subtract))
                dve.sem_inc(m_split, 1)

            def rest(n, u, i):
                dve.wait_ge(den_out, n + 1)
                nc.vector.reciprocal(rden[:], ps_x[:]).then_inc(x_read, 1)
                dve.wait_ge(x_read, 3 * i + u + 2)
                nc.vector.tensor_tensor(On[:, u, :], O[:, u, :], rden[:], ALU.mult).then_inc(o_normed, 1)
                dve.wait_ge(o_normed, n + 3)
                if u == 1:
                    dve.wait_ge(picked, i + 1)
                    dve.wait_ge(tm_loaded, 16 * i + 16)
                    nc.vector.scalar_tensor_tensor(out=res[:], in0=ps_x[:], scalar=gate[:, 0:1], in1=tmb[:],
                                                   op0=ALU.mult, op1=ALU.mult).then_inc(x_read, 1)
                    dve.wait_ge(x_read, 3 * i + 4)
                    dve.sem_inc(tm_free, 1)
                    x = X[:, bass.ds(i, 1), :].rearrange("p a t -> p (a t)")
                    nc.vector.tensor_tensor(x, x, res[:], ALU.add).then_inc(added, 1)
                    dve.wait_ge(added, i + 1)

            schedule(dve, maxima, rest)



BIG = 1048576.0
MAGIC = 12582912.0


def route(nc, io, X, K, S, tag, E, TOP, logit_w, mean, rstd, table, slots, dense=None, scale=None, owner=None):
    ident = K["ident"]
    per_tile = owner is None
    with ExitStack() as ctx:
        r = Room(nc, ctx, tag)
        wraw = r.sb("wraw", [P, HC, E])
        grow = r.sb("grow", [E, T]) if per_tile else None
        rsc = r.sb("rsc", [P, HC])
        pre = r.sb("pre", [P, HC])
        xn = r.sb("xn", [P, T])
        xnT = r.sb("xnT", [P, T])
        lg = r.sb("lg", [P, E])
        m8 = r.sb("m8", [P, 8])
        i8 = r.sb("i8", [P, 8], U32)
        if8 = r.sb("if8", [P, 8])
        nm = r.sb("nm", [P, 1])
        e8 = r.sb("e8", [P, TOP])
        esum = r.sb("esum", [P, 1])
        NE = 1 if per_tile else NT
        eq = r.sb("eq", [P, NE, TOP, E])
        eqs = r.sb("eqs", [P, NE, TOP, E])
        pos = r.sb("pos", [P, NE, E])
        t1 = r.sb("t1", [P, NE, E])
        row = r.sb("row", [P, NE, E])
        rowf = r.sb("rowf", [P, NE, TOP])
        rowi = r.sb("rowi", [P, NE, TOP], I32)
        pair = r.sb("pair", [P, NE, TOP, 2], I32)
        sel = r.sb("sel", [P, E], BF16)
        ssum = r.sb("ssum", [P, E], BF16)
        upper = r.sb("upper", [P, P], BF16)
        ones = r.sb("ones", [P, P], BF16)
        ioe = r.sb("ioe", [P, E])
        tok = r.sb("tok", [P, NT], I32)
        first = r.sb("first", [P, slots, 2], I32)
        zeros = r.sb("zeros", [P, T])
        psb = r.sb("psb", [P, E])
        counts = r.sb("counts", [P, 4, E])
        iob = r.sb("iob", [P, slots, E])
        own = r.sb("own", [P, slots])
        owni = r.sb("owni", [P, slots], I32)
        ps_t = r.ps("ps_t", [P, 512])
        ps_l = r.ps("ps_l", [P, 512])
        ps_p = r.ps("ps_p", [P, 512])
        made = r.sem("made")
        loaded = r.sem("loaded")
        inited = r.sem("inited")
        wready = r.sem("wready")
        wturned = r.sem("wturned")
        normed = r.sem("normed")
        stored = r.sem("stored")
        turned = r.sem("turned")
        xT_ready = r.sem("xT_ready")
        logits = r.sem("logits")
        top_ready = r.sem("top_ready")
        e_ready = r.sem("e_ready")
        sel_ready = r.sem("sel_ready")
        pos_ready = r.sem("pos_ready")
        sum_ready = r.sem("sum_ready")
        pair_ready = r.sem("pair_ready")
        scattered = r.sem("scattered")
        pair_free = r.sem("pair_free")
        own_ready = r.sem("own_ready")
        own_stored = r.sem("own_stored")
        dv = r.sem("dv")
        apart = r.sem("apart")
        block = r.block()

        @block.gpsimd
        def _(pool):
            nc.gpsimd.memset(ones[:], 1.0).then_inc(made, 1)
            nc.gpsimd.memset(upper[:], 1.0).then_inc(made, 1)
            nc.gpsimd.memset(ssum[:], 0.0).then_inc(made, 1)
            nc.gpsimd.memset(zeros[:], 0.0).then_inc(made, 1)
            nc.gpsimd.memset(first[:], 0).then_inc(made, 1)
            pool.wait_ge(made, 5)
            nc.gpsimd.affine_select(out=upper[:], in_=upper[:], compare_op=ALU.is_gt, fill=0.0, base=0,
                                    pattern=[[1, P]], channel_multiplier=-1).then_inc(made, 1)
            nc.gpsimd.iota(ioe[:], [[1, E]], base=0, channel_multiplier=0,
                           allow_small_or_imprecise_dtypes=True).then_inc(made, 1)
            nc.gpsimd.iota(tok[:], [[P, NT]], base=0, channel_multiplier=1).then_inc(made, 1)
            nc.gpsimd.iota(first[:, :, 0], [[0, slots]], base=NTOK, channel_multiplier=1).then_inc(made, 1)
            nc.gpsimd.iota(iob[:], [[1, slots], [0, E]], base=0, channel_multiplier=0,
                           allow_small_or_imprecise_dtypes=True).then_inc(made, 1)
            pool.sem_inc(stored, 16)
            pool.sem_inc(pair_free, 1)
            pool.wait_ge(inited, 16)

            def scatter(t, i):
                for k in range(TOP):
                    pool.indirect_dma_start(
                        out=table.rearrange("c b w -> (c b) w"),
                        out_offset=bass.IndirectOffsetOnAxis(ap=rowi[:, t, k:k + 1], axis=0),
                        in_=pair[:, t, k, :], in_offset=None, bounds_check=P * slots - 1, oob_is_err=False)\
                        .then_inc(scattered, 16)

            if per_tile:
                with pool.Fori(0, NT) as i:
                    pool.wait_ge(pair_ready, i + 1)
                    pool.sem_inc(apart, 1)
                    scatter(0, i)
                    pool.wait_ge(scattered, 16 * TOP * i + 16 * TOP)
                    pool.sem_inc(pair_free, 1)
            else:
                pool.wait_ge(pair_ready, 1)
                for t in range(NT):
                    scatter(t, 0)
            pool.wait_ge(scattered, 16 * TOP * NT)

        @block.sync
        def _(sp):
            if per_tile:
                sp.dma_start(grow[:], logit_w).then_inc(loaded, 16)
            else:
                sp.dma_start(wraw[:], logit_w.rearrange("(p c) e -> p c e", c=HC)).then_inc(loaded, 16)
                sp.dma_start(rsc[:], io["f1_router_scale"].rearrange("(p c) -> p c", c=HC)).then_inc(loaded, 16)
                sp.dma_start(pre[:], io["f1_rn_pre1"].rearrange("(p c) -> p c", c=HC)).then_inc(loaded, 16)
                sp.dma_start(psb[:], row_of(scale)).then_inc(loaded, 16)
            sp.wait_ge(made, 10)
            sp.dma_start(table, first[:]).then_inc(inited, 16)
            for y in range(NTOK // P + 1):
                sp.dma_start(S["y"][y * P:y * P + P], zeros[:]).then_inc(own_stored, 16)
            sp.dma_start(S["xg"][NTOK:NTOK + P], zeros[:]).then_inc(own_stored, 16)
            with sp.Fori(0, NT) as i:
                sp.wait_ge(normed, i + 1)
                sp.dma_start(S["xg"][bass.ds(P * i, P)], xn[:]).then_inc(stored, 16)
            sp.wait_ge(stored, 16 * NT + 16)
            n = 16 * (NTOK // P + 2)
            if not per_tile:
                sp.wait_ge(own_ready, 1)
                sp.dma_start(owner, owni[0:1, :]).then_inc(own_stored, 16)
                n += 16
            sp.wait_ge(own_stored, n)

        @block.tensor
        def _(pe):
            if per_tile:
                pe.wait_ge(loaded, 16)
                gv = grow[:].rearrange("e (p c) -> e c p", c=HC)
                for c in range(HC):
                    last = nc.tensor.transpose(ps_t[:, c * E:c * E + E], gv[:, c, :], ident[0:E, 0:E])
                last.then_inc(wturned, 1)
            pe.wait_ge(made, 10)
            pe.wait_ge(wready, 1)
            xv = xn[:].rearrange("q (p c) -> q c p", c=HC)
            with pe.Fori(0, NT) as i:
                pe.wait_ge(normed, i + 1)
                for c in range(HC):
                    last = nc.tensor.transpose(ps_t[:, c * P:c * P + P], xv[:, c, :], ident[:])
                last.then_inc(turned, 1)
                pe.wait_ge(xT_ready, i + 1)
                for c in range(HC):
                    last = nc.tensor.matmul(ps_l[:, 0:E], xnT[:, c * P:c * P + P], wraw[:, c, :],
                                            start=(c == 0), stop=(c == HC - 1))
                last.then_inc(logits, 1)
                pe.wait_ge(sel_ready, i + 1)
                nc.tensor.matmul(ps_p[:, 0:E], ones[:], ssum[:], start=True, stop=False)
                nc.tensor.matmul(ps_p[:, 0:E], upper[:], sel[:], start=False, stop=True).then_inc(pos_ready, 1)
            if not per_tile:
                pe.wait_ge(sum_ready, 1)
                nc.tensor.matmul(ps_p[:, 0:E], ones[:], ssum[:], start=True, stop=True).then_inc(pos_ready, 1)

        @block.scalar
        def _(act):
            with act.Fori(0, NT) as i:
                act.wait_ge(turned, i + 1)
                nc.scalar.activation(xnT[:], ps_t[:], ACT.Copy).then_inc(xT_ready, 1)
                act.wait_ge(top_ready, i + 1)
                nc.scalar.activation(e8[:], m8[:, 0:TOP], ACT.Exp, bias=nm[:, 0:1]).then_inc(e_ready, 1)

        @block.vector
        def _(dve):
            setup = Chain(dve, dv)
            dve.wait_ge(made, 10)
            if per_tile:
                dve.wait_ge(wturned, 1)
                setup(nc.vector.tensor_copy(wraw[:], ps_t[:, 0:HC * E].rearrange("p (c e) -> p c e", c=HC)))
            else:
                dve.wait_ge(loaded, 64)
                for c in range(HC):
                    ins = nc.vector.tensor_scalar(wraw[:, c, :], wraw[:, c, :], rsc[:, c:c + 1], T ** -0.5,
                                                  ALU.mult, ALU.mult)
                setup(ins)
            dve.sem_inc(wready, 1)
            base = setup.n
            per = PER_TILE_STEPS[per_tile]

            with dve.Fori(0, NT) as i:
                c = Chain(dve, dv, base + i * per)
                t = 0 if per_tile else i
                one = bass.ds(t, 1)
                dve.wait_ge(stored, 16 * i + 16)
                c(nc.vector.tensor_scalar(xn[:], X[:, bass.ds(i, 1), :].rearrange("p a t -> p (a t)"),
                                          mean[:, bass.ds(i, 1)], rstd[:, bass.ds(i, 1)],
                                          ALU.subtract, ALU.mult))
                dve.sem_inc(normed, 1)
                if dense is not None:
                    dve.wait_ge(xT_ready, i + 1)
                    d = dense[:, :, bass.ds(P * i, P)]
                    c(nc.vector.tensor_tensor(d, xnT[:].rearrange("p (c n) -> p c n", c=HC),
                                              pre[:].unsqueeze(2).broadcast_to([P, HC, P]), ALU.mult))
                dve.wait_ge(logits, i + 1)
                c(nc.vector.tensor_copy(lg[:], ps_l[:, 0:E]))
                dve.sem_inc(apart, 1)
                c(nc.vector.max(m8[:], lg[:]))
                c(nc.vector.tensor_scalar(nm[:], m8[:, 0:1], -1.0, None, ALU.mult))
                dve.sem_inc(top_ready, 1)
                c(nc.vector.max_index(i8[:], m8[:], lg[:]))
                c(nc.vector.tensor_copy(if8[:], i8[:]))
                shape = [P, TOP, E]
                e3 = eq[:, one, :, :].rearrange("p a k e -> p (a k) e")
                c(nc.vector.tensor_tensor(e3, ioe[:].unsqueeze(1).broadcast_to(shape),
                                          if8[:, 0:TOP].unsqueeze(2).broadcast_to(shape), ALU.is_equal))
                dve.sem_inc(apart, 1)
                with nc.allow_low_precision(reason="counts of zero or one"):
                    c(nc.vector.tensor_reduce(sel[:], e3.rearrange("p k e -> p e k"), AX.X, ALU.add))
                dve.sem_inc(sel_ready, 1)
                dve.wait_ge(pos_ready, i + 1)
                p2 = pos[:, one, :].rearrange("p a e -> p (a e)")
                c(nc.vector.tensor_copy(p2, ps_p[:, 0:E]))
                c(nc.vector.tensor_tensor(ssum[:], ssum[:], sel[:], ALU.add))
                if per_tile:
                    dve.wait_ge(pair_free, i + 1)
                    c(nc.vector.tensor_scalar(t1[:, 0, :], pos[:, 0, :], float(P), BIG, ALU.is_ge, ALU.mult))
                    c(nc.vector.scalar_tensor_tensor(out=row[:, 0, :], in0=pos[:, 0, :], scalar=float(E),
                                                     in1=t1[:, 0, :], op0=ALU.mult, op1=ALU.add))
                    c(nc.vector.tensor_tensor(row[:, 0, :], row[:, 0, :], ioe[:], ALU.add))
                    c(nc.vector.tensor_tensor(eqs[:, 0], eq[:, 0], row[:, 0, :].unsqueeze(1).broadcast_to(shape),
                                              ALU.mult))
                    c(nc.vector.tensor_reduce(rowf[:, 0, :], eqs[:, 0], AX.X, ALU.add))
                    c(nc.vector.tensor_copy(rowi[:, 0, :], rowf[:, 0, :]))
                dve.wait_ge(e_ready, i + 1)
                c(nc.vector.tensor_reduce(esum[:], e8[:], AX.X, ALU.add))
                c(nc.vector.reciprocal(esum[:], esum[:]))
                w = pair[:, one, :, 1:2].bitcast(F32).rearrange("p a k w -> p (a k w)")
                c(nc.vector.tensor_scalar(w, e8[:], esum[:, 0:1], None, ALU.mult))
                tk = pair[:, one, :, 0:1].rearrange("p a k w -> p (a k w)")
                c(nc.vector.tensor_copy(tk, tok[:, bass.ds(i, 1)].broadcast_to([P, TOP])))
                if scale is not None:
                    g3 = eqs[:, one, :, :].rearrange("p a k e -> p (a k) e")
                    c(nc.vector.tensor_tensor(g3, e3, psb[:].unsqueeze(1).broadcast_to(shape), ALU.mult))
                    dve.sem_inc(apart, 1)
                    r2 = rowf[:, one, :].rearrange("p a k -> p (a k)")
                    c(nc.vector.tensor_reduce(r2, g3, AX.X, ALU.add))
                    c(nc.vector.tensor_tensor(w, w, r2, ALU.mult))
                if per_tile:
                    dve.sem_inc(pair_ready, 1)
                assert c.n == per, c.n
            if not per_tile:
                c = Chain(dve, dv, base + NT * per)
                dve.sem_inc(sum_ready, 1)
                dve.wait_ge(pos_ready, NT + 1)
                total, nblk, incl, ob = (counts[:, k, :] for k in range(4))
                c(nc.vector.tensor_scalar(total, ps_p[:, 0:E], P / 2 - 0.5, 1.0 / P, ALU.add, ALU.mult))
                c(nc.vector.tensor_scalar(nblk, total, MAGIC, None, ALU.add))
                c(nc.vector.tensor_scalar(nblk, nblk, -MAGIC, None, ALU.add))
                c(nc.vector.memset(total, 1.0))
                c(nc.vector.tensor_tensor_scan(incl, total, nblk, 0.0, ALU.mult, ALU.add))
                c(nc.vector.tensor_tensor(ob, incl, nblk, ALU.subtract))
                c(nc.vector.tensor_tensor(iob[:], iob[:], incl.unsqueeze(1).broadcast_to([P, slots, E]), ALU.is_ge))
                c(nc.vector.tensor_reduce(own[:], iob[:], AX.X, ALU.add))
                c(nc.vector.tensor_scalar(own[:], own[:], float(E - 1), None, ALU.min))
                c(nc.vector.tensor_copy(owni[:], own[:]))
                dve.sem_inc(own_ready, 1)
                c(nc.vector.tensor_scalar(t1[:], pos[:], -(P / 2 - 0.5), 1.0 / P, ALU.add, ALU.mult))
                c(nc.vector.tensor_scalar(t1[:], t1[:], MAGIC, None, ALU.add))
                c(nc.vector.tensor_scalar(t1[:], t1[:], -MAGIC, 1.0 - P * slots, ALU.add, ALU.mult))
                c(nc.vector.scalar_tensor_tensor(out=row[:], in0=pos[:], scalar=float(slots), in1=t1[:],
                                                 op0=ALU.mult, op1=ALU.add))
                c(nc.vector.tensor_tensor(row[:], row[:], ob.unsqueeze(1).broadcast_to([P, NT, E]), ALU.add))
                for k in range(TOP):
                    c(nc.vector.tensor_tensor(eqs[:, :, k, :], eq[:, :, k, :], row[:], ALU.mult))
                c(nc.vector.tensor_reduce(rowf[:], eqs[:], AX.X, ALU.add))
                c(nc.vector.tensor_copy(rowi[:], rowf[:]))
                dve.sem_inc(pair_ready, 1)


PER_TILE_STEPS = {True: 20, False: 18}


def experts(nc, io, S, tag, I, blocks, table, wg, wu, wd, func, pre, owner=None):
    IC = I // 2
    with ExitStack() as ctx:
        r = Room(nc, ctx, tag)
        tab = r.sb("tab", [P, blocks, 2], I32)
        ow = r.sb("ow", [1, blocks], I32)
        prec = r.sb("prec", [P, HC])
        idx = r.sb("idx", [P, 2, 1], I32)
        xe = r.sb("xe", [P, 2, T])
        xeT = r.sb("xeT", [P, 2, T])
        wgu = r.sb("wgu", [P, 2, HC, 2 * I])
        wdn = r.sb("wdn", [IC, 2, 2, T])
        sg = r.sb("sg", [P, I])
        h = r.sb("h", [P, I])
        hT = r.sb("hT", [IC, 2, P])
        oe = r.sb("oe", [P, 2, T])
        ident = r.sb("id", [P, P])
        ps_t = r.ps("ps_t", [P, 2, 512])
        ps_g = r.ps("ps_g", [P, 2, 512])
        ps_h = r.ps("ps_h", [P, 512])
        ps_d = r.ps("ps_d", [P, 2, 512])
        made = r.sem("made")
        tabbed = r.sem("tabbed")
        indexed = r.sem("indexed")
        gathered = [r.sem(f"gathered{u}") for u in range(2)]
        turned = r.sem("turned")
        xT_ready = r.sem("xT_ready")
        w_in = [r.sem(f"w_in{u}") for u in range(2)]
        w_free = [r.sem(f"w_free{u}") for u in range(2)]
        d_in = [r.sem(f"d_in{u}") for u in range(2)]
        d_free = [r.sem(f"d_free{u}") for u in range(2)]
        gated = r.sem("gated")
        acted = r.sem("acted")
        h_ready = r.sem("h_ready")
        h_turned = r.sem("h_turned")
        hT_ready = r.sem("hT_ready")
        downed = r.sem("downed")
        o_ready = r.sem("o_ready")
        added = r.sem("added")
        oe_free = r.sem("oe_free")
        apart = r.sem("apart")
        block = r.block()

        def schedule(eng, front, back):
            front(0, 0, 0)
            with eng.Fori(0, (blocks - 1) // 2) as i:
                front(2 * i + 1, 1, i)
                back(2 * i, 0, i)
                front(2 * i + 2, 0, i + 1)
                back(2 * i + 1, 1, i)
            if blocks % 2 == 0:
                k = blocks // 2 - 1
                front(blocks - 1, 1, k)
                back(blocks - 2, 0, k)
                back(blocks - 1, 1, k)
            else:
                back(blocks - 1, 0, (blocks - 1) // 2)

        @block.gpsimd
        def _(pool):
            nc.gpsimd.memset(ident[:], 0.0).then_inc(made, 1)
            pool.wait_ge(made, 1)
            nc.gpsimd.affine_select(out=ident[:], in_=ident[:], compare_op=ALU.not_equal, fill=1.0,
                                    base=0, pattern=[[-1, P]], channel_multiplier=1).then_inc(made, 1)
            for u in range(2):
                pool.sem_inc(w_free[u], 1)
                pool.sem_inc(d_free[u], 1)
            pool.sem_inc(oe_free, 2)
            pool.wait_ge(tabbed, 48 if owner is not None else 32)

            def front(n, u, i):
                if not (isinstance(n, int) and n < 2):
                    pool.wait_ge(turned, n - 1)
                    pool.wait_ge(added, 16 * n - 16)
                    pool.sem_inc(oe_free, 1)
                nc.gpsimd.tensor_copy(idx[:, u, :], tab[:, bass.ds(n, 1), 0]).then_inc(indexed, 1)
                pool.wait_ge(indexed, n + 1)
                pool.sem_inc(apart, 1)
                pool.indirect_dma_start(out=xe[:, u, :], out_offset=None, in_=S["xg"],
                                        in_offset=bass.IndirectOffsetOnAxis(ap=idx[:, u, 0:1], axis=0))\
                    .then_inc(gathered[u], 16)

            def back(n, u, i):
                pool.wait_ge(o_ready, n + 1)
                pool.sem_inc(apart, 1)
                pool.indirect_dma_start(out=S["y"], out_offset=bass.IndirectOffsetOnAxis(ap=idx[:, u, 0:1], axis=0),
                                        in_=oe[:, u, :], in_offset=None, compute_op=ALU.add).then_inc(added, 16)

            front(0, 0, 0)
            front(1, 1, 0)
            with pool.Fori(0, (blocks - 2) // 2) as i:
                back(2 * i, 0, i)
                front(2 * i + 2, 0, i + 1)
                back(2 * i + 1, 1, i)
                front(2 * i + 3, 1, i + 1)
            done = 2 * ((blocks - 2) // 2)
            for n in range(done, blocks):
                if n > done:
                    pool.wait_ge(added, 16 * n)
                back(n, n % 2, n // 2)
                if n + 2 < blocks:
                    front(n + 2, n % 2, n // 2 + 1)
            pool.wait_ge(added, 16 * blocks)

        @block.sync
        def _(sp):
            sp.dma_start(tab[:], table).then_inc(tabbed, 16)
            if pre is not None:
                sp.dma_start(prec[:], pre.rearrange("(p c) -> p c", c=HC)).then_inc(tabbed, 16)
            else:
                sp.sem_inc(tabbed, 16)
            if owner is not None:
                sp.dma_start(ow[:], owner).then_inc(tabbed, 16)
                sp.wait_ge(tabbed, 48)

            def weights(n, u, i):
                e = n
                if owner is not None:
                    e = sp.value_load(ow[0:1, bass.ds(n, 1)], min_val=0, max_val=wg.shape[0] - 1)
                e = bass.ds(e, 1)
                sp.wait_ge(w_free[u], i + 1)
                for k, w in enumerate((wg, wu)):
                    sp.dma_start(wgu[:, u, :, k * I:k * I + I],
                                 w[e].rearrange("a (p c) i -> p (a c) i", c=HC)).then_inc(w_in[u], 16)
                sp.wait_ge(d_free[u], i + 1)
                sp.dma_start(wdn[:, u, :, :], wd[e].rearrange("a (p c) n -> p (a c) n", c=2)).then_inc(d_in[u], 16)

            with sp.Fori(0, blocks // 2) as i:
                for u in range(2):
                    weights(2 * i + u, u, i)
            if blocks % 2:
                weights(blocks - 1, 0, blocks // 2)

        @block.tensor
        def _(pe):
            pe.wait_ge(made, 2)
            hv = h[:].rearrange("q (p c) -> q c p", c=2)

            def front(n, u, i):
                pe.wait_ge(gathered[u], 16 * i + 16)
                xv = xe[:, u, :].rearrange("q (p c) -> q c p", c=HC)
                for c in range(HC):
                    last = nc.tensor.transpose(ps_t[:, u, c * P:c * P + P], xv[:, c, :], ident[:])
                last.then_inc(turned, 1)
                pe.wait_ge(xT_ready, n + 1)
                pe.wait_ge(w_in[u], 32 * i + 32)
                for c in range(HC):
                    last = nc.tensor.matmul(ps_g[:, u, 0:2 * I], xeT[:, u, c * P:c * P + P], wgu[:, u, c, :],
                                            start=(c == 0), stop=(c == HC - 1))
                last.then_inc(gated, 1)

            def back(n, u, i):
                pe.wait_ge(h_ready, n + 1)
                pe.sem_inc(w_free[u], 1)
                for c in range(2):
                    last = nc.tensor.transpose(ps_h[0:IC, c * P:c * P + P], hv[:, c, :], ident[:])
                last.then_inc(h_turned, 1)
                pe.wait_ge(hT_ready, n + 1)
                pe.wait_ge(d_in[u], 16 * i + 16)
                for c in range(2):
                    last = nc.tensor.matmul(ps_d[:, u, :], hT[:, c, :], wdn[:, u, c, :], start=(c == 0), stop=(c == 1))
                last.then_inc(downed, 1)

            schedule(pe, front, back)

        @block.scalar
        def _(act):
            act.wait_ge(tabbed, 48 if owner is not None else 32)

            def front(n, u, i):
                act.wait_ge(turned, n + 1)
                if pre is None:
                    nc.scalar.activation(xeT[:, u, :], ps_t[:, u, :], ACT.Copy).then_inc(xT_ready, 1)
                else:
                    for c in range(HC):
                        ins = nc.scalar.activation(xeT[:, u, c * P:c * P + P], ps_t[:, u, c * P:c * P + P],
                                                   ACT.Copy, scale=prec[:, c:c + 1])
                    ins.then_inc(xT_ready, 1)
                act.wait_ge(gated, n + 1)
                if not (isinstance(n, int) and n == 0):
                    act.wait_ge(h_ready, n)
                nc.scalar.activation(sg[:], ps_g[:, u, 0:I], func).then_inc(acted, 1)

            def back(n, u, i):
                act.wait_ge(h_turned, n + 1)
                nc.scalar.activation(hT[:].rearrange("p c n -> p (c n)"), ps_h[0:IC, 0:2 * P], ACT.Copy)\
                  .then_inc(hT_ready, 1)

            schedule(act, front, back)

        @block.vector
        def _(dve):
            dve.wait_ge(tabbed, 48 if owner is not None else 32)
            wcol = tab[:].bitcast(F32)

            def front(n, u, i):
                return

            def back(n, u, i):
                dve.wait_ge(acted, n + 1)
                nc.vector.scalar_tensor_tensor(out=h[:], in0=ps_g[:, u, I:2 * I], scalar=wcol[:, bass.ds(n, 1), 1],
                                               in1=sg[:], op0=ALU.mult, op1=ALU.mult).then_inc(h_ready, 1)
                dve.wait_ge(downed, n + 1)
                dve.sem_inc(d_free[u], 1)
                dve.wait_ge(oe_free, n + 1)
                nc.vector.tensor_copy(oe[:, u, :], ps_d[:, u, :]).then_inc(o_ready, 1)

            schedule(dve, front, back)


def moe0(nc, io, X, K, S):
    gate = K["gate"]
    E = io["m0_gate_w"].shape[0]
    with ExitStack() as outer:
        o = Room(nc, outer, "m0")
        mean = o.sb("mean", [P, NT])
        rstd = o.sb("rstd", [P, NT])
        row_stats(nc, X, "m0_st", 1e-5, False, mean, rstd)
        route(nc, io, X, K, S, "m0r", E, 8, io["m0_gate_w"], mean, rstd, S["table0"], E)
    experts(nc, io, S, "m0e", io["m0_wg"].shape[2], E, S["table0"], io["m0_wg"], io["m0_wu"], io["m0_wd"],
            ACT.Silu, None)
    with ExitStack() as ctx:
        r = Room(nc, ctx, "m0a")
        y = r.sb("y", [P, 4, T])
        loaded = [r.sem(f"loaded{k}") for k in range(4)]
        added = r.sem("added")
        block = r.block()

        @block.sync
        def _(sp):
            for i in range(NT):
                if i >= 4:
                    sp.wait_ge(added, i - 3)
                sp.dma_start(y[:, i % 4, :], S["y"][i * P:i * P + P]).then_inc(loaded[i % 4], 16)

        @block.vector
        def _(dve):
            for i in range(NT):
                dve.wait_ge(loaded[i % 4], 16 * (i // 4) + 16)
                nc.vector.scalar_tensor_tensor(out=X[:, i, :], in0=y[:, i % 4, :], scalar=gate[:, 2:3],
                                               in1=X[:, i, :], op0=ALU.mult, op1=ALU.add).then_inc(added, 1)
            dve.wait_ge(added, NT)



DH = T // NH
HB = P // DH
SW = C + P
HW = DH + 1
MASKED = -1.0e30
LN_EPS = 1e-6


def mlstm(nc, io, X, K, S):
    ident, gate = K["ident"], K["gate"]
    with ExitStack() as outer:
        o = Room(nc, outer, "ml")
        mean = o.sb("mean", [P, NT])
        rstd = o.sb("rstd", [P, NT])
        row_stats(nc, X, "ml_st", 1e-5, False, mean, rstd)
        with ExitStack() as ctx:
            r = Room(nc, ctx, "mx")
            wq = r.sb("wq", [P, HC, 64])
            wkv = r.sb("wkv", [P, HC, 64])
            wraw = r.sb("wraw", [P, 2, HC, 64])
            bcol = r.sb("bcol", [64, 1])
            lnb = r.sb("lnb", [P, T])
            ones = r.sb("ones", [NH, C])
            xn = r.sb("xn", [P, CT, T])
            cx = r.sb("cx", [P, 2, CT, T])
            qT = r.sb("qT", [P, 2, HC, C])
            cT = r.sb("cT", [P, 2, HC, C])
            va = r.sb("va", [P, 2, CT, NH * HW])
            g = r.sb("g", [NH, 2, C])
            ga = r.sb("ga", [NH, C])
            gl = r.sb("gl", [NH, C])
            Fc = r.sb("F", [NH, C])
            a = r.sb("a", [NH, C])
            M = r.sb("M", [NH, C])
            mx = r.sb("mx", [NH, C])
            nM = r.sb("nM", [NH, C])
            D0 = r.sb("D0", [P, 2, NH, SW])
            acol = r.sb("acol", [P, 2, 2, CT, NH])
            en = r.sb("en", [P, CT * NH])
            D = r.sb("D", [P, 2, HB, SW])
            Cm = r.sb("C", [P, 2, HB, SW])
            hr = r.sb("hr", [P, CT, NH, HW])
            nrm = r.sb("nrm", [P, CT * NH])
            hv = r.sb("hv", [P, CT * NH, DH])
            sq = r.sb("sq", [P, CT * NH, DH])
            st = r.sb("st", [P, CT * NH])
            rs = r.sb("rs", [P, CT * NH])
            ps_s = r.ps("ps_s", [P, HB, 512])
            ps_h = r.ps("ps_h", [P, CT, 512])
            ps_t = r.ps("ps_t", [P, 512])
            ps_g = r.ps("ps_g", [P, 512])
            made = r.sem("made")
            wload = r.sem("wload")
            summed = r.sem("summed")
            ctx_in = [r.sem(f"ctx_in{u}") for u in range(2)]
            ctx_free = [r.sem(f"ctx_free{u}") for u in range(2)]
            xn_ready = r.sem("xn_ready")
            turned = r.sem("turned")
            copied = r.sem("copied")
            va_ready = r.sem("va_ready")
            gated = r.sem("gated")
            g_ready = r.sem("g_ready")
            abs_ready = r.sem("abs_ready")
            ln_ready = r.sem("ln_ready")
            nM_ready = r.sem("nM_ready")
            nM_stored = r.sem("nM_stored")
            spread = [r.sem(f"spread{u}") for u in range(2)]
            masked = r.sem("masked")
            cols = r.sem("cols")
            cols_ready = r.sem("cols_ready")
            en_ready = r.sem("en_ready")
            scored = r.sem("scored")
            d_ready = r.sem("d_ready")
            c_ready = r.sem("c_ready")
            mixed = r.sem("mixed")
            h_copied = r.sem("h_copied")
            var_ready = r.sem("var_ready")
            root = r.sem("root")
            fin = r.sem("fin")
            done = r.sem("done")
            dv = r.sem("dv")
            df = r.sem("df")
            apart = r.sem("apart")
            av = r.sem("av")
            block = r.block()
            NCH = NH // HB

            def schedule(eng, prep, chunk, finish):
                for k in range(4):
                    prep(0, 0, 0, k)

                def body(n, u, i, more=True):
                    for k in range(NCH):
                        chunk(n, u, i, k)
                        if more:
                            prep(n + 1, 1 - u, i + u, k)
                    finish(n, u, i)
                with eng.Fori(0, B // 2 - 1) as i:
                    body(2 * i, 0, i)
                    body(2 * i + 1, 1, i)
                body(B - 2, 0, B // 2 - 1)
                body(B - 1, 1, B // 2 - 1, False)

            @block.gpsimd
            def _(pool):
                nc.gpsimd.memset(wraw[:], 0.0).then_inc(made, 1)
                nc.gpsimd.memset(wq[:], 0.0).then_inc(made, 1)
                nc.gpsimd.memset(bcol[:], 0.0).then_inc(made, 1)
                nc.gpsimd.memset(ones[:], 1.0).then_inc(made, 1)
                for u in range(2):
                    pool.sem_inc(ctx_free[u], 1)
                pool.sem_inc(c_ready, 8)
                pool.sem_inc(mixed, 8)
                pool.sem_inc(h_copied, 1)

                def prep(n, u, i, k):
                    if k == 3:
                        pool.wait_ge(spread[u], 32 * i + 32)
                        pool.sem_inc(apart, 1)
                        for lo in (0, C):
                            v = D0[:, u, :, lo:lo + P]
                            last = nc.gpsimd.affine_select(out=v, in_=v, compare_op=ALU.is_ge, fill=MASKED, base=0,
                                                           pattern=[[0, NH], [1, P]], channel_multiplier=-1)
                        last.then_inc(masked, 1)

                schedule(pool, prep, lambda *_: None, lambda *_: None)

            @block.sync
            def _(sp):
                sp.wait_ge(made, 4)
                for half, (w, b) in enumerate((("l1_Wi", "l1_bi"), ("l1_Wf", "l1_bf"))):
                    v = io[w].rearrange("(k c p) n -> k p c n", k=3, p=P)
                    at = slice(32 * half, 32 * half + NH)
                    sp.dma_start(wq[:, :, at], v[0]).then_inc(wload, 16)
                    for k in range(2):
                        sp.dma_start(wraw[:, k, :, at], v[1 + k]).then_inc(wload, 16)
                    sp.dma_start(bcol[at, :], io[b].rearrange("(n a) -> n a", a=1)).then_inc(wload, 16)
                sp.dma_start(lnb[:], row_of(io["l1_ln_scale"])).then_inc(wload, 16)
                vc = io["ctx"].rearrange("b (c p) t -> b p c t", p=P)

                def load(n, u, i):
                    sp.wait_ge(ctx_free[u], i + 1)
                    sp.dma_start(cx[:, u, :, :], vc[n]).then_inc(ctx_in[u], 16)

                def prep(n, u, i, k):
                    if k == 0:
                        load(n, u, i)
                    if k == 3:
                        sp.wait_ge(nM_ready, n + 1)
                        sp.dma_start(S["nm"], nM[:]).then_inc(nM_stored, 16)
                        sp.wait_ge(nM_stored, 16 * n + 16)
                        sp.dma_start(D0[:, u, :, 0:C], S["nm1"].broadcast_to([P, NH * C])
                                     .rearrange("p (h s) -> p h s", h=NH)).then_inc(spread[u], 16)
                        sp.dma_start(D0[:, u, :, C:SW], S["nm1"].broadcast_to([P, NH * C])
                                     .rearrange("p (h s) -> p h s", h=NH)[:, :, P:C]).then_inc(spread[u], 16)

                schedule(sp, prep, lambda *_: None, lambda *_: None)

            @block.tensor
            def _(pe):
                def prep(n, u, i, k):
                    if k < 2:
                        if k == 0:
                            pe.wait_ge(xn_ready, n + 1)
                        else:
                            pe.wait_ge(ctx_in[u], 16 * i + 16)
                        for ct in range(CT):
                            m = 2 * k + ct
                            if not (isinstance(n, int) and n == 0 and m == 0):
                                pe.wait_ge(copied, 4 * n + m)
                            src = xn[:, ct, :] if k == 0 else cx[:, u, ct, :]
                            for c in range(HC):
                                last = nc.tensor.transpose(ps_t[:, c * P:c * P + P], src[:, c * P:c * P + P], ident[:])
                            last.then_inc(turned, 1)
                    if k == 2:
                        pe.wait_ge(summed, 1)
                        pe.wait_ge(copied, 4 * n + 4)
                        for c in range(HC):
                            nc.tensor.matmul(ps_g[0:64, 0:C], wq[:, c, :], qT[:, u, c, :], start=(c == 0), stop=False)
                        for c in range(HC):
                            last = nc.tensor.matmul(ps_g[0:64, 0:C], wkv[:, c, :], cT[:, u, c, :],
                                                    start=False, stop=(c == HC - 1))
                        last.then_inc(gated, 1)
                    if k == 3:
                        pe.wait_ge(nM_ready, n + 1)
                        pe.sem_inc(apart, 1)
                        for j, src in enumerate((a, mx)):
                            for ct in range(CT):
                                last = nc.tensor.transpose(ps_g[:, (j * CT + ct) * NH:(j * CT + ct + 1) * NH],
                                                           src[:, ct * P:ct * P + P], ident[0:NH, 0:NH])
                        last.then_inc(cols, 1)

                def chunk(n, u, i, k):
                    for j in range(HB):
                        pe.wait_ge(c_ready, NH * n + HB * k + j + 5)
                        row = slice(DH * j, DH * j + DH)
                        nc.tensor.matmul(ps_s[:, j, 0:C], cT[row, u, k, 0:P], qT[row, u, k, :], start=True, stop=True)
                    for j in range(HB):
                        row = slice(DH * j, DH * j + DH)
                        nc.tensor.matmul(ps_s[:, j, C:SW], cT[row, u, k, P:C], qT[row, u, k, P:C],
                                         start=True, stop=True).then_inc(scored, 1)
                    pe.wait_ge(va_ready, n + 1)
                    if k % 2 == 0:
                        pe.wait_ge(h_copied, 2 * n + k // 2 + 1)
                    for j in range(HB):
                        h = HB * k + j
                        pe.wait_ge(c_ready, NH * n + h + 9)
                        at = slice((h % 8) * HW, (h % 8) * HW + HW)
                        v = [va[:, u, ct, h * HW:h * HW + HW] for ct in range(CT)]
                        c = Cm[:, k % 2, j, :]
                        nc.tensor.matmul(ps_h[:, 0, at], c[:, 0:P], v[0], start=True, stop=True)
                        nc.tensor.matmul(ps_h[:, 1, at], c[:, P:C], v[0], start=True, stop=False)
                        nc.tensor.matmul(ps_h[:, 1, at], c[:, C:SW], v[1], start=False, stop=True).then_inc(mixed, 1)

                schedule(pe, prep, chunk, lambda *_: None)

            @block.scalar
            def _(act):
                def prep(n, u, i, k):
                    if k < 2:
                        for ct in range(CT):
                            act.wait_ge(turned, 4 * n + 2 * k + ct + 1)
                            dst = (qT, cT)[k][:, u, :, ct * P:ct * P + P]
                            nc.scalar.activation(dst, ps_t[:].rearrange("p (c n) -> p c n", c=HC), ACT.Copy)\
                              .then_inc(copied, 1)
                    if k == 2:
                        act.wait_ge(gated, n + 1)
                        act.wait_ge(wload, 16 * 9)
                        nc.scalar.activation(g[:, 0, :], ps_g[0:NH, 0:C], ACT.Identity, bias=bcol[0:NH, :]).then_inc(g_ready, 1)
                        nc.scalar.activation(g[:, 1, :], ps_g[32:32 + NH, 0:C], ACT.Identity, bias=bcol[32:32 + NH, :])\
                          .then_inc(g_ready, 1)
                        act.wait_ge(abs_ready, n + 1)
                        nc.scalar.activation(gl[:], ga[:], ACT.Exp, scale=-1.0).then_inc(av, 1)
                        act.wait_ge(av, n + 1)
                        nc.scalar.activation(gl[:], gl[:], ACT.Ln, bias=1.0).then_inc(ln_ready, 1)

                def chunk(n, u, i, k):
                    if k == 0:
                        act.wait_ge(cols_ready, n + 1)
                        act.wait_ge(masked, n + 1)
                    for j in range(HB):
                        h = HB * k + j
                        act.wait_ge(c_ready, NH * n + h + 1)
                        nc.scalar.activation(D[:, k % 2, j, 0:C], D0[:, u, h, 0:C], ACT.Exp,
                                             bias=acol[:, u, 0, 0, h:h + 1])
                        nc.scalar.activation(D[:, k % 2, j, C:SW], D0[:, u, h, C:SW], ACT.Exp,
                                             bias=acol[:, u, 0, 1, h:h + 1]).then_inc(d_ready, 1)
                    if k == NCH - 1:
                        nc.scalar.activation(en[:], acol[:, u, 1, :, :].rearrange("p c h -> p (c h)"), ACT.Exp,
                                             scale=-1.0).then_inc(en_ready, 1)

                def finish(n, u, i):
                    act.wait_ge(var_ready, n + 1)
                    nc.scalar.activation(rs[:], st[:], ACT.Sqrt).then_inc(root, 1)

                schedule(act, prep, chunk, finish)

            STEPS_G, STEPS_F = 7, 12

            @block.vector
            def _(dve):
                dve.wait_ge(made, 4)
                dve.wait_ge(wload, 16 * 9)
                nc.vector.tensor_tensor(wkv[:], wraw[:, 0], wraw[:, 1], ALU.add).then_inc(summed, 1)
                setup = Chain(dve, dv)
                setup(nc.vector.memset(va[:], 1.0))

                def prep(n, u, i, k):
                    if k == 0:
                        for ct in range(CT):
                            tile = CT * n + ct
                            ins = nc.vector.tensor_scalar(xn[:, ct, :],
                                                          X[:, bass.ds(tile, 1), :].rearrange("p a t -> p (a t)"),
                                                          mean[:, bass.ds(tile, 1)], rstd[:, bass.ds(tile, 1)],
                                                          ALU.subtract, ALU.mult)
                        ins.then_inc(xn_ready, 1)
                    if k == 1:
                        dve.wait_ge(ctx_in[u], 16 * i + 16)
                        nc.vector.tensor_copy(va[:, u, :, :].rearrange("p c (h w) -> p c h w", w=HW)[:, :, :, 0:DH],
                                              cx[:, u, :, :].rearrange("p c (h d) -> p c h d", d=DH)).then_inc(va_ready, 1)
                        dve.wait_ge(va_ready, n + 1)
                        dve.wait_ge(turned, 4 * n + 4)
                        dve.sem_inc(ctx_free[u], 1)
                    if k == 2:
                        c = Chain(dve, dv, 1 + STEPS_G * n)
                        dve.wait_ge(g_ready, 2 * n + 2)
                        nc.vector.scalar_tensor_tensor(out=ga[:], in0=g[:, 1, :], scalar=-1.0, in1=g[:, 1, :],
                                                       op0=ALU.mult, op1=ALU.max).then_inc(abs_ready, 1)
                        c(nc.vector.tensor_scalar(Fc[:], g[:, 1, :], 0.0, None, ALU.min))
                        dve.wait_ge(ln_ready, n + 1)
                        c(nc.vector.tensor_tensor(gl[:], Fc[:], gl[:], ALU.subtract))
                        c(nc.vector.tensor_tensor_scan(Fc[:], ones[:], gl[:], 0.0, ALU.mult, ALU.add))
                        if not (isinstance(n, int) and n == 0):
                            dve.wait_ge(cols, n)
                        c(nc.vector.tensor_tensor(a[:], g[:, 0, :], Fc[:], ALU.subtract))
                        c(nc.vector.tensor_tensor_scan(M[:], ones[:], a[:], -3.0e38, ALU.mult, ALU.max))
                        c(nc.vector.tensor_tensor(mx[:], Fc[:], M[:], ALU.add))
                        c(nc.vector.tensor_scalar(nM[:], M[:], -1.0, None, ALU.mult))
                        assert c.n == STEPS_G
                        dve.sem_inc(nM_ready, 1)
                    if k == 3:
                        dve.wait_ge(cols, n + 1)
                        nc.vector.tensor_copy(acol[:, u, :, :, :].rearrange("p j c h -> p (j c h)"),
                                              ps_g[:, 0:2 * CT * NH]).then_inc(cols_ready, 1)

                def chunk(n, u, i, k):
                    for j in range(HB):
                        h = HB * k + j
                        dve.wait_ge(scored, NH * n + h + 1)
                        dve.wait_ge(d_ready, NH * n + h + 1)
                        dve.wait_ge(mixed, NH * n + h + 1)
                        nc.vector.scalar_tensor_tensor(out=Cm[:, k % 2, j, :], in0=ps_s[:, j, 0:SW], scalar=DH ** -0.5,
                                                       in1=D[:, k % 2, j, :], op0=ALU.mult, op1=ALU.mult)\
                          .then_inc(c_ready, 1)
                    if k % 2 == 1:
                        dve.wait_ge(mixed, NH * n + HB * k + HB + 8)
                        half = (k // 2) * 8
                        nc.vector.tensor_copy(hr[:, :, half:half + 8, :].rearrange("p c h w -> p c (h w)"),
                                              ps_h[:, :, 0:8 * HW]).then_inc(h_copied, 1)

                def finish(n, u, i):
                    c = Chain(dve, df, STEPS_F * n)
                    hh = hr[:].rearrange("p c h w -> p (c h) w")
                    wide = [P, CT * NH, DH]
                    dve.wait_ge(h_copied, 2 * n + 3)
                    dve.wait_ge(en_ready, n + 1)
                    c(nc.vector.scalar_tensor_tensor(out=nrm[:], in0=hh[:, :, DH], scalar=-1.0, in1=hh[:, :, DH],
                                                     op0=ALU.mult, op1=ALU.max))
                    c(nc.vector.tensor_tensor(nrm[:], nrm[:], en[:], ALU.max))
                    c(nc.vector.tensor_scalar(nrm[:], nrm[:], LN_EPS, None, ALU.add))
                    c(nc.vector.reciprocal(nrm[:], nrm[:]))
                    c(nc.vector.tensor_tensor(hv[:], hh[:, :, 0:DH], nrm[:].unsqueeze(2).broadcast_to(wide), ALU.mult))
                    c(nc.vector.tensor_reduce(st[:], hv[:], AX.X, ALU.add))
                    c(nc.vector.tensor_scalar(st[:], st[:], 1.0 / DH, None, ALU.mult))
                    c(nc.vector.tensor_tensor(hv[:], hv[:], st[:].unsqueeze(2).broadcast_to(wide), ALU.subtract))
                    c(nc.vector.tensor_tensor(sq[:], hv[:], hv[:], ALU.mult))
                    c(nc.vector.tensor_reduce(st[:], sq[:], AX.X, ALU.add))
                    c(nc.vector.tensor_scalar(st[:], st[:], 1.0 / DH, LN_EPS, ALU.mult, ALU.add))
                    dve.sem_inc(var_ready, 1)
                    dve.wait_ge(root, n + 1)
                    c(nc.vector.reciprocal(rs[:], rs[:]))
                    assert c.n == STEPS_F
                    nc.vector.tensor_tensor(hv[:], hv[:], rs[:].unsqueeze(2).broadcast_to(wide), ALU.mult)\
                      .then_inc(fin, 1)
                    dve.wait_ge(fin, 2 * n + 1)
                    h2 = hv[:].rearrange("p (c h) d -> p c (h d)", c=CT)
                    nc.vector.scalar_tensor_tensor(out=h2, in0=h2, scalar=gate[:, 1:2],
                                                   in1=lnb[:].unsqueeze(1).broadcast_to([P, CT, T]),
                                                   op0=ALU.mult, op1=ALU.mult).then_inc(fin, 1)
                    dve.wait_ge(fin, 2 * n + 2)
                    x = X[:, bass.ds(CT * n, CT), :]
                    nc.vector.tensor_tensor(x, x, h2, ALU.add).then_inc(done, 1)

                schedule(dve, prep, chunk, finish)
                dve.wait_ge(done, B)




def dense_ffn(nc, io, S, dT):
    I = io["f1_w_gate"].shape[1]
    IC = I // P
    TG = 512
    TT = TG // P
    with ExitStack() as ctx:
        r = Room(nc, ctx, "dn")
        w = r.sb("w", [P, 2, HC, I])
        wd = r.sb("wd", [P, IC, T])
        g = r.sb("g", [P, 2, TG])
        h = r.sb("h", [P, 2, TG])
        out = r.sb("out", [P, 2, T])
        ps_g = r.ps("ps_g", [P, 2, 512])
        ps_u = r.ps("ps_u", [P, 2, 512])
        ps_o = r.ps("ps_o", [P, TT, 512])
        w_in = [r.sem(f"w_in{k}") for k in range(4)]
        d_in = r.sem("d_in")
        up = r.sem("up")
        acted = r.sem("acted")
        h_ready = r.sem("h_ready")
        down = r.sem("down")
        copied = [r.sem("copied_a"), r.sem("copied_d")]
        stored = [r.sem("stored_a"), r.sem("stored_d")]
        credit = r.sem("credit")
        block = r.block()
        NG4 = NTOK // TG

        @block.sync
        def _(sp):
            for k in range(4):
                cols = slice(k * I // 4, (k + 1) * I // 4)
                for j, name in enumerate(("f1_w_gate", "f1_w_up")):
                    sp.dma_start(w[:, j, :, cols], io[name].rearrange("(p c) i -> p c i", c=HC)[:, :, cols])\
                      .then_inc(w_in[k], 16)
            sp.dma_start(wd[:], io["f1_w_down"].rearrange("(c p) n -> p c n", p=P)).then_inc(d_in, 16)
            for k in range(2):
                sp.sem_inc(copied[k], 1)
                sp.sem_inc(stored[k], 16)
            with sp.Fori(0, NG4) as q:
                for t in range(TT):
                    k = t % 2
                    sp.wait_ge(copied[k], 2 * q + t // 2 + 2)
                    sp.dma_start(S["dn"][bass.ds(TT * q + t, 1)].rearrange("a p t -> p (a t)"), out[:, k, :])\
                      .then_inc(stored[k], 16)
            for k in range(2):
                sp.wait_ge(stored[k], 32 * NG4 + 16)

        @block.tensor
        def _(pe):
            def group(q, first):
                for ic in range(IC + 1):
                    if ic < IC:
                        if first and ic % (IC // 4) == 0:
                            pe.wait_ge(w_in[ic * 4 // IC], 32)
                        if not first or ic >= 2:
                            pe.wait_ge(h_ready, IC * q + ic - 1)
                        for ps, j in ((ps_g, 0), (ps_u, 1)):
                            for c in range(HC):
                                last = nc.tensor.matmul(ps[:, ic % 2, :], w[:, j, c, ic * P:ic * P + P],
                                                        dT[:, c, bass.ds(TG * q, TG)],
                                                        start=(c == 0), stop=(c == HC - 1))
                        last.then_inc(up, 1)
                    if ic > 0:
                        if first and ic == 1:
                            pe.wait_ge(d_in, 16)
                        if ic == 1:
                            for k in range(2):
                                pe.wait_ge(copied[k], 2 * q + 1)
                        pe.wait_ge(h_ready, IC * q + ic)
                        for t in range(TT):
                            last = nc.tensor.matmul(ps_o[:, t, :], h[:, (ic - 1) % 2, t * P:t * P + P], wd[:, ic - 1, :],
                                                    start=(ic == 1), stop=(ic == IC))
                        last.then_inc(down, 1)

            group(0, True)
            with pe.Fori(1, NG4) as q:
                group(q, False)

        @block.scalar
        def _(act):
            with act.Fori(0, NG4) as q:
                for ic in range(IC):
                    act.wait_ge(up, IC * q + ic + 1)
                    nc.scalar.activation(g[:, ic % 2, :], ps_g[:, ic % 2, :], ACT.Gelu_apprx_tanh).then_inc(acted, 1)
                act.wait_ge(down, IC * q + IC)
                for t in (0, 2):
                    act.wait_ge(stored[0], 32 * q + 8 * t + 16)
                    nc.scalar.activation(out[:, 0, :], ps_o[:, t, :], ACT.Copy).then_inc(copied[0], 1)

        @block.vector
        def _(dve):
            dve.sem_inc(credit, 2)
            with dve.Fori(0, NG4) as q:
                for ic in range(IC):
                    dve.wait_ge(acted, IC * q + ic + 1)
                    dve.wait_ge(credit, IC * q + ic + 1)
                    nc.vector.tensor_tensor(h[:, ic % 2, :], g[:, ic % 2, :], ps_u[:, ic % 2, :], ALU.mult)\
                      .then_inc(h_ready, 1)
                dve.wait_ge(down, IC * q + IC)
                for t in (1, 3):
                    dve.wait_ge(stored[1], 32 * q + 8 * (t - 1) + 16)
                    nc.vector.tensor_copy(out[:, 1, :], ps_o[:, t, :]).then_inc(copied[1], 1)

        @block.gpsimd
        def _(pool):
            with pool.Fori(0, NG4) as q:
                for ic in range(IC):
                    pool.wait_ge(down, IC * q + ic + 1)
                    pool.sem_inc(credit, 1)


def ffn1(nc, io, X, K, S):
    gate = K["gate"]
    E = io["f1_router_w"].shape[1]
    with ExitStack() as outer:
        o = Room(nc, outer, "f1")
        dT = o.sb("dT", [P, HC, NTOK])
        with ExitStack() as inner:
            o2 = Room(nc, inner, "f1s")
            mean = o2.sb("mean", [P, NT])
            rstd = o2.sb("rstd", [P, NT])
            row_stats(nc, X, "f1_st", 1e-5, False, mean, rstd, second=1e-6)
            route(nc, io, X, K, S, "f1r", E, 2, io["f1_router_w"], mean, rstd, S["table1"], BLOCKS1,
                  dense=dT, scale=io["f1_per_expert_scale"], owner=S["owner"])
        dense_ffn(nc, io, S, dT)
    experts(nc, io, S, "f1e", io["f1_we_gate"].shape[2], BLOCKS1, S["table1"], io["f1_we_gate"], io["f1_we_up"],
            io["f1_we_down"], ACT.Gelu_apprx_tanh, io["f1_rn_pre2"], owner=S["owner"])
    with ExitStack() as outer:
        o = Room(nc, outer, "fn")
        d = o.sb("d", [P, NT, T])
        m = o.sb("m", [P, NT, T])
        post = o.sb("post", [P, 3, T])
        mean = o.sb("mean", [P, NT])
        rd = o.sb("rd", [P, NT])
        rm = o.sb("rm", [P, NT])
        with ExitStack() as ctx:
            r = Room(nc, ctx, "fl")
            loaded = r.sem("loaded")
            block = r.block()

            @block.sync
            def _(sp):
                for i in range(NT):
                    sp.dma_start(d[:, i, :], S["dn"][i]).then_inc(loaded, 16)
                    sp.dma_start(m[:, i, :], S["y"][i * P:i * P + P]).then_inc(loaded, 16)
                for k, w in enumerate(("f1_rn_post1", "f1_rn_post2", "f1_rn_post")):
                    sp.dma_start(post[:, k, :], row_of(io[w])).then_inc(loaded, 16)
                sp.wait_ge(loaded, 16 * (2 * NT + 3))

        row_stats(nc, d, "fn_d", 1e-6, True, mean, rd)
        row_stats(nc, m, "fn_m", 1e-6, True, mean, rm)
        with ExitStack() as ctx:
            r = Room(nc, ctx, "fs")
            dv = r.sem("dv")
            block = r.block()

            @block.vector
            def _(dve):
                with dve.Fori(0, NT) as i:
                    c = Chain(dve, dv, 3 * i)
                    dd = d[:, bass.ds(i, 1), :].rearrange("p a t -> p (a t)")
                    mm = m[:, bass.ds(i, 1), :].rearrange("p a t -> p (a t)")
                    c(nc.vector.scalar_tensor_tensor(out=dd, in0=dd, scalar=rd[:, bass.ds(i, 1)], in1=post[:, 0, :],
                                                     op0=ALU.mult, op1=ALU.mult))
                    c(nc.vector.scalar_tensor_tensor(out=mm, in0=mm, scalar=rm[:, bass.ds(i, 1)], in1=post[:, 1, :],
                                                     op0=ALU.mult, op1=ALU.mult))
                    c(nc.vector.tensor_tensor(dd, dd, mm, ALU.add))

        row_stats(nc, d, "fn_s", 1e-6, True, mean, rd)
        with ExitStack() as ctx:
            r = Room(nc, ctx, "fx")
            dv = r.sem("dv")
            block = r.block()

            @block.vector
            def _(dve):
                with dve.Fori(0, NT) as i:
                    c = Chain(dve, dv, 2 * i)
                    dd = d[:, bass.ds(i, 1), :].rearrange("p a t -> p (a t)")
                    xx = X[:, bass.ds(i, 1), :].rearrange("p a t -> p (a t)")
                    c(nc.vector.scalar_tensor_tensor(out=dd, in0=dd, scalar=rd[:, bass.ds(i, 1)], in1=post[:, 2, :],
                                                     op0=ALU.mult, op1=ALU.mult))
                    c(nc.vector.scalar_tensor_tensor(out=xx, in0=dd, scalar=gate[:, 3:4], in1=xx,
                                                     op0=ALU.mult, op1=ALU.add))


BLOCKS1 = (2 * NTOK - 8) // P + 8


def scratch(nc):
    d = {}
    def dram(name, shape, dt=F32):
        d[name] = nc.dram_tensor(f"scr_{name}", shape, dt, kind="Internal").ap()
    dram("qs", [NN, 3, HD, GH, T], BF16)
    dram("ks", [NN, 3, HD, GH, T], BF16)
    dram("mq", [NN, 9, T], BF16)
    dram("mk", [NN, 12, T], BF16)
    dram("mx", [2, 3, GH * HC, P], BF16)
    dram("mrep", [NT, T])
    dram("xg", [NTOK + P, T])
    dram("y", [NTOK + P, T])
    dram("table0", [P, 64, 2], I32)
    dram("nm", [NH, C])
    d["nm1"] = d["nm"].rearrange("(a h) s -> a (h s)", a=1)
    dram("table1", [P, BLOCKS1, 2], I32)
    dram("owner", [1, BLOCKS1], I32)
    dram("dn", [NT, P, T])
    return d


def program(nc, io, out):
    with ExitStack() as ctx:
        X = ctx.enter_context(nc.sbuf_tensor("residual", [P, NT, T], F32))
        K = {"ident": ctx.enter_context(nc.sbuf_tensor("ident", [P, P], F32)),
             "gate": ctx.enter_context(nc.sbuf_tensor("gate", [P, 4], F32)),
             "g_xattn": io["g_xattn"], "g_ffn": io["g_ffn"]}
        S = scratch(nc)
        load_x(nc, io["x"].rearrange("b (c p) t -> (b c) p t", p=P), X)
        constants(nc, K)
        attention(nc, io, X, K, S)
        moe0(nc, io, X, K, S)
        mlstm(nc, io, X, K, S)
        ffn1(nc, io, X, K, S)
        store_x(nc, out.rearrange("b (c p) t -> (b c) p t", p=P), X)


_NAMES = {
    "x": "x", "ctx": "ctx_2048", "mask": "mask_Bx1x2048_fk1", "g_xattn": "g_xattn", "g_ffn": "g_ffn",
    "Wq": "L0_xattn_Wq", "bq": "L0_xattn_bq", "Wk": "L0_xattn_Wk", "bk": "L0_xattn_bk", "Wv": "L0_xattn_Wv",
    "bv": "L0_xattn_bv", "m0_gate_w": "L0_ffn_gate_w", "m0_wg": "L0_ffn_wg", "m0_wu": "L0_ffn_wu",
    "m0_wd": "L0_ffn_wd", "l1_Wi": "L1_xattn_Wi", "l1_bi": "L1_xattn_bi", "l1_Wf": "L1_xattn_Wf",
    "l1_bf": "L1_xattn_bf", "l1_ln_scale": "L1_xattn_ln_scale", "f1_rn_pre1": "L1_ffn_rn_pre1",
    "f1_rn_pre2": "L1_ffn_rn_pre2", "f1_rn_post1": "L1_ffn_rn_post1", "f1_rn_post2": "L1_ffn_rn_post2",
    "f1_rn_post": "L1_ffn_rn_post", "f1_w_gate": "L1_ffn_w_gate", "f1_w_up": "L1_ffn_w_up",
    "f1_w_down": "L1_ffn_w_down", "f1_router_w": "L1_ffn_router_w", "f1_router_scale": "L1_ffn_router_scale",
    "f1_per_expert_scale": "L1_ffn_per_expert_scale", "f1_we_gate": "L1_ffn_we_gate",
    "f1_we_up": "L1_ffn_we_up", "f1_we_down": "L1_ffn_we_down",
}


def kernel(**inputs):
    import numpy as _np
    import concourse.bacc as _bacc
    from concourse import mybir as _mybir
    from concourse.bass_utils import run_bass_kernel_spmd as _run

    nc = _bacc.Bacc("TRN2", target_bir_lowering=False, num_devices=1)
    arrays, io = {}, {}
    for short, name in _NAMES.items():
        a = _np.ascontiguousarray(inputs[name])
        arrays[f"in_{name}"] = a
        io[short] = nc.dram_tensor(f"in_{name}", a.shape, _mybir.dt.from_np(a.dtype), kind="ExternalInput").ap()
    out = nc.dram_tensor("out_0", (B, C, T), F32, kind="ExternalOutput").ap()
    program(nc, io, out)
    r = _run(nc, [arrays], core_ids=[0])
    return r.results[0]["out_0"]
```

```python
import numpy as np
import concourse.bass as bass
from concourse import mybir
from contextlib import ExitStack

F32 = mybir.dt.float32
BF16 = mybir.dt.bfloat16
I32 = mybir.dt.int32
U32 = mybir.dt.uint32
ALU = mybir.AluOpType
ACT = mybir.ActivationFunctionType
AX = mybir.AxisListType

P = 128
B, C, T = 8, 256, 512
CT = C // P
NT = B * CT
NTOK = B * C
HC = T // P
NH = 16


class Chain:

    def __init__(self, eng, sem, base=0):
        self.eng, self.sem, self.base, self.n = eng, sem, base, 0

    def __call__(self, ins):
        self.n += 1
        ins.then_inc(self.sem, 1)
        self.eng.wait_ge(self.sem, self.base + self.n)


class Room:

    def __init__(self, nc, ctx, tag):
        self.nc, self.ctx, self.tag, self.sems = nc, ctx, tag, []
        ctx.callback(self.clear)

    def clear(self):
        if self.sems:
            self.nc.clear_and_free_semaphores(self.sems)
            self.nc.all_engine_barrier()

    def sb(self, name, shape, dt=F32):
        return self.ctx.enter_context(self.nc.sbuf_tensor(f"{self.tag}_{name}", shape, dt))

    def ps(self, name, shape, dt=F32):
        return self.ctx.enter_context(self.nc.psum_tensor(f"{self.tag}_{name}", shape, dt))

    def sem(self, name):
        self.sems.append(self.nc.alloc_semaphore(f"{self.tag}_{name}"))
        return self.sems[-1]

    def block(self):
        return self.ctx.enter_context(self.nc.Block())


def row_of(vector):
    n = vector.shape[0]
    return vector.rearrange("(a n) -> a n", a=1).broadcast_to([P, n])


def load_x(nc, x_dram, X):
    with ExitStack() as ctx:
        r = Room(nc, ctx, "ld")
        loaded = r.sem("loaded")
        block = r.block()

        @block.sync
        def _(sp):
            for i in range(NT):
                sp.dma_start(X[:, i, :], x_dram[i]).then_inc(loaded, 16)
            sp.wait_ge(loaded, 16 * NT)


def store_x(nc, out_dram, X):
    with ExitStack() as ctx:
        r = Room(nc, ctx, "st")
        stored = r.sem("stored")
        block = r.block()

        @block.sync
        def _(sp):
            for i in range(NT):
                sp.dma_start(out_dram[i], X[:, i, :]).then_inc(stored, 16)
            sp.wait_ge(stored, 16 * NT)


def constants(nc, K):
    with ExitStack() as ctx:
        r = Room(nc, ctx, "cst")
        filled = r.sem("filled")
        graw = r.sb("graw", [P, 4])
        gload = r.sem("gload")
        block = r.block()

        @block.gpsimd
        def _(pool):
            nc.gpsimd.memset(K["ident"][:], 0.0).then_inc(filled, 1)
            pool.wait_ge(filled, 1)
            nc.gpsimd.affine_select(out=K["ident"][:], in_=K["ident"][:], compare_op=ALU.not_equal, fill=1.0,
                                    base=0, pattern=[[-1, P]], channel_multiplier=1).then_inc(filled, 1)
            pool.wait_ge(filled, 2)

        @block.sync
        def _(sp):
            sp.dma_start(graw[:, 0:2], row_of(K["g_xattn"])).then_inc(gload, 16)
            sp.dma_start(graw[:, 2:4], row_of(K["g_ffn"])).then_inc(gload, 16)

        @block.scalar
        def _(act):
            act.wait_ge(gload, 32)
            nc.scalar.activation(K["gate"][:], graw[:], ACT.Tanh)


def row_stats(nc, X, tag, eps, rms, mean, rstd, second=None):
    with ExitStack() as ctx:
        r = Room(nc, ctx, tag)
        st = r.sb("bn", [P, NT, 6])
        ag = r.sb("ag", [P, NT, 2])
        v = r.sb("v", [P, NT])
        dv = r.sem("dv")
        root = r.sem("root")
        ready = r.sem("ready")
        block = r.block()

        @block.vector
        def _(dve):
            with dve.Fori(0, NT) as i:
                ins = nc.vector.bn_stats(st[:, i, :], X[:, i, :])
                ins.then_inc(dv, 1)
            dve.wait_ge(dv, NT)
            c = Chain(dve, dv, NT)
            for i in range(NT):
                ins = nc.vector.bn_aggr(ag[:, i, :], st[:, i, :])
            c(ins)
            c(nc.vector.tensor_copy(mean[:], ag[:, :, 0]))
            if rms:
                c(nc.vector.tensor_tensor(v[:], mean[:], mean[:], ALU.mult))
                c(nc.vector.scalar_tensor_tensor(out=v[:], in0=v[:], scalar=eps, in1=ag[:, :, 1],
                                                 op0=ALU.add, op1=ALU.add))
            elif second is not None:
                c(nc.vector.tensor_scalar(v[:], ag[:, :, 1], 1.0 + second, eps * second, ALU.mult, ALU.add))
            else:
                c(nc.vector.tensor_scalar(v[:], ag[:, :, 1], eps, None, ALU.add))
            dve.sem_inc(ready, 1)
            dve.wait_ge(root, 1)
            c(nc.vector.reciprocal(rstd[:], v[:]))

        @block.scalar
        def _(act):
            act.wait_ge(ready, 1)
            nc.scalar.activation(v[:], v[:], ACT.Sqrt).then_inc(root, 1)



HD = 16
GH = 4
NG = NH // GH
NN = B * NG
QROWS = ("h", "h", "m", "h", "l", "m")
KROWS = ("h", "m", "h", "l", "h", "m")
NEG = 1000000.0
MROW = 6 * HD
MAXROW = MROW + 9
NROW = MAXROW + 3
VW = HD + 1


def split3(dve, nc, chain, parts, rest, src):
    chain(nc.vector.tensor_copy(parts[0], src))
    chain(nc.vector.tensor_tensor(rest, src, parts[0], ALU.subtract))
    chain(nc.vector.tensor_copy(parts[1], rest))
    chain(nc.vector.tensor_tensor(rest, rest, parts[1], ALU.subtract))
    chain(nc.vector.tensor_copy(parts[2], rest))


def attention(nc, io, X, K, S):
    ident, gate = K["ident"], K["gate"]
    mask8 = io["mask"].rearrange("b a t -> (b a) t")
    with ExitStack() as outer:
        o = Room(nc, outer, "at")
        mean = o.sb("mean", [P, NT])
        rstd = o.sb("rstd", [P, NT])
        V = o.sb("V", [P, NN, HC * GH * VW])
        row_stats(nc, X, "at_st", 1e-5, False, mean, rstd)

        with ExitStack() as ctx:
            r = Room(nc, ctx, "mk")
            m = r.sb("m", [B, T])
            a = r.sb("a", [B, T])
            rest = r.sb("rest", [B, T])
            mp = r.sb("mp", [B, 3, T], BF16)
            ap = r.sb("ap", [B, 3, T], BF16)
            one = r.sb("one", [B, 3, T], BF16)
            loaded = r.sem("loaded")
            dv = r.sem("dv")
            split = r.sem("split")
            stored = r.sem("stored")
            block = r.block()

            @block.vector
            def _(dve):
                c = Chain(dve, dv)
                c(nc.vector.memset(one[:], 1.0))
                dve.wait_ge(loaded, 16)
                c(nc.vector.tensor_scalar(a[:], m[:], -1.0, NEG, ALU.add, ALU.mult))
                split3(dve, nc, c, [mp[:, j, :] for j in range(3)], rest[:], m[:])
                split3(dve, nc, c, [ap[:, j, :] for j in range(3)], rest[:], a[:])
                dve.sem_inc(split, 1)

            @block.sync
            def _(sp):
                sp.dma_start(m[:], mask8).then_inc(loaded, 16)
                sp.wait_ge(split, 1)
                n = 0
                part = {"h": 0, "m": 1, "l": 2}
                for rows, dst, src in ((QROWS, S["mq"], ap), (KROWS, S["mk"], mp)):
                    view = dst.rearrange("(b g) r t -> b g r t", g=NG)
                    for g in range(NG):
                        for k, w in enumerate(rows):
                            sp.dma_start(view[:, g, k, :], src[:, part[w], :]).then_inc(stored, 16)
                            n += 1
                        tail = one if dst is S["mq"] else ap
                        sp.dma_start(view[:, g, 6:9, :], tail[:]).then_inc(stored, 16)
                        n += 1
                        if dst is S["mk"]:
                            sp.dma_start(view[:, g, 9:12, :], one[:]).then_inc(stored, 16)
                            n += 1
                view = S["mrep"].rearrange("(b c) t -> b c t", c=CT)
                for ct in range(CT):
                    sp.dma_start(view[:, ct, :], m[:]).then_inc(stored, 16)
                    n += 1
                sp.wait_ge(stored, 16 * n)

        with ExitStack() as ctx:
            r = Room(nc, ctx, "pj")
            wraw = r.sb("wraw", [P, 3, CT, C])
            wT = r.sb("wT", [P, 3, CT, C])
            bcol = r.sb("bcol", [P, 2, CT])
            bvb = r.sb("bvb", [P, C])
            smc = r.sb("smc", [P, B, HC])
            tmb = r.sb("tmb", [P, 2, T])
            src = r.sb("src", [P, 2, CT, T])
            xn = r.sb("xn", [P, 2, CT, T])
            full = r.sb("full", [P, 2, T])
            rest = r.sb("rest", [P, 2, T])
            parts = r.sb("parts", [P, 2, 2, 3, T], BF16)
            vt = r.sb("vt", [P, 2, C])
            pt = r.ps("pt", [P, 2, 512])
            pq = r.ps("pq", [P, 2, 512])
            pv = r.ps("pv", [P, 2, 512])
            wload = r.sem("wload")
            transposed = r.sem("transposed")
            evacuated = r.sem("evacuated")
            in_loaded = [r.sem(f"in_loaded{u}") for u in range(2)]
            in_free = [r.sem(f"in_free{u}") for u in range(2)]
            src_free = [r.sem(f"src_free{u}") for u in range(2)]
            normed = r.sem("normed")
            projected = r.sem("projected")
            proj_free = r.sem("proj_free")
            vproj = r.sem("vproj")
            vfree = r.sem("vfree")
            vpart = r.sem("vpart")
            dv = r.sem("dv")
            split_done = [r.sem(f"split_done{u}") for u in range(2)]
            split_stored = [r.sem(f"split_stored{u}") for u in range(2)]
            block = r.block()
            ctx_v = io["ctx"].rearrange("b (c p) t -> b p c t", p=P)

            @block.sync
            def _(sp):
                for k, w in enumerate(("Wq", "Wk", "Wv")):
                    sp.dma_start(wraw[:, k, :, :], io[w].rearrange("(c p) n -> p c n", p=P)).then_inc(wload, 16)
                for k, w in enumerate(("bq", "bk")):
                    for c in range(CT):
                        sp.dma_start(bcol[:, k, c:c + 1], io[w].rearrange("(c p a) -> c p a", p=P, a=1)[c])\
                          .then_inc(wload, 16)
                sp.dma_start(bvb[:], row_of(io["bv"])).then_inc(wload, 16)
                for b in range(B):
                    for c in range(HC):
                        sp.dma_start(smc[:, b, c:c + 1],
                                     io["mask"][b, 0].rearrange("(c p a) -> c p a", p=P, a=1)[c]).then_inc(wload, 16)
                with sp.Fori(0, B // 2) as i:
                    for u in range(2):
                        b = 2 * i + u
                        sp.wait_ge(in_free[u], i + 1)
                        sp.wait_ge(src_free[u], i + 1)
                        sp.dma_start(src[:, u, :, :], ctx_v[b]).then_inc(in_loaded[u], 16)
                        sp.dma_start(tmb[:, u, :], mask8[bass.ds(b, 1)].broadcast_to([P, T])).then_inc(in_loaded[u], 16)

            @block.gpsimd
            def _(pool):
                for u in range(2):
                    pool.sem_inc(in_free[u], 1)
                    pool.sem_inc(src_free[u], 1)
                    pool.sem_inc(split_stored[u], 16)
                pool.sem_inc(proj_free, 2)
                pool.sem_inc(vfree, 2)

            qs_v = [S[k].rearrange("n j d h t -> n h d j t") for k in ("qs", "ks")]

            @block.scalar
            def _(act):
                with act.Fori(0, B) as b:
                    for ct in range(CT):
                        act.wait_ge(split_done[ct], b + 1)
                        for k in range(2):
                            for hh in range(8):
                                n = 4 * b + (ct * 8 + hh) // GH
                                act.dma_start(qs_v[k][n, hh % GH], parts[HD * hh:HD * hh + HD, ct, k, :, :])\
                                   .then_inc(split_stored[ct], 16)
                for ct in range(CT):
                    act.wait_ge(split_stored[ct], 256 * B + 16)

            @block.tensor
            def _(pe):
                pe.wait_ge(wload, 16 * (3 + 4 + 1 + B * HC))
                n = 0
                for k in range(3):
                    for co in range(CT):
                        if n >= 2:
                            pe.wait_ge(evacuated, n - 1)
                        for ci in range(CT):
                            last = nc.tensor.transpose(pt[:, n % 2, ci * P:ci * P + P],
                                                       wraw[:, k, co, ci * P:ci * P + P], ident[:])
                        last.then_inc(transposed, 1)
                        n += 1
                pe.wait_ge(evacuated, n)
                with pe.Fori(0, B // 2) as i:
                    for u in range(2):
                        b = 2 * i + u
                        pe.wait_ge(in_loaded[u], 32 * i + 32)
                        pe.wait_ge(normed, b + 1)
                        for ct in range(CT):
                            for k, rhs in enumerate((xn, src)):
                                pe.wait_ge(proj_free, 4 * b + 2 * ct + k + 1)
                                for c in range(CT):
                                    last = nc.tensor.matmul(pq[:, k, :], wT[:, k, c, ct * P:ct * P + P],
                                                            rhs[:, u, c, :], start=(c == 0), stop=(c == CT - 1))
                                last.then_inc(projected, 1)
                        for s in range(HC):
                            pe.wait_ge(vfree, 4 * b + s + 1)
                            for c in range(CT):
                                last = nc.tensor.matmul(pv[:, s % 2, 0:C], src[:, u, c, s * P:s * P + P],
                                                        wT[:, 2, c, :], start=(c == 0), stop=(c == CT - 1))
                            last.then_inc(vproj, 1)
                        pe.wait_ge(vfree, 4 * b + HC + 2)
                        pe.sem_inc(src_free[u], 1)

            @block.vector
            def _(dve):
                n = 0
                for k in range(3):
                    for co in range(CT):
                        dve.wait_ge(transposed, n + 1)
                        nc.vector.tensor_copy(wT[:, k, :, co * P:co * P + P],
                                              pt[:, n % 2, 0:CT * P].rearrange("p (c n) -> p c n", c=CT))\
                          .then_inc(evacuated, 1)
                        n += 1
                per = CT + CT * 2 * (2 + 5) + HC * 2
                first = Chain(dve, dv)
                first(nc.vector.memset(V[:], 1.0))
                with dve.Fori(0, B // 2) as i:
                    c = Chain(dve, dv, 1 + i * (2 * per))
                    for u in range(2):
                        b = 2 * i + u
                        for ct in range(CT):
                            tile = CT * b + ct
                            c(nc.vector.tensor_scalar(xn[:, u, ct, :], X[:, tile, :],
                                                      mean[:, bass.ds(tile, 1)], rstd[:, bass.ds(tile, 1)],
                                                      ALU.subtract, ALU.mult))
                        dve.sem_inc(normed, 1)
                        dve.wait_ge(in_loaded[u], 32 * i + 32)
                        for ct in range(CT):
                            dve.wait_ge(split_stored[ct], 256 * b + 16)
                            for k in range(2):
                                dve.wait_ge(projected, 4 * b + 2 * ct + k + 1)
                                c(nc.vector.tensor_scalar(full[:, k, :], pq[:, k, :], bcol[:, k, ct:ct + 1],
                                                          HD ** -0.5 if k == 0 else 1.0, ALU.add, ALU.mult))
                                dve.sem_inc(proj_free, 1)
                                c(nc.vector.tensor_tensor(full[:, k, :], full[:, k, :], tmb[:, u, :], ALU.mult))
                                split3(dve, nc, c, [parts[:, ct, k, j, :] for j in range(3)],
                                       rest[:, k, :], full[:, k, :])
                            dve.sem_inc(split_done[ct], 1)
                        dve.sem_inc(in_free[u], 1)
                        for s in range(HC):
                            dve.wait_ge(vproj, 4 * b + s + 1)
                            c(nc.vector.tensor_tensor(vt[:, s % 2, :], pv[:, s % 2, 0:C], bvb[:], ALU.add))
                            dve.sem_inc(vfree, 1)
                            dst = V[:, bass.ds(4 * b, NG), s * GH * VW:(s + 1) * GH * VW]\
                                .rearrange("p g (h w) -> p g h w", h=GH)[:, :, :, 0:HD]
                            c(nc.vector.tensor_scalar(
                                dst, vt[:, s % 2, :].rearrange("p (g h w) -> p g h w", g=NG, h=GH),
                                smc[:, bass.ds(b, 1), s:s + 1].rearrange("p a b -> p (a b)"), None, ALU.mult))
                    assert c.n == 2 * per

        attend(nc, io, X, K, S, V)


def attend(nc, io, X, K, S, V):
    ident, gate = K["ident"], K["gate"]
    RING = 4
    NI = NN // 2
    with ExitStack() as ctx:
        r = Room(nc, ctx, "sm")
        Q = r.sb("Q", [P, RING, GH, T], BF16)
        Kk = r.sb("K", [P, RING, GH, T], BF16)
        negm = r.sb("negm", [P, 2, GH * HC])
        mrow = r.sb("mrow", [GH * HC, 2, P])
        mrest = r.sb("mrest", [GH * HC, P])
        mparts = r.sb("mparts", [GH * HC, 2, 3, P], BF16)
        Pe = r.sb("P", [P, 4, 2, T])
        Vg = r.sb("Vg", [P, 2, HC, GH, 32])
        O = r.sb("O", [P, 4, T])
        rden = r.sb("rden", [P, T])
        tmb = r.sb("tmb", [P, 2, T])
        res = r.sb("res", [P, 2, T])
        dsel = r.sb("dsel", [P, 2, P])
        sel = r.sb("sel", [P, 2, P])
        ps_m = r.ps("ps_m", [P, 2, 512])
        ps_s = r.ps("ps_s", [P, 2, 2, 512])
        ps_o = r.ps("ps_o", [P, 512])
        ps_x = r.ps("ps_x", [P, 512])
        made = r.sem("made")
        stacked = [r.sem(f"stacked{u}") for u in range(RING)]
        m_scored = r.sem("m_scored")
        m_read = r.sem("m_read")
        m_turned = r.sem("m_turned")
        m_copied = r.sem("m_copied")
        cut = r.sem("cut")
        m_split = r.sem("m_split")
        m_stored = r.sem("m_stored")
        m_rows = [r.sem(f"m_rows{u}") for u in range(RING)]
        scored = r.sem("scored")
        exped = r.sem("exped")
        v_ready = r.sem("v_ready")
        valued = r.sem("valued")
        o_copied = r.sem("o_copied")
        den_out = r.sem("den_out")
        reciped = r.sem("reciped")
        picked = r.sem("picked")
        num_read = r.sem("num_read")
        tm_loaded = [r.sem(f"tm_loaded{u}") for u in range(2)]
        masked = r.sem("masked")
        finished = r.sem("finished")
        apart = r.sem("apart")
        block = r.block()

        def steps(eng, step):
            for j in range(2 * RING):
                step(j, j // RING, j % RING)
            with eng.Fori(2, NN // RING) as g:
                for u in range(RING):
                    step(RING * g + u, g, u)
            for j in range(NN, NN + 4):
                step(j, j // RING, j % RING)

        def within(n, lo, hi):
            return not isinstance(n, int) or lo <= n < hi

        @block.gpsimd
        def _(pool):
            nc.gpsimd.memset(dsel[:], 0.0).then_inc(made, 1)
            nc.gpsimd.memset(sel[:], 0.0).then_inc(made, 1)
            nc.gpsimd.memset(Vg[:], 0.0).then_inc(made, 1)
            pool.wait_ge(made, 3)
            for q in range(2):
                v = dsel[:, q, 64 * q:64 * q + 64].rearrange("p (j d) -> p j d", j=GH)
                nc.gpsimd.affine_select(out=v, in_=v, compare_op=ALU.not_equal, fill=1.0, base=-HD,
                                        pattern=[[-32, GH], [0, HD]], channel_multiplier=1).then_inc(made, 1)
                v = sel[:, q, 64 * q:64 * q + 64].rearrange("p (j d) -> p j d", j=GH)
                nc.gpsimd.affine_select(out=v, in_=v, compare_op=ALU.not_equal, fill=1.0, base=0,
                                        pattern=[[-32, GH], [-1, HD]], channel_multiplier=1).then_inc(made, 1)
            pool.wait_ge(made, 7)

            def step(j, g, u):
                q = j - 1
                if within(q, 0, NN):
                    pool.wait_ge(m_copied, q + 1)
                    c = Chain(pool, cut, 4 * q)
                    w = (u - 1) % RING
                    m, mp = mrow[:, w % 2, :], [mparts[:, w % 2, k, :] for k in range(3)]
                    pool.sem_inc(apart, 1)
                    c(nc.gpsimd.tensor_copy(mp[0], m))
                    c(nc.gpsimd.tensor_tensor(mrest[:], m, mp[0], ALU.subtract))
                    pool.sem_inc(apart, 1)
                    c(nc.gpsimd.tensor_copy(mp[1], mrest[:]))
                    c(nc.gpsimd.tensor_tensor(mp[2], mrest[:], mp[1], ALU.subtract))
                    pool.sem_inc(m_split, 1)
                    turn = g + (u - 1) // RING
                    if within(q, RING, NN):
                        pool.wait_ge(m_rows[w], 16 * turn)
                    pool.sem_inc(apart, 1)
                    pool.dma_start(S["mx"][w].rearrange("j k p -> k j p"), mparts[:, w % 2, :, :])\
                        .then_inc(m_stored, 16)
                    pool.wait_ge(m_stored, 16 * q + 16)
                    pool.sem_inc(apart, 1)
                    pool.dma_start(Q[MAXROW:NROW, w, :, :].rearrange("p h t -> p (h t)"),
                                   S["mx"][w].rearrange("j k p -> j (k p)")).then_inc(m_rows[w], 16)
                    if within(q, 2, NN):
                        pool.wait_ge(valued, 4 * q - 4)
                    pool.sem_inc(apart, 1)
                    nc.gpsimd.tensor_copy(Vg[:, w % 2, :, :, 0:VW],
                                          V[:, bass.ds(q, 1), :].rearrange("p a (s h w) -> p (a s) h w", s=HC, h=GH))\
                      .then_inc(v_ready, 1)
                if u % 2 == 1 and within(j, 5, NN + 4):
                    i, b = 2 * g + u // 2 - 2, (u // 2) % 2
                    pool.wait_ge(num_read, i + 1)
                    pool.wait_ge(tm_loaded[b], 16 * g)
                    nc.gpsimd.tensor_tensor(res[:, b, :], res[:, b, :], tmb[:, b, :], ALU.mult).then_inc(masked, 1)
                    pool.wait_ge(masked, i + 1)
                    x = X[:, bass.ds(i, 1), :].rearrange("p a t -> p (a t)")
                    nc.gpsimd.tensor_tensor(x, x, res[:, b, :], ALU.add).then_inc(finished, 1)

            steps(pool, step)
            pool.wait_ge(finished, NI)

        @block.sync
        def _(sp):
            def load(q, w):
                for k in range(6):
                    for dst, name, rows in ((Q, "qs", QROWS), (Kk, "ks", KROWS)):
                        part = {"h": 0, "m": 1, "l": 2}[rows[k]]
                        sp.dma_start(dst[HD * k:HD * k + HD, w, :, :], S[name][q, part]).then_inc(stacked[w], 16)
                for dst, name, rows in ((Q, "mq", 9), (Kk, "mk", 12)):
                    sp.dma_start(dst[MROW:MROW + rows, w, :, :],
                                 S[name][q].unsqueeze(1).broadcast_to([rows, GH, T])).then_inc(stacked[w], 16)

            for q in range(RING):
                load(q, q)

            def step(j, g, u):
                if u % 2 == 0 and within(j, 4, NN + 4):
                    i, b = 2 * g + u // 2 - 2, (u // 2) % 2
                    if within(i, 2, NI):
                        sp.wait_ge(finished, i - 1)
                    sp.dma_start(tmb[:, b, :], S["mrep"][bass.ds(i, 1)].broadcast_to([P, T]))\
                      .then_inc(tm_loaded[b], 16)
                q = j + 2
                if within(q, RING, NN):
                    sp.wait_ge(scored, 8 * q - 24)
                    load(q, (u + 2) % RING)

            for j in range(2 * RING):
                step(j, j // RING, j % RING)
            with sp.Fori(2, NN // RING - 1) as g:
                for u in range(RING):
                    step(RING * g + u, g, u)
            for j in range(NN - RING, NN + 4):
                step(j, j // RING, j % RING)

        STACK = 16 * (12 + 2)

        @block.tensor
        def _(pe):
            pe.wait_ge(made, 7)

            def maxima(n, g, u, half):
                for k in (2 * half, 2 * half + 1):
                    h, t = k // HC, k % HC
                    if k == 0:
                        pe.wait_ge(stacked[u], STACK * g + STACK)
                    if not isinstance(n, int) or n > 0 or k >= 2:
                        pe.wait_ge(m_read, GH * HC * n + k - 1)
                    nc.tensor.matmul(ps_m[:, k % 2, :], Q[0:MAXROW, u, h, t * P:t * P + P],
                                     Kk[0:MAXROW, u, h, :], start=True, stop=True).then_inc(m_scored, 1)

            def values(n, w, s):
                pe.wait_ge(exped, 8 * n + 2 * s + 2)
                if s == 0:
                    pe.wait_ge(v_ready, n + 1)
                    if within(n, 1, NN):
                        pe.wait_ge(o_copied, n)
                for h in range(GH):
                    last = nc.tensor.matmul(ps_o[32 * h:32 * h + 32, :], Vg[:, w % 2, s, h, :],
                                            Pe[:, 2 * (s % 2) + h // 2, h % 2, :],
                                            start=(s == 0), stop=(s == HC - 1), skip_group_check=True)
                last.then_inc(valued, 1)

            def step(j, g, u):
                n, w = j - 2, (u - 2) % RING
                i = 2 * g + u // 2 - 2
                for half in range(8):
                    s, hp = half // 2, half % 2
                    if within(j, 0, NN):
                        maxima(j, g, u, half)
                    if within(n, 0, NN):
                        if half == 0:
                            pe.wait_ge(m_rows[w], 16 * (g + (u - 2) // RING) + 16)
                        if not isinstance(n, int) or n > 0 or half >= 2:
                            pe.wait_ge(exped, 8 * n + half - 1)
                        for h in range(2):
                            last = nc.tensor.matmul(ps_s[:, hp, h, :],
                                                    Kk[0:NROW, w, 2 * hp + h, s * P:s * P + P],
                                                    Q[0:NROW, w, 2 * hp + h, :], start=True, stop=True)
                        last.then_inc(scored, 1)
                    if half == 1 and within(j - 1, 0, NN):
                        pe.wait_ge(m_read, GH * HC * j)
                        if u % 2 == 0 and within(j, 6, NN + 4):
                            pe.wait_ge(num_read, i)
                        elif u % 2 == 1 and within(j, 5, NN + 4):
                            pe.wait_ge(reciped, 4 * i + 4)
                        elif j >= 2:
                            pe.wait_ge(m_copied, j - 1)
                        nc.tensor.transpose(ps_x[0:GH * HC, 0:P], negm[:, (u - 1) % 2, :], ident[:]).then_inc(m_turned, 1)
                    if half == 1 and within(j - 3, 0, NN):
                        values(j - 3, (u - 3) % RING, HC - 1)
                    elif hp == 1 and half > 1 and within(n, 0, NN):
                        values(n, w, s - 1)
                    if half == 3 and within(j, 4, NN + 4):
                        if within(j - 1, 0, NN):
                            pe.wait_ge(m_copied, j)
                        elif u % 2 == 0:
                            pe.wait_ge(num_read, i)
                        if u % 2 == 0:
                            pe.wait_ge(o_copied, 2 * i + 2)
                            for q in range(2):
                                last = nc.tensor.matmul(ps_x[:], dsel[:, q, :], O[:, 2 * (u // 2 % 2) + q, :],
                                                        start=(q == 0), stop=(q == 1))
                            last.then_inc(den_out, 1)
                        elif within(j, 5, NN + 4):
                            pe.wait_ge(reciped, 4 * i + 4)
                            for q in range(2):
                                last = nc.tensor.matmul(ps_x[:], sel[:, q, :], O[:, 2 * (u // 2 % 2) + q, :],
                                                        start=(q == 0), stop=(q == 1))
                            last.then_inc(picked, 1)

            steps(pe, step)

        @block.scalar
        def _(act):
            def step(j, g, u):
                n = j - 2
                for half in range(8):
                    s, hp = half // 2, half % 2
                    if within(n, 0, NN):
                        if hp == 0 and (not isinstance(n, int) or n > 0 or s >= 2):
                            act.wait_ge(valued, 4 * n + s - 1)
                        act.wait_ge(scored, 8 * n + half + 1)
                        nc.scalar.activation(Pe[:, 2 * (s % 2) + hp, :, :], ps_s[:, hp, :, :], ACT.Exp)\
                          .then_inc(exped, 1)
                    if half == 1 and within(j - 1, 0, NN):
                        act.wait_ge(m_turned, j)
                        if within(j - 1, 2, NN):
                            act.wait_ge(m_split, j - 2)
                        nc.scalar.activation(mrow[:, (u - 1) % 2, :], ps_x[0:GH * HC, 0:P], ACT.Copy)\
                          .then_inc(m_copied, 1)
                    if half == 1 and within(j - 3, 0, NN):
                        act.wait_ge(valued, 4 * (j - 3) + 4)
                        if within(j - 3, 4, NN):
                            act.wait_ge(picked, 2 * g + (u - 3) // 2 - 1)
                        nc.scalar.activation(O[:, (u - 3) % 4, :], ps_o[:], ACT.Copy).then_inc(o_copied, 1)

            steps(act, step)

        @block.vector
        def _(dve):
            def step(j, g, u):
                i, b = 2 * g + u // 2 - 2, (u // 2) % 2
                for half in range(8):
                    if within(j, 0, NN):
                        if half == 0 and within(j, 2, NN):
                            dve.wait_ge(m_turned, j - 1)
                        for k in (2 * half, 2 * half + 1):
                            dve.wait_ge(m_scored, GH * HC * j + k + 1)
                            nc.vector.tensor_reduce(negm[:, u % 2, k:k + 1], ps_m[:, k % 2, :], AX.X, ALU.max,
                                                    negate=True).then_inc(m_read, 1)
                    if u % 2 == 0 and half >= 4 and within(j, 4, NN + 4):
                        dve.wait_ge(den_out, i + 1)
                        if within(i, 1, NI):
                            dve.wait_ge(num_read, i)
                        q = slice((half - 4) * P, (half - 3) * P)
                        nc.vector.reciprocal(rden[:, q], ps_x[:, q]).then_inc(reciped, 1)
                    if u % 2 == 1 and half == 5 and within(j, 5, NN + 4):
                        dve.wait_ge(picked, i + 1)
                        dve.wait_ge(reciped, 4 * i + 4)
                        if within(i, 2, NI):
                            dve.wait_ge(finished, i - 1)
                        nc.vector.scalar_tensor_tensor(out=res[:, b, :], in0=ps_x[:], scalar=gate[:, 0:1],
                                                       in1=rden[:], op0=ALU.mult, op1=ALU.mult).then_inc(num_read, 1)

            steps(dve, step)



BIG = 1048576.0
MAGIC = 12582912.0


def route(nc, io, X, K, S, tag, E, TOP, logit_w, mean, rstd, table, slots, dense=None, scale=None, owner=None):
    ident = K["ident"]
    per_tile = owner is None
    with ExitStack() as ctx:
        r = Room(nc, ctx, tag)
        wraw = r.sb("wraw", [P, HC, E])
        grow = r.sb("grow", [E, T]) if per_tile else None
        rsc = r.sb("rsc", [P, HC])
        pre = r.sb("pre", [P, HC])
        xn = r.sb("xn", [P, T])
        xnT = r.sb("xnT", [P, T])
        lg = r.sb("lg", [P, E])
        m8 = r.sb("m8", [P, 8])
        i8 = r.sb("i8", [P, 8], U32)
        if8 = r.sb("if8", [P, 8])
        nm = r.sb("nm", [P, 1])
        e8 = r.sb("e8", [P, TOP])
        esum = r.sb("esum", [P, 1])
        NE = 1 if per_tile else NT
        eq = r.sb("eq", [P, NE, TOP, E])
        eqs = r.sb("eqs", [P, NE, TOP, E])
        pos = r.sb("pos", [P, NE, E])
        t1 = r.sb("t1", [P, NE, E])
        row = r.sb("row", [P, NE, E])
        rowf = r.sb("rowf", [P, NE, TOP])
        rowi = r.sb("rowi", [P, NE, TOP], I32)
        pair = r.sb("pair", [P, NE, TOP, 2], I32)
        sel = r.sb("sel", [P, E], BF16)
        ssum = r.sb("ssum", [P, E], BF16)
        upper = r.sb("upper", [P, P], BF16)
        ones = r.sb("ones", [P, P], BF16)
        ioe = r.sb("ioe", [P, E])
        tok = r.sb("tok", [P, NT], I32)
        first = r.sb("first", [P, slots, 2], I32)
        zeros = r.sb("zeros", [P, T])
        psb = r.sb("psb", [P, E])
        counts = r.sb("counts", [P, 4, E])
        iob = r.sb("iob", [P, slots, E])
        own = r.sb("own", [P, slots])
        owni = r.sb("owni", [P, slots], I32)
        ps_t = r.ps("ps_t", [P, 512])
        ps_l = r.ps("ps_l", [P, 512])
        ps_p = r.ps("ps_p", [P, 512])
        made = r.sem("made")
        loaded = r.sem("loaded")
        inited = r.sem("inited")
        wready = r.sem("wready")
        wturned = r.sem("wturned")
        normed = r.sem("normed")
        stored = r.sem("stored")
        turned = r.sem("turned")
        xT_ready = r.sem("xT_ready")
        logits = r.sem("logits")
        top_ready = r.sem("top_ready")
        e_ready = r.sem("e_ready")
        sel_ready = r.sem("sel_ready")
        pos_ready = r.sem("pos_ready")
        sum_ready = r.sem("sum_ready")
        pair_ready = r.sem("pair_ready")
        scattered = r.sem("scattered")
        pair_free = r.sem("pair_free")
        own_ready = r.sem("own_ready")
        own_stored = r.sem("own_stored")
        dv = r.sem("dv")
        apart = r.sem("apart")
        block = r.block()

        @block.gpsimd
        def _(pool):
            nc.gpsimd.memset(ones[:], 1.0).then_inc(made, 1)
            nc.gpsimd.memset(upper[:], 1.0).then_inc(made, 1)
            nc.gpsimd.memset(ssum[:], 0.0).then_inc(made, 1)
            nc.gpsimd.memset(zeros[:], 0.0).then_inc(made, 1)
            nc.gpsimd.memset(first[:], 0).then_inc(made, 1)
            pool.wait_ge(made, 5)
            nc.gpsimd.affine_select(out=upper[:], in_=upper[:], compare_op=ALU.is_gt, fill=0.0, base=0,
                                    pattern=[[1, P]], channel_multiplier=-1).then_inc(made, 1)
            nc.gpsimd.iota(ioe[:], [[1, E]], base=0, channel_multiplier=0,
                           allow_small_or_imprecise_dtypes=True).then_inc(made, 1)
            nc.gpsimd.iota(tok[:], [[P, NT]], base=0, channel_multiplier=1).then_inc(made, 1)
            nc.gpsimd.iota(first[:, :, 0], [[0, slots]], base=NTOK, channel_multiplier=1).then_inc(made, 1)
            nc.gpsimd.iota(iob[:], [[1, slots], [0, E]], base=0, channel_multiplier=0,
                           allow_small_or_imprecise_dtypes=True).then_inc(made, 1)
            pool.sem_inc(stored, 16)
            pool.sem_inc(pair_free, 1)
            pool.wait_ge(inited, 16)

            def scatter(t, i):
                for k in range(TOP):
                    pool.indirect_dma_start(
                        out=table.rearrange("c b w -> (c b) w"),
                        out_offset=bass.IndirectOffsetOnAxis(ap=rowi[:, t, k:k + 1], axis=0),
                        in_=pair[:, t, k, :], in_offset=None, bounds_check=P * slots - 1, oob_is_err=False)\
                        .then_inc(scattered, 16)

            if per_tile:
                with pool.Fori(0, NT) as i:
                    pool.wait_ge(pair_ready, i + 1)
                    pool.sem_inc(apart, 1)
                    scatter(0, i)
                    pool.wait_ge(scattered, 16 * TOP * i + 16 * TOP)
                    pool.sem_inc(pair_free, 1)
            else:
                pool.wait_ge(pair_ready, 1)
                for t in range(NT):
                    scatter(t, 0)
            pool.wait_ge(scattered, 16 * TOP * NT)

        @block.sync
        def _(sp):
            if per_tile:
                sp.dma_start(grow[:], logit_w).then_inc(loaded, 16)
            else:
                sp.dma_start(wraw[:], logit_w.rearrange("(p c) e -> p c e", c=HC)).then_inc(loaded, 16)
                sp.dma_start(rsc[:], io["f1_router_scale"].rearrange("(p c) -> p c", c=HC)).then_inc(loaded, 16)
                sp.dma_start(pre[:], io["f1_rn_pre1"].rearrange("(p c) -> p c", c=HC)).then_inc(loaded, 16)
                sp.dma_start(psb[:], row_of(scale)).then_inc(loaded, 16)
            sp.wait_ge(made, 10)
            sp.dma_start(table, first[:]).then_inc(inited, 16)
            for y in range(NTOK // P + 1):
                for k in range(2):
                    sp.dma_start(S[f"y{k}"][y * P:y * P + P], zeros[:]).then_inc(own_stored, 16)
            sp.dma_start(S["xg"][NTOK:NTOK + P], zeros[:]).then_inc(own_stored, 16)
            with sp.Fori(0, NT) as i:
                sp.wait_ge(normed, i + 1)
                sp.dma_start(S["xg"][bass.ds(P * i, P)], xn[:]).then_inc(stored, 16)
            sp.wait_ge(stored, 16 * NT + 16)
            n = 16 * (2 * (NTOK // P + 1) + 1)
            if not per_tile:
                sp.wait_ge(own_ready, 1)
                sp.dma_start(owner, owni[0:1, :]).then_inc(own_stored, 16)
                n += 16
            sp.wait_ge(own_stored, n)

        @block.tensor
        def _(pe):
            if per_tile:
                pe.wait_ge(loaded, 16)
                gv = grow[:].rearrange("e (p c) -> e c p", c=HC)
                for c in range(HC):
                    last = nc.tensor.transpose(ps_t[:, c * E:c * E + E], gv[:, c, :], ident[0:E, 0:E])
                last.then_inc(wturned, 1)
            pe.wait_ge(made, 10)
            pe.wait_ge(wready, 1)
            xv = xn[:].rearrange("q (p c) -> q c p", c=HC)
            with pe.Fori(0, NT) as i:
                pe.wait_ge(normed, i + 1)
                for c in range(HC):
                    last = nc.tensor.transpose(ps_t[:, c * P:c * P + P], xv[:, c, :], ident[:])
                last.then_inc(turned, 1)
                pe.wait_ge(xT_ready, i + 1)
                for c in range(HC):
                    last = nc.tensor.matmul(ps_l[:, 0:E], xnT[:, c * P:c * P + P], wraw[:, c, :],
                                            start=(c == 0), stop=(c == HC - 1))
                last.then_inc(logits, 1)
                pe.wait_ge(sel_ready, i + 1)
                nc.tensor.matmul(ps_p[:, 0:E], ones[:], ssum[:], start=True, stop=False)
                nc.tensor.matmul(ps_p[:, 0:E], upper[:], sel[:], start=False, stop=True).then_inc(pos_ready, 1)
            if not per_tile:
                pe.wait_ge(sum_ready, 1)
                nc.tensor.matmul(ps_p[:, 0:E], ones[:], ssum[:], start=True, stop=True).then_inc(pos_ready, 1)

        @block.scalar
        def _(act):
            with act.Fori(0, NT) as i:
                act.wait_ge(turned, i + 1)
                nc.scalar.activation(xnT[:], ps_t[:], ACT.Copy).then_inc(xT_ready, 1)
                act.wait_ge(top_ready, i + 1)
                nc.scalar.activation(e8[:], m8[:, 0:TOP], ACT.Exp, bias=nm[:, 0:1]).then_inc(e_ready, 1)

        @block.vector
        def _(dve):
            setup = Chain(dve, dv)
            dve.wait_ge(made, 10)
            if per_tile:
                dve.wait_ge(wturned, 1)
                setup(nc.vector.tensor_copy(wraw[:], ps_t[:, 0:HC * E].rearrange("p (c e) -> p c e", c=HC)))
            else:
                dve.wait_ge(loaded, 64)
                for c in range(HC):
                    ins = nc.vector.tensor_scalar(wraw[:, c, :], wraw[:, c, :], rsc[:, c:c + 1], T ** -0.5,
                                                  ALU.mult, ALU.mult)
                setup(ins)
            dve.sem_inc(wready, 1)
            base = setup.n
            per = PER_TILE_STEPS[per_tile]

            with dve.Fori(0, NT) as i:
                c = Chain(dve, dv, base + i * per)
                t = 0 if per_tile else i
                one = bass.ds(t, 1)
                dve.wait_ge(stored, 16 * i + 16)
                c(nc.vector.tensor_scalar(xn[:], X[:, bass.ds(i, 1), :].rearrange("p a t -> p (a t)"),
                                          mean[:, bass.ds(i, 1)], rstd[:, bass.ds(i, 1)],
                                          ALU.subtract, ALU.mult))
                dve.sem_inc(normed, 1)
                if dense is not None:
                    dve.wait_ge(xT_ready, i + 1)
                    d = dense[:, :, bass.ds(P * i, P)]
                    c(nc.vector.tensor_tensor(d, xnT[:].rearrange("p (c n) -> p c n", c=HC),
                                              pre[:].unsqueeze(2).broadcast_to([P, HC, P]), ALU.mult))
                dve.wait_ge(logits, i + 1)
                c(nc.vector.tensor_copy(lg[:], ps_l[:, 0:E]))
                dve.sem_inc(apart, 1)
                c(nc.vector.max(m8[:], lg[:]))
                c(nc.vector.tensor_scalar(nm[:], m8[:, 0:1], -1.0, None, ALU.mult))
                dve.sem_inc(top_ready, 1)
                c(nc.vector.max_index(i8[:], m8[:], lg[:]))
                c(nc.vector.tensor_copy(if8[:], i8[:]))
                shape = [P, TOP, E]
                e3 = eq[:, one, :, :].rearrange("p a k e -> p (a k) e")
                c(nc.vector.tensor_tensor(e3, ioe[:].unsqueeze(1).broadcast_to(shape),
                                          if8[:, 0:TOP].unsqueeze(2).broadcast_to(shape), ALU.is_equal))
                dve.sem_inc(apart, 1)
                with nc.allow_low_precision(reason="counts of zero or one"):
                    c(nc.vector.tensor_reduce(sel[:], e3.rearrange("p k e -> p e k"), AX.X, ALU.add))
                dve.sem_inc(sel_ready, 1)
                dve.wait_ge(pos_ready, i + 1)
                p2 = pos[:, one, :].rearrange("p a e -> p (a e)")
                c(nc.vector.tensor_copy(p2, ps_p[:, 0:E]))
                c(nc.vector.tensor_tensor(ssum[:], ssum[:], sel[:], ALU.add))
                if per_tile:
                    dve.wait_ge(pair_free, i + 1)
                    c(nc.vector.tensor_scalar(t1[:, 0, :], pos[:, 0, :], float(P), BIG, ALU.is_ge, ALU.mult))
                    c(nc.vector.scalar_tensor_tensor(out=row[:, 0, :], in0=pos[:, 0, :], scalar=float(E),
                                                     in1=t1[:, 0, :], op0=ALU.mult, op1=ALU.add))
                    c(nc.vector.tensor_tensor(row[:, 0, :], row[:, 0, :], ioe[:], ALU.add))
                    c(nc.vector.tensor_tensor(eqs[:, 0], eq[:, 0], row[:, 0, :].unsqueeze(1).broadcast_to(shape),
                                              ALU.mult))
                    c(nc.vector.tensor_reduce(rowf[:, 0, :], eqs[:, 0], AX.X, ALU.add))
                    c(nc.vector.tensor_copy(rowi[:, 0, :], rowf[:, 0, :]))
                dve.wait_ge(e_ready, i + 1)
                c(nc.vector.tensor_reduce(esum[:], e8[:], AX.X, ALU.add))
                c(nc.vector.reciprocal(esum[:], esum[:]))
                w = pair[:, one, :, 1:2].bitcast(F32).rearrange("p a k w -> p (a k w)")
                c(nc.vector.tensor_scalar(w, e8[:], esum[:, 0:1], None, ALU.mult))
                tk = pair[:, one, :, 0:1].rearrange("p a k w -> p (a k w)")
                c(nc.vector.tensor_copy(tk, tok[:, bass.ds(i, 1)].broadcast_to([P, TOP])))
                if scale is not None:
                    g3 = eqs[:, one, :, :].rearrange("p a k e -> p (a k) e")
                    c(nc.vector.tensor_tensor(g3, e3, psb[:].unsqueeze(1).broadcast_to(shape), ALU.mult))
                    dve.sem_inc(apart, 1)
                    r2 = rowf[:, one, :].rearrange("p a k -> p (a k)")
                    c(nc.vector.tensor_reduce(r2, g3, AX.X, ALU.add))
                    c(nc.vector.tensor_tensor(w, w, r2, ALU.mult))
                if per_tile:
                    dve.sem_inc(pair_ready, 1)
                assert c.n == per, c.n
            if not per_tile:
                c = Chain(dve, dv, base + NT * per)
                dve.sem_inc(sum_ready, 1)
                dve.wait_ge(pos_ready, NT + 1)
                total, nblk, incl, ob = (counts[:, k, :] for k in range(4))
                c(nc.vector.tensor_scalar(total, ps_p[:, 0:E], P / 2 - 0.5, 1.0 / P, ALU.add, ALU.mult))
                c(nc.vector.tensor_scalar(nblk, total, MAGIC, None, ALU.add))
                c(nc.vector.tensor_scalar(nblk, nblk, -MAGIC, None, ALU.add))
                c(nc.vector.memset(total, 1.0))
                c(nc.vector.tensor_tensor_scan(incl, total, nblk, 0.0, ALU.mult, ALU.add))
                c(nc.vector.tensor_tensor(ob, incl, nblk, ALU.subtract))
                c(nc.vector.tensor_tensor(iob[:], iob[:], incl.unsqueeze(1).broadcast_to([P, slots, E]), ALU.is_ge))
                c(nc.vector.tensor_reduce(own[:], iob[:], AX.X, ALU.add))
                c(nc.vector.tensor_scalar(own[:], own[:], float(E - 1), None, ALU.min))
                c(nc.vector.tensor_copy(owni[:], own[:]))
                dve.sem_inc(own_ready, 1)
                c(nc.vector.tensor_scalar(t1[:], pos[:], -(P / 2 - 0.5), 1.0 / P, ALU.add, ALU.mult))
                c(nc.vector.tensor_scalar(t1[:], t1[:], MAGIC, None, ALU.add))
                c(nc.vector.tensor_scalar(t1[:], t1[:], -MAGIC, 1.0 - P * slots, ALU.add, ALU.mult))
                c(nc.vector.scalar_tensor_tensor(out=row[:], in0=pos[:], scalar=float(slots), in1=t1[:],
                                                 op0=ALU.mult, op1=ALU.add))
                c(nc.vector.tensor_tensor(row[:], row[:], ob.unsqueeze(1).broadcast_to([P, NT, E]), ALU.add))
                for k in range(TOP):
                    c(nc.vector.tensor_tensor(eqs[:, :, k, :], eq[:, :, k, :], row[:], ALU.mult))
                c(nc.vector.tensor_reduce(rowf[:], eqs[:], AX.X, ALU.add))
                c(nc.vector.tensor_copy(rowi[:], rowf[:]))
                dve.sem_inc(pair_ready, 1)


PER_TILE_STEPS = {True: 20, False: 18}


def experts(nc, io, S, tag, I, blocks, table, wg, wu, wd, func, pre, owner=None):
    IC = I // 2
    RING = 4
    AHEAD = 6
    RI = 8
    with ExitStack() as ctx:
        r = Room(nc, ctx, tag)
        tab = r.sb("tab", [P, blocks, 2], I32)
        ow = r.sb("ow", [1, blocks], I32)
        prec = r.sb("prec", [P, HC])
        idx = r.sb("idx", [P, RI, 1], I32)
        xe = r.sb("xe", [P, RING, T])
        xeT = r.sb("xeT", [P, 2, T])
        wgu = r.sb("wgu", [P, RING, HC, 2 * I])
        wdn = r.sb("wdn", [IC, RING, 2, T])
        sg = r.sb("sg", [P, 2, I])
        h = r.sb("h", [P, 2, I])
        hT = r.sb("hT", [IC, 2, 2 * P])
        oe = r.sb("oe", [P, RING, T])
        ident = r.sb("id", [P, P])
        ps_t = r.ps("ps_t", [P, 2, 512])
        ps_g = r.ps("ps_g", [P, 2, 512])
        ps_h = r.ps("ps_h", [P, 2, 512])
        ps_d = r.ps("ps_d", [P, 2, 512])
        made = r.sem("made")
        tabbed = r.sem("tabbed")
        indexed = r.sem("indexed")
        gathered = [r.sem(f"gathered{u}") for u in range(RING)]
        turned = r.sem("turned")
        xT_ready = r.sem("xT_ready")
        w_in = [r.sem(f"w_in{u}") for u in range(RING)]
        d_in = [r.sem(f"d_in{u}") for u in range(RING)]
        gated = r.sem("gated")
        acted = r.sem("acted")
        h_ready = r.sem("h_ready")
        h_turned = r.sem("h_turned")
        hT_ready = r.sem("hT_ready")
        downed = r.sem("downed")
        o_ready = r.sem("o_ready")
        added = [r.sem(f"added{u}") for u in range(2)]
        apart = r.sem("apart")
        block = r.block()
        TABBED = 48 if owner is not None else 32

        def schedule(eng, *stages):
            def turn(g, u):
                for s, stage in enumerate(stages):
                    n, past = RING * g + u - s, (u - s) // RING
                    if not isinstance(n, int) or 0 <= n < blocks:
                        stage(n, g + past, (u - s) % RING)

            for j in range(2 * RING):
                turn(j // RING, j % RING)
            with eng.Fori(2, blocks // RING) as g:
                for u in range(RING):
                    turn(g, u)
            for j in range(blocks // RING * RING, blocks + len(stages) - 1):
                turn(j // RING, j % RING)

        @block.gpsimd
        def _(pool):
            nc.gpsimd.memset(ident[:], 0.0).then_inc(made, 1)
            pool.wait_ge(made, 1)
            nc.gpsimd.affine_select(out=ident[:], in_=ident[:], compare_op=ALU.not_equal, fill=1.0,
                                    base=0, pattern=[[-1, P]], channel_multiplier=1).then_inc(made, 1)
            pool.wait_ge(tabbed, TABBED)

            def gather(n, u):
                nc.gpsimd.tensor_copy(idx[:, u, :], tab[:, bass.ds(n, 1), 0]).then_inc(indexed, 1)
                pool.wait_ge(indexed, n + 1)
                if not isinstance(n, int) or n >= RING:
                    pool.wait_ge(turned, n - RING + 1)
                pool.sem_inc(apart, 1)
                pool.indirect_dma_start(out=xe[:, u % RING, :], out_offset=None, in_=S["xg"],
                                        in_offset=bass.IndirectOffsetOnAxis(ap=idx[:, u, 0:1], axis=0))\
                    .then_inc(gathered[u % RING], 16)

            def scatter(n, g, u):
                if not isinstance(n, int) or n >= 2:
                    pool.wait_ge(added[u % 2], 16 * (RI // 2 * g + u // 2))
                pool.wait_ge(o_ready, n + 1)
                pool.sem_inc(apart, 1)
                pool.indirect_dma_start(out=S[f"y{u % 2}"],
                                        out_offset=bass.IndirectOffsetOnAxis(ap=idx[:, u, 0:1], axis=0),
                                        in_=oe[:, u % RING, :], in_offset=None, compute_op=ALU.add)\
                    .then_inc(added[u % 2], 16)

            for n in range(AHEAD):
                gather(n, n)
            for n in range(RI):
                scatter(n, 0, n)
                gather(n + AHEAD, (n + AHEAD) % RI)
            groups = (blocks - AHEAD) // RI
            with pool.Fori(1, groups) as g:
                for u in range(RI):
                    scatter(RI * g + u, g, u)
                    gather(RI * g + u + AHEAD, (u + AHEAD) % RI)
            for n in range(RI * groups, blocks):
                scatter(n, n // RI, n % RI)
                if n + AHEAD < blocks:
                    gather(n + AHEAD, (n + AHEAD) % RI)
            for k in range(2):
                pool.wait_ge(added[k], 16 * ((blocks + 1 - k) // 2))

        @block.sync
        def _(sp):
            sp.dma_start(tab[:], table).then_inc(tabbed, 16)
            if pre is not None:
                sp.dma_start(prec[:], pre.rearrange("(p c) -> p c", c=HC)).then_inc(tabbed, 16)
            else:
                sp.sem_inc(tabbed, 16)
            if owner is not None:
                sp.dma_start(ow[:], owner).then_inc(tabbed, 16)
                sp.wait_ge(tabbed, TABBED)

            def weights(n, g, u):
                e = n
                if owner is not None:
                    e = sp.value_load(ow[0:1, bass.ds(n, 1)], min_val=0, max_val=wg.shape[0] - 1)
                e = bass.ds(e, 1)
                old = not isinstance(n, int) or n >= RING
                if old:
                    sp.wait_ge(gated, n - RING + 1)
                for k, w in enumerate((wg, wu)):
                    sp.dma_start(wgu[:, u, :, k * I:k * I + I],
                                 w[e].rearrange("a (p c) i -> p (a c) i", c=HC)).then_inc(w_in[u], 16)
                if old:
                    sp.wait_ge(downed, n - RING + 1)
                sp.dma_start(wdn[:, u, :, :], wd[e].rearrange("a (p c) n -> p (a c) n", c=2)).then_inc(d_in[u], 16)

            schedule(sp, weights)

        @block.tensor
        def _(pe):
            pe.wait_ge(made, 2)

            def turn_rows(n, g, u):
                pe.wait_ge(gathered[u], 16 * g + 16)
                if not isinstance(n, int) or n >= 2:
                    pe.wait_ge(xT_ready, n - 1)
                xv = xe[:, u, :].rearrange("q (p c) -> q c p", c=HC)
                for c in range(HC):
                    last = nc.tensor.transpose(ps_t[:, u % 2, c * P:c * P + P], xv[:, c, :], ident[:])
                last.then_inc(turned, 1)

            def gate_up(n, g, u):
                pe.wait_ge(xT_ready, n + 1)
                pe.wait_ge(w_in[u], 32 * g + 32)
                if not isinstance(n, int) or n >= 2:
                    pe.wait_ge(h_ready, n - 1)
                for c in range(HC):
                    last = nc.tensor.matmul(ps_g[:, u % 2, 0:2 * I], xeT[:, u % 2, c * P:c * P + P],
                                            wgu[:, u, c, :], start=(c == 0), stop=(c == HC - 1))
                last.then_inc(gated, 1)

            def turn_hidden(n, g, u):
                pe.wait_ge(h_ready, n + 1)
                if not isinstance(n, int) or n >= 2:
                    pe.wait_ge(hT_ready, n - 1)
                hv = h[:, u % 2, :].rearrange("q (p c) -> q c p", c=2)
                for c in range(2):
                    last = nc.tensor.transpose(ps_h[0:IC, u % 2, c * P:c * P + P], hv[:, c, :], ident[:])
                last.then_inc(h_turned, 1)

            def down(n, g, u):
                pe.wait_ge(hT_ready, n + 1)
                pe.wait_ge(d_in[u], 16 * g + 16)
                if not isinstance(n, int) or n >= 2:
                    pe.wait_ge(o_ready, n - 1)
                for c in range(2):
                    last = nc.tensor.matmul(ps_d[:, u % 2, :], hT[:, u % 2, c * P:c * P + P], wdn[:, u, c, :],
                                            start=(c == 0), stop=(c == 1))
                last.then_inc(downed, 1)

            schedule(pe, turn_rows, gate_up, turn_hidden, down)

        @block.scalar
        def _(act):
            act.wait_ge(tabbed, TABBED)

            def copy_rows(n, g, u):
                act.wait_ge(turned, n + 1)
                if not isinstance(n, int) or n >= 2:
                    act.wait_ge(gated, n - 1)
                if pre is None:
                    nc.scalar.activation(xeT[:, u % 2, :], ps_t[:, u % 2, :], ACT.Copy).then_inc(xT_ready, 1)
                else:
                    for c in range(HC):
                        ins = nc.scalar.activation(xeT[:, u % 2, c * P:c * P + P], ps_t[:, u % 2, c * P:c * P + P],
                                                   ACT.Copy, scale=prec[:, c:c + 1])
                    ins.then_inc(xT_ready, 1)

            def gate(n, g, u):
                act.wait_ge(gated, n + 1)
                if not isinstance(n, int) or n >= 2:
                    act.wait_ge(h_ready, n - 1)
                nc.scalar.activation(sg[:, u % 2, :], ps_g[:, u % 2, 0:I], func).then_inc(acted, 1)

            def copy_hidden(n, g, u):
                act.wait_ge(h_turned, n + 1)
                if not isinstance(n, int) or n >= 2:
                    act.wait_ge(downed, n - 1)
                nc.scalar.activation(hT[:, u % 2, :], ps_h[0:IC, u % 2, 0:2 * P], ACT.Copy).then_inc(hT_ready, 1)

            schedule(act, copy_rows, gate, copy_hidden)

        @block.vector
        def _(dve):
            dve.wait_ge(tabbed, TABBED)
            wcol = tab[:].bitcast(F32)

            def rows_alone(n, g, u):
                return

            def hidden(n, g, u):
                dve.wait_ge(acted, n + 1)
                if not isinstance(n, int) or n >= 2:
                    dve.wait_ge(h_turned, n - 1)
                nc.vector.scalar_tensor_tensor(out=h[:, u % 2, :], in0=ps_g[:, u % 2, I:2 * I],
                                               scalar=wcol[:, bass.ds(n, 1), 1],
                                               in1=sg[:, u % 2, :], op0=ALU.mult, op1=ALU.mult).then_inc(h_ready, 1)

            def results(n, g, u):
                dve.wait_ge(downed, n + 1)
                if not isinstance(n, int) or n >= RING:
                    dve.wait_ge(added[u % 2], 16 * (RING // 2 * (g - 1) + u // 2 + 1))
                nc.vector.tensor_copy(oe[:, u, :], ps_d[:, u % 2, :]).then_inc(o_ready, 1)

            schedule(dve, rows_alone, hidden, rows_alone, results)


def moe0(nc, io, X, K, S):
    gate = K["gate"]
    E = io["m0_gate_w"].shape[0]
    with ExitStack() as outer:
        o = Room(nc, outer, "m0")
        mean = o.sb("mean", [P, NT])
        rstd = o.sb("rstd", [P, NT])
        row_stats(nc, X, "m0_st", 1e-5, False, mean, rstd)
        route(nc, io, X, K, S, "m0r", E, 8, io["m0_gate_w"], mean, rstd, S["table0"], E)
    experts(nc, io, S, "m0e", io["m0_wg"].shape[2], E, S["table0"], io["m0_wg"], io["m0_wu"], io["m0_wd"],
            ACT.Silu, None)
    with ExitStack() as ctx:
        r = Room(nc, ctx, "m0a")
        y = r.sb("y", [P, 8, T])
        loaded = [r.sem(f"loaded{k}") for k in range(8)]
        added = r.sem("added")
        block = r.block()

        @block.sync
        def _(sp):
            for i in range(2 * NT):
                if i >= 8:
                    sp.wait_ge(added, i - 7)
                sp.dma_start(y[:, i % 8, :], S[f"y{i % 2}"][i // 2 * P:i // 2 * P + P]).then_inc(loaded[i % 8], 16)

        @block.vector
        def _(dve):
            for i in range(2 * NT):
                dve.wait_ge(loaded[i % 8], 16 * (i // 8) + 16)
                if i % 2:
                    dve.wait_ge(added, i)
                nc.vector.scalar_tensor_tensor(out=X[:, i // 2, :], in0=y[:, i % 8, :], scalar=gate[:, 2:3],
                                               in1=X[:, i // 2, :], op0=ALU.mult, op1=ALU.add).then_inc(added, 1)
            dve.wait_ge(added, 2 * NT)



DH = T // NH
HB = P // DH
SW = C + P
HW = DH + 1
MASKED = -1.0e30
LN_EPS = 1e-6


def mlstm(nc, io, X, K, S):
    ident, gate = K["ident"], K["gate"]
    with ExitStack() as outer:
        o = Room(nc, outer, "ml")
        mean = o.sb("mean", [P, NT])
        rstd = o.sb("rstd", [P, NT])
        row_stats(nc, X, "ml_st", 1e-5, False, mean, rstd)
        with ExitStack() as ctx:
            r = Room(nc, ctx, "mx")
            wq = r.sb("wq", [P, HC, 64])
            wkv = r.sb("wkv", [P, HC, 64])
            wraw = r.sb("wraw", [P, 2, HC, 64])
            bcol = r.sb("bcol", [64, 1])
            lnb = r.sb("lnb", [P, T])
            ones = r.sb("ones", [NH, C])
            xn = r.sb("xn", [P, CT, T])
            cx = r.sb("cx", [P, 2, CT, T])
            qT = r.sb("qT", [P, 2, HC, C])
            cT = r.sb("cT", [P, 2, HC, C])
            va = r.sb("va", [P, 2, CT, NH * HW])
            g = r.sb("g", [NH, 2, C])
            ga = r.sb("ga", [NH, C])
            gl = r.sb("gl", [NH, C])
            Fc = r.sb("F", [NH, C])
            a = r.sb("a", [NH, C])
            M = r.sb("M", [NH, C])
            mx = r.sb("mx", [NH, C])
            nM = r.sb("nM", [NH, C])
            D0 = r.sb("D0", [P, 2, NH, SW])
            acol = r.sb("acol", [P, 2, 2, CT, NH])
            en = r.sb("en", [P, CT * NH])
            D = r.sb("D", [P, 2, HB, SW])
            Cm = r.sb("C", [P, 2, HB, SW])
            hr = r.sb("hr", [P, CT, NH, HW])
            nrm = r.sb("nrm", [P, CT * NH])
            hv = r.sb("hv", [P, CT * NH, DH])
            sq = r.sb("sq", [P, CT * NH, DH])
            st = r.sb("st", [P, CT * NH])
            rs = r.sb("rs", [P, CT * NH])
            ps_s = r.ps("ps_s", [P, HB, 512])
            ps_h = r.ps("ps_h", [P, CT, 512])
            ps_t = r.ps("ps_t", [P, 512])
            ps_g = r.ps("ps_g", [P, 512])
            made = r.sem("made")
            wload = r.sem("wload")
            summed = r.sem("summed")
            ctx_in = [r.sem(f"ctx_in{u}") for u in range(2)]
            ctx_free = [r.sem(f"ctx_free{u}") for u in range(2)]
            xn_ready = r.sem("xn_ready")
            turned = r.sem("turned")
            copied = r.sem("copied")
            va_ready = r.sem("va_ready")
            gated = r.sem("gated")
            g_ready = r.sem("g_ready")
            abs_ready = r.sem("abs_ready")
            ln_ready = r.sem("ln_ready")
            nM_ready = r.sem("nM_ready")
            nM_stored = r.sem("nM_stored")
            spread = [r.sem(f"spread{u}") for u in range(2)]
            masked = r.sem("masked")
            cols = r.sem("cols")
            cols_ready = r.sem("cols_ready")
            en_ready = r.sem("en_ready")
            scored = r.sem("scored")
            d_ready = r.sem("d_ready")
            c_ready = r.sem("c_ready")
            mixed = r.sem("mixed")
            h_copied = r.sem("h_copied")
            var_ready = r.sem("var_ready")
            root = r.sem("root")
            fin = r.sem("fin")
            done = r.sem("done")
            dv = r.sem("dv")
            df = r.sem("df")
            apart = r.sem("apart")
            av = r.sem("av")
            block = r.block()
            NCH = NH // HB

            def schedule(eng, prep, chunk, finish):
                for k in range(4):
                    prep(0, 0, 0, k)

                def body(n, u, i, more=True):
                    for k in range(NCH):
                        chunk(n, u, i, k)
                        if more:
                            prep(n + 1, 1 - u, i + u, k)
                    finish(n, u, i)
                with eng.Fori(0, B // 2 - 1) as i:
                    body(2 * i, 0, i)
                    body(2 * i + 1, 1, i)
                body(B - 2, 0, B // 2 - 1)
                body(B - 1, 1, B // 2 - 1, False)

            @block.gpsimd
            def _(pool):
                nc.gpsimd.memset(wraw[:], 0.0).then_inc(made, 1)
                nc.gpsimd.memset(wq[:], 0.0).then_inc(made, 1)
                nc.gpsimd.memset(bcol[:], 0.0).then_inc(made, 1)
                nc.gpsimd.memset(ones[:], 1.0).then_inc(made, 1)
                for u in range(2):
                    pool.sem_inc(ctx_free[u], 1)
                pool.sem_inc(c_ready, 8)
                pool.sem_inc(mixed, 8)
                pool.sem_inc(h_copied, 1)

                def prep(n, u, i, k):
                    if k == 3:
                        pool.wait_ge(spread[u], 32 * i + 32)
                        pool.sem_inc(apart, 1)
                        for lo in (0, C):
                            v = D0[:, u, :, lo:lo + P]
                            last = nc.gpsimd.affine_select(out=v, in_=v, compare_op=ALU.is_ge, fill=MASKED, base=0,
                                                           pattern=[[0, NH], [1, P]], channel_multiplier=-1)
                        last.then_inc(masked, 1)

                schedule(pool, prep, lambda *_: None, lambda *_: None)

            @block.sync
            def _(sp):
                sp.wait_ge(made, 4)
                for half, (w, b) in enumerate((("l1_Wi", "l1_bi"), ("l1_Wf", "l1_bf"))):
                    v = io[w].rearrange("(k c p) n -> k p c n", k=3, p=P)
                    at = slice(32 * half, 32 * half + NH)
                    sp.dma_start(wq[:, :, at], v[0]).then_inc(wload, 16)
                    for k in range(2):
                        sp.dma_start(wraw[:, k, :, at], v[1 + k]).then_inc(wload, 16)
                    sp.dma_start(bcol[at, :], io[b].rearrange("(n a) -> n a", a=1)).then_inc(wload, 16)
                sp.dma_start(lnb[:], row_of(io["l1_ln_scale"])).then_inc(wload, 16)
                vc = io["ctx"].rearrange("b (c p) t -> b p c t", p=P)

                def load(n, u, i):
                    sp.wait_ge(ctx_free[u], i + 1)
                    sp.dma_start(cx[:, u, :, :], vc[n]).then_inc(ctx_in[u], 16)

                def prep(n, u, i, k):
                    if k == 0:
                        load(n, u, i)
                    if k == 3:
                        sp.wait_ge(nM_ready, n + 1)
                        sp.dma_start(S["nm"], nM[:]).then_inc(nM_stored, 16)
                        sp.wait_ge(nM_stored, 16 * n + 16)
                        sp.dma_start(D0[:, u, :, 0:C], S["nm1"].broadcast_to([P, NH * C])
                                     .rearrange("p (h s) -> p h s", h=NH)).then_inc(spread[u], 16)
                        sp.dma_start(D0[:, u, :, C:SW], S["nm1"].broadcast_to([P, NH * C])
                                     .rearrange("p (h s) -> p h s", h=NH)[:, :, P:C]).then_inc(spread[u], 16)

                schedule(sp, prep, lambda *_: None, lambda *_: None)

            @block.tensor
            def _(pe):
                def prep(n, u, i, k):
                    if k < 2:
                        if k == 0:
                            pe.wait_ge(xn_ready, n + 1)
                        else:
                            pe.wait_ge(ctx_in[u], 16 * i + 16)
                        for ct in range(CT):
                            m = 2 * k + ct
                            if not (isinstance(n, int) and n == 0 and m == 0):
                                pe.wait_ge(copied, 4 * n + m)
                            src = xn[:, ct, :] if k == 0 else cx[:, u, ct, :]
                            for c in range(HC):
                                last = nc.tensor.transpose(ps_t[:, c * P:c * P + P], src[:, c * P:c * P + P], ident[:])
                            last.then_inc(turned, 1)
                    if k == 2:
                        pe.wait_ge(summed, 1)
                        pe.wait_ge(copied, 4 * n + 4)
                        for c in range(HC):
                            nc.tensor.matmul(ps_g[0:64, 0:C], wq[:, c, :], qT[:, u, c, :], start=(c == 0), stop=False)
                        for c in range(HC):
                            last = nc.tensor.matmul(ps_g[0:64, 0:C], wkv[:, c, :], cT[:, u, c, :],
                                                    start=False, stop=(c == HC - 1))
                        last.then_inc(gated, 1)
                    if k == 3:
                        pe.wait_ge(nM_ready, n + 1)
                        pe.sem_inc(apart, 1)
                        for j, src in enumerate((a, mx)):
                            for ct in range(CT):
                                last = nc.tensor.transpose(ps_g[:, (j * CT + ct) * NH:(j * CT + ct + 1) * NH],
                                                           src[:, ct * P:ct * P + P], ident[0:NH, 0:NH])
                        last.then_inc(cols, 1)

                def chunk(n, u, i, k):
                    for j in range(HB):
                        pe.wait_ge(c_ready, NH * n + HB * k + j + 5)
                        row = slice(DH * j, DH * j + DH)
                        nc.tensor.matmul(ps_s[:, j, 0:C], cT[row, u, k, 0:P], qT[row, u, k, :], start=True, stop=True)
                    for j in range(HB):
                        row = slice(DH * j, DH * j + DH)
                        nc.tensor.matmul(ps_s[:, j, C:SW], cT[row, u, k, P:C], qT[row, u, k, P:C],
                                         start=True, stop=True).then_inc(scored, 1)
                    pe.wait_ge(va_ready, n + 1)
                    if k % 2 == 0:
                        pe.wait_ge(h_copied, 2 * n + k // 2 + 1)
                    for j in range(HB):
                        h = HB * k + j
                        pe.wait_ge(c_ready, NH * n + h + 9)
                        at = slice((h % 8) * HW, (h % 8) * HW + HW)
                        v = [va[:, u, ct, h * HW:h * HW + HW] for ct in range(CT)]
                        c = Cm[:, k % 2, j, :]
                        nc.tensor.matmul(ps_h[:, 0, at], c[:, 0:P], v[0], start=True, stop=True)
                        nc.tensor.matmul(ps_h[:, 1, at], c[:, P:C], v[0], start=True, stop=False)
                        nc.tensor.matmul(ps_h[:, 1, at], c[:, C:SW], v[1], start=False, stop=True).then_inc(mixed, 1)

                schedule(pe, prep, chunk, lambda *_: None)

            @block.scalar
            def _(act):
                def prep(n, u, i, k):
                    if k < 2:
                        for ct in range(CT):
                            act.wait_ge(turned, 4 * n + 2 * k + ct + 1)
                            dst = (qT, cT)[k][:, u, :, ct * P:ct * P + P]
                            nc.scalar.activation(dst, ps_t[:].rearrange("p (c n) -> p c n", c=HC), ACT.Copy)\
                              .then_inc(copied, 1)
                    if k == 2:
                        act.wait_ge(gated, n + 1)
                        act.wait_ge(wload, 16 * 9)
                        nc.scalar.activation(g[:, 0, :], ps_g[0:NH, 0:C], ACT.Identity, bias=bcol[0:NH, :]).then_inc(g_ready, 1)
                        nc.scalar.activation(g[:, 1, :], ps_g[32:32 + NH, 0:C], ACT.Identity, bias=bcol[32:32 + NH, :])\
                          .then_inc(g_ready, 1)
                        act.wait_ge(abs_ready, n + 1)
                        nc.scalar.activation(gl[:], ga[:], ACT.Exp, scale=-1.0).then_inc(av, 1)
                        act.wait_ge(av, n + 1)
                        nc.scalar.activation(gl[:], gl[:], ACT.Ln, bias=1.0).then_inc(ln_ready, 1)

                def chunk(n, u, i, k):
                    if k == 0:
                        act.wait_ge(cols_ready, n + 1)
                        act.wait_ge(masked, n + 1)
                    for j in range(HB):
                        h = HB * k + j
                        act.wait_ge(c_ready, NH * n + h + 1)
                        nc.scalar.activation(D[:, k % 2, j, 0:C], D0[:, u, h, 0:C], ACT.Exp,
                                             bias=acol[:, u, 0, 0, h:h + 1])
                        nc.scalar.activation(D[:, k % 2, j, C:SW], D0[:, u, h, C:SW], ACT.Exp,
                                             bias=acol[:, u, 0, 1, h:h + 1]).then_inc(d_ready, 1)
                    if k == NCH - 1:
                        nc.scalar.activation(en[:], acol[:, u, 1, :, :].rearrange("p c h -> p (c h)"), ACT.Exp,
                                             scale=-1.0).then_inc(en_ready, 1)

                def finish(n, u, i):
                    act.wait_ge(var_ready, n + 1)
                    nc.scalar.activation(rs[:], st[:], ACT.Sqrt).then_inc(root, 1)

                schedule(act, prep, chunk, finish)

            STEPS_G, STEPS_F = 7, 12

            @block.vector
            def _(dve):
                dve.wait_ge(made, 4)
                dve.wait_ge(wload, 16 * 9)
                nc.vector.tensor_tensor(wkv[:], wraw[:, 0], wraw[:, 1], ALU.add).then_inc(summed, 1)
                setup = Chain(dve, dv)
                setup(nc.vector.memset(va[:], 1.0))

                def prep(n, u, i, k):
                    if k == 0:
                        for ct in range(CT):
                            tile = CT * n + ct
                            ins = nc.vector.tensor_scalar(xn[:, ct, :],
                                                          X[:, bass.ds(tile, 1), :].rearrange("p a t -> p (a t)"),
                                                          mean[:, bass.ds(tile, 1)], rstd[:, bass.ds(tile, 1)],
                                                          ALU.subtract, ALU.mult)
                        ins.then_inc(xn_ready, 1)
                    if k == 1:
                        dve.wait_ge(ctx_in[u], 16 * i + 16)
                        nc.vector.tensor_copy(va[:, u, :, :].rearrange("p c (h w) -> p c h w", w=HW)[:, :, :, 0:DH],
                                              cx[:, u, :, :].rearrange("p c (h d) -> p c h d", d=DH)).then_inc(va_ready, 1)
                        dve.wait_ge(va_ready, n + 1)
                        dve.wait_ge(turned, 4 * n + 4)
                        dve.sem_inc(ctx_free[u], 1)
                    if k == 2:
                        c = Chain(dve, dv, 1 + STEPS_G * n)
                        dve.wait_ge(g_ready, 2 * n + 2)
                        nc.vector.scalar_tensor_tensor(out=ga[:], in0=g[:, 1, :], scalar=-1.0, in1=g[:, 1, :],
                                                       op0=ALU.mult, op1=ALU.max).then_inc(abs_ready, 1)
                        c(nc.vector.tensor_scalar(Fc[:], g[:, 1, :], 0.0, None, ALU.min))
                        dve.wait_ge(ln_ready, n + 1)
                        c(nc.vector.tensor_tensor(gl[:], Fc[:], gl[:], ALU.subtract))
                        c(nc.vector.tensor_tensor_scan(Fc[:], ones[:], gl[:], 0.0, ALU.mult, ALU.add))
                        if not (isinstance(n, int) and n == 0):
                            dve.wait_ge(cols, n)
                        c(nc.vector.tensor_tensor(a[:], g[:, 0, :], Fc[:], ALU.subtract))
                        c(nc.vector.tensor_tensor_scan(M[:], ones[:], a[:], -3.0e38, ALU.mult, ALU.max))
                        c(nc.vector.tensor_tensor(mx[:], Fc[:], M[:], ALU.add))
                        c(nc.vector.tensor_scalar(nM[:], M[:], -1.0, None, ALU.mult))
                        assert c.n == STEPS_G
                        dve.sem_inc(nM_ready, 1)
                    if k == 3:
                        dve.wait_ge(cols, n + 1)
                        nc.vector.tensor_copy(acol[:, u, :, :, :].rearrange("p j c h -> p (j c h)"),
                                              ps_g[:, 0:2 * CT * NH]).then_inc(cols_ready, 1)

                def chunk(n, u, i, k):
                    for j in range(HB):
                        h = HB * k + j
                        dve.wait_ge(scored, NH * n + h + 1)
                        dve.wait_ge(d_ready, NH * n + h + 1)
                        dve.wait_ge(mixed, NH * n + h + 1)
                        nc.vector.scalar_tensor_tensor(out=Cm[:, k % 2, j, :], in0=ps_s[:, j, 0:SW], scalar=DH ** -0.5,
                                                       in1=D[:, k % 2, j, :], op0=ALU.mult, op1=ALU.mult)\
                          .then_inc(c_ready, 1)
                    if k % 2 == 1:
                        dve.wait_ge(mixed, NH * n + HB * k + HB + 8)
                        half = (k // 2) * 8
                        nc.vector.tensor_copy(hr[:, :, half:half + 8, :].rearrange("p c h w -> p c (h w)"),
                                              ps_h[:, :, 0:8 * HW]).then_inc(h_copied, 1)

                def finish(n, u, i):
                    c = Chain(dve, df, STEPS_F * n)
                    hh = hr[:].rearrange("p c h w -> p (c h) w")
                    wide = [P, CT * NH, DH]
                    dve.wait_ge(h_copied, 2 * n + 3)
                    dve.wait_ge(en_ready, n + 1)
                    c(nc.vector.scalar_tensor_tensor(out=nrm[:], in0=hh[:, :, DH], scalar=-1.0, in1=hh[:, :, DH],
                                                     op0=ALU.mult, op1=ALU.max))
                    c(nc.vector.tensor_tensor(nrm[:], nrm[:], en[:], ALU.max))
                    c(nc.vector.tensor_scalar(nrm[:], nrm[:], LN_EPS, None, ALU.add))
                    c(nc.vector.reciprocal(nrm[:], nrm[:]))
                    c(nc.vector.tensor_tensor(hv[:], hh[:, :, 0:DH], nrm[:].unsqueeze(2).broadcast_to(wide), ALU.mult))
                    c(nc.vector.tensor_reduce(st[:], hv[:], AX.X, ALU.add))
                    c(nc.vector.tensor_scalar(st[:], st[:], 1.0 / DH, None, ALU.mult))
                    c(nc.vector.tensor_tensor(hv[:], hv[:], st[:].unsqueeze(2).broadcast_to(wide), ALU.subtract))
                    c(nc.vector.tensor_tensor(sq[:], hv[:], hv[:], ALU.mult))
                    c(nc.vector.tensor_reduce(st[:], sq[:], AX.X, ALU.add))
                    c(nc.vector.tensor_scalar(st[:], st[:], 1.0 / DH, LN_EPS, ALU.mult, ALU.add))
                    dve.sem_inc(var_ready, 1)
                    dve.wait_ge(root, n + 1)
                    c(nc.vector.reciprocal(rs[:], rs[:]))
                    assert c.n == STEPS_F
                    nc.vector.tensor_tensor(hv[:], hv[:], rs[:].unsqueeze(2).broadcast_to(wide), ALU.mult)\
                      .then_inc(fin, 1)
                    dve.wait_ge(fin, 2 * n + 1)
                    h2 = hv[:].rearrange("p (c h) d -> p c (h d)", c=CT)
                    nc.vector.scalar_tensor_tensor(out=h2, in0=h2, scalar=gate[:, 1:2],
                                                   in1=lnb[:].unsqueeze(1).broadcast_to([P, CT, T]),
                                                   op0=ALU.mult, op1=ALU.mult).then_inc(fin, 1)
                    dve.wait_ge(fin, 2 * n + 2)
                    x = X[:, bass.ds(CT * n, CT), :]
                    nc.vector.tensor_tensor(x, x, h2, ALU.add).then_inc(done, 1)

                schedule(dve, prep, chunk, finish)
                dve.wait_ge(done, B)




def dense_ffn(nc, io, S, dT):
    I = io["f1_w_gate"].shape[1]
    IC = I // P
    TG = 512
    TT = TG // P
    with ExitStack() as ctx:
        r = Room(nc, ctx, "dn")
        w = r.sb("w", [P, 2, HC, I])
        wd = r.sb("wd", [P, IC, T])
        g = r.sb("g", [P, 2, TG])
        h = r.sb("h", [P, 2, TG])
        out = r.sb("out", [P, 2, T])
        ps_g = r.ps("ps_g", [P, 2, 512])
        ps_u = r.ps("ps_u", [P, 2, 512])
        ps_o = r.ps("ps_o", [P, TT, 512])
        w_in = [r.sem(f"w_in{k}") for k in range(4)]
        d_in = r.sem("d_in")
        up = r.sem("up")
        acted = r.sem("acted")
        h_ready = r.sem("h_ready")
        down = r.sem("down")
        copied = [r.sem("copied_a"), r.sem("copied_d")]
        stored = [r.sem("stored_a"), r.sem("stored_d")]
        credit = r.sem("credit")
        block = r.block()
        NG4 = NTOK // TG

        @block.sync
        def _(sp):
            for k in range(4):
                cols = slice(k * I // 4, (k + 1) * I // 4)
                for j, name in enumerate(("f1_w_gate", "f1_w_up")):
                    sp.dma_start(w[:, j, :, cols], io[name].rearrange("(p c) i -> p c i", c=HC)[:, :, cols])\
                      .then_inc(w_in[k], 16)
            sp.dma_start(wd[:], io["f1_w_down"].rearrange("(c p) n -> p c n", p=P)).then_inc(d_in, 16)
            for k in range(2):
                sp.sem_inc(copied[k], 1)
                sp.sem_inc(stored[k], 16)
            with sp.Fori(0, NG4) as q:
                for t in range(TT):
                    k = t % 2
                    sp.wait_ge(copied[k], 2 * q + t // 2 + 2)
                    sp.dma_start(S["dn"][bass.ds(TT * q + t, 1)].rearrange("a p t -> p (a t)"), out[:, k, :])\
                      .then_inc(stored[k], 16)
            for k in range(2):
                sp.wait_ge(stored[k], 32 * NG4 + 16)

        @block.tensor
        def _(pe):
            def group(q, first):
                for ic in range(IC + 1):
                    if ic < IC:
                        if first and ic % (IC // 4) == 0:
                            pe.wait_ge(w_in[ic * 4 // IC], 32)
                        if not first or ic >= 2:
                            pe.wait_ge(h_ready, IC * q + ic - 1)
                        for ps, j in ((ps_g, 0), (ps_u, 1)):
                            for c in range(HC):
                                last = nc.tensor.matmul(ps[:, ic % 2, :], w[:, j, c, ic * P:ic * P + P],
                                                        dT[:, c, bass.ds(TG * q, TG)],
                                                        start=(c == 0), stop=(c == HC - 1))
                        last.then_inc(up, 1)
                    if ic > 0:
                        if first and ic == 1:
                            pe.wait_ge(d_in, 16)
                        if ic == 1:
                            for k in range(2):
                                pe.wait_ge(copied[k], 2 * q + 1)
                        pe.wait_ge(h_ready, IC * q + ic)
                        for t in range(TT):
                            last = nc.tensor.matmul(ps_o[:, t, :], h[:, (ic - 1) % 2, t * P:t * P + P], wd[:, ic - 1, :],
                                                    start=(ic == 1), stop=(ic == IC))
                        last.then_inc(down, 1)

            group(0, True)
            with pe.Fori(1, NG4) as q:
                group(q, False)

        @block.scalar
        def _(act):
            with act.Fori(0, NG4) as q:
                for ic in range(IC):
                    act.wait_ge(up, IC * q + ic + 1)
                    nc.scalar.activation(g[:, ic % 2, :], ps_g[:, ic % 2, :], ACT.Gelu_apprx_tanh).then_inc(acted, 1)
                act.wait_ge(down, IC * q + IC)
                for t in (0, 2):
                    act.wait_ge(stored[0], 32 * q + 8 * t + 16)
                    nc.scalar.activation(out[:, 0, :], ps_o[:, t, :], ACT.Copy).then_inc(copied[0], 1)

        @block.vector
        def _(dve):
            dve.sem_inc(credit, 2)
            with dve.Fori(0, NG4) as q:
                for ic in range(IC):
                    dve.wait_ge(acted, IC * q + ic + 1)
                    dve.wait_ge(credit, IC * q + ic + 1)
                    nc.vector.tensor_tensor(h[:, ic % 2, :], g[:, ic % 2, :], ps_u[:, ic % 2, :], ALU.mult)\
                      .then_inc(h_ready, 1)
                dve.wait_ge(down, IC * q + IC)
                for t in (1, 3):
                    dve.wait_ge(stored[1], 32 * q + 8 * (t - 1) + 16)
                    nc.vector.tensor_copy(out[:, 1, :], ps_o[:, t, :]).then_inc(copied[1], 1)

        @block.gpsimd
        def _(pool):
            with pool.Fori(0, NG4) as q:
                for ic in range(IC):
                    pool.wait_ge(down, IC * q + ic + 1)
                    pool.sem_inc(credit, 1)


def ffn1(nc, io, X, K, S):
    gate = K["gate"]
    E = io["f1_router_w"].shape[1]
    with ExitStack() as outer:
        o = Room(nc, outer, "f1")
        dT = o.sb("dT", [P, HC, NTOK])
        with ExitStack() as inner:
            o2 = Room(nc, inner, "f1s")
            mean = o2.sb("mean", [P, NT])
            rstd = o2.sb("rstd", [P, NT])
            row_stats(nc, X, "f1_st", 1e-5, False, mean, rstd, second=1e-6)
            route(nc, io, X, K, S, "f1r", E, 2, io["f1_router_w"], mean, rstd, S["table1"], BLOCKS1,
                  dense=dT, scale=io["f1_per_expert_scale"], owner=S["owner"])
        dense_ffn(nc, io, S, dT)
    experts(nc, io, S, "f1e", io["f1_we_gate"].shape[2], BLOCKS1, S["table1"], io["f1_we_gate"], io["f1_we_up"],
            io["f1_we_down"], ACT.Gelu_apprx_tanh, io["f1_rn_pre2"], owner=S["owner"])
    with ExitStack() as outer:
        o = Room(nc, outer, "fn")
        d = o.sb("d", [P, NT, T])
        m = o.sb("m", [P, NT, T])
        m1 = o.sb("m1", [P, 4, T])
        post = o.sb("post", [P, 3, T])
        mean = o.sb("mean", [P, NT])
        rd = o.sb("rd", [P, NT])
        rm = o.sb("rm", [P, NT])
        with ExitStack() as ctx:
            r = Room(nc, ctx, "fl")
            loaded = r.sem("loaded")
            m_in = [r.sem(f"m_in{k}") for k in range(4)]
            summed = r.sem("summed")
            block = r.block()

            @block.vector
            def _(dve):
                for i in range(NT):
                    dve.wait_ge(m_in[i % 4], 32 * (i // 4) + 32)
                    nc.vector.tensor_tensor(m[:, i, :], m[:, i, :], m1[:, i % 4, :], ALU.add).then_inc(summed, 1)

            @block.sync
            def _(sp):
                for i in range(NT):
                    if i >= 4:
                        sp.wait_ge(summed, i - 3)
                    sp.dma_start(m[:, i, :], S["y0"][i * P:i * P + P]).then_inc(m_in[i % 4], 16)
                    sp.dma_start(m1[:, i % 4, :], S["y1"][i * P:i * P + P]).then_inc(m_in[i % 4], 16)
                for i in range(NT):
                    sp.dma_start(d[:, i, :], S["dn"][i]).then_inc(loaded, 16)
                for k, w in enumerate(("f1_rn_post1", "f1_rn_post2", "f1_rn_post")):
                    sp.dma_start(post[:, k, :], row_of(io[w])).then_inc(loaded, 16)
                sp.wait_ge(loaded, 16 * (NT + 3))
                sp.wait_ge(summed, NT)

        row_stats(nc, d, "fn_d", 1e-6, True, mean, rd)
        row_stats(nc, m, "fn_m", 1e-6, True, mean, rm)
        with ExitStack() as ctx:
            r = Room(nc, ctx, "fs")
            dv = r.sem("dv")
            block = r.block()

            @block.vector
            def _(dve):
                with dve.Fori(0, NT) as i:
                    c = Chain(dve, dv, 3 * i)
                    dd = d[:, bass.ds(i, 1), :].rearrange("p a t -> p (a t)")
                    mm = m[:, bass.ds(i, 1), :].rearrange("p a t -> p (a t)")
                    c(nc.vector.scalar_tensor_tensor(out=dd, in0=dd, scalar=rd[:, bass.ds(i, 1)], in1=post[:, 0, :],
                                                     op0=ALU.mult, op1=ALU.mult))
                    c(nc.vector.scalar_tensor_tensor(out=mm, in0=mm, scalar=rm[:, bass.ds(i, 1)], in1=post[:, 1, :],
                                                     op0=ALU.mult, op1=ALU.mult))
                    c(nc.vector.tensor_tensor(dd, dd, mm, ALU.add))

        row_stats(nc, d, "fn_s", 1e-6, True, mean, rd)
        with ExitStack() as ctx:
            r = Room(nc, ctx, "fx")
            dv = r.sem("dv")
            block = r.block()

            @block.vector
            def _(dve):
                with dve.Fori(0, NT) as i:
                    c = Chain(dve, dv, 2 * i)
                    dd = d[:, bass.ds(i, 1), :].rearrange("p a t -> p (a t)")
                    xx = X[:, bass.ds(i, 1), :].rearrange("p a t -> p (a t)")
                    c(nc.vector.scalar_tensor_tensor(out=dd, in0=dd, scalar=rd[:, bass.ds(i, 1)], in1=post[:, 2, :],
                                                     op0=ALU.mult, op1=ALU.mult))
                    c(nc.vector.scalar_tensor_tensor(out=xx, in0=dd, scalar=gate[:, 3:4], in1=xx,
                                                     op0=ALU.mult, op1=ALU.add))


BLOCKS1 = (2 * NTOK - 8) // P + 8


def scratch(nc):
    d = {}
    def dram(name, shape, dt=F32):
        d[name] = nc.dram_tensor(f"scr_{name}", shape, dt, kind="Internal").ap()
    dram("qs", [NN, 3, HD, GH, T], BF16)
    dram("ks", [NN, 3, HD, GH, T], BF16)
    dram("mq", [NN, 9, T], BF16)
    dram("mk", [NN, 12, T], BF16)
    dram("mx", [4, 3, GH * HC, P], BF16)
    dram("mrep", [NT, T])
    dram("xg", [NTOK + P, T])
    dram("y0", [NTOK + P, T])
    dram("y1", [NTOK + P, T])
    dram("table0", [P, 64, 2], I32)
    dram("nm", [NH, C])
    d["nm1"] = d["nm"].rearrange("(a h) s -> a (h s)", a=1)
    dram("table1", [P, BLOCKS1, 2], I32)
    dram("owner", [1, BLOCKS1], I32)
    dram("dn", [NT, P, T])
    return d


def program(nc, io, out):
    with ExitStack() as ctx:
        X = ctx.enter_context(nc.sbuf_tensor("residual", [P, NT, T], F32))
        K = {"ident": ctx.enter_context(nc.sbuf_tensor("ident", [P, P], F32)),
             "gate": ctx.enter_context(nc.sbuf_tensor("gate", [P, 4], F32)),
             "g_xattn": io["g_xattn"], "g_ffn": io["g_ffn"]}
        S = scratch(nc)
        load_x(nc, io["x"].rearrange("b (c p) t -> (b c) p t", p=P), X)
        constants(nc, K)
        attention(nc, io, X, K, S)
        moe0(nc, io, X, K, S)
        mlstm(nc, io, X, K, S)
        ffn1(nc, io, X, K, S)
        store_x(nc, out.rearrange("b (c p) t -> (b c) p t", p=P), X)


_NAMES = {
    "x": "x", "ctx": "ctx_2048", "mask": "mask_Bx1x2048_fk1", "g_xattn": "g_xattn", "g_ffn": "g_ffn",
    "Wq": "L0_xattn_Wq", "bq": "L0_xattn_bq", "Wk": "L0_xattn_Wk", "bk": "L0_xattn_bk", "Wv": "L0_xattn_Wv",
    "bv": "L0_xattn_bv", "m0_gate_w": "L0_ffn_gate_w", "m0_wg": "L0_ffn_wg", "m0_wu": "L0_ffn_wu",
    "m0_wd": "L0_ffn_wd", "l1_Wi": "L1_xattn_Wi", "l1_bi": "L1_xattn_bi", "l1_Wf": "L1_xattn_Wf",
    "l1_bf": "L1_xattn_bf", "l1_ln_scale": "L1_xattn_ln_scale", "f1_rn_pre1": "L1_ffn_rn_pre1",
    "f1_rn_pre2": "L1_ffn_rn_pre2", "f1_rn_post1": "L1_ffn_rn_post1", "f1_rn_post2": "L1_ffn_rn_post2",
    "f1_rn_post": "L1_ffn_rn_post", "f1_w_gate": "L1_ffn_w_gate", "f1_w_up": "L1_ffn_w_up",
    "f1_w_down": "L1_ffn_w_down", "f1_router_w": "L1_ffn_router_w", "f1_router_scale": "L1_ffn_router_scale",
    "f1_per_expert_scale": "L1_ffn_per_expert_scale", "f1_we_gate": "L1_ffn_we_gate",
    "f1_we_up": "L1_ffn_we_up", "f1_we_down": "L1_ffn_we_down",
}


def kernel(**inputs):
    import numpy as _np
    import concourse.bacc as _bacc
    from concourse import mybir as _mybir
    from concourse.bass_utils import run_bass_kernel_spmd as _run

    nc = _bacc.Bacc("TRN2", target_bir_lowering=False, num_devices=1)
    arrays, io = {}, {}
    for short, name in _NAMES.items():
        a = _np.ascontiguousarray(inputs[name])
        arrays[f"in_{name}"] = a
        io[short] = nc.dram_tensor(f"in_{name}", a.shape, _mybir.dt.from_np(a.dtype), kind="ExternalInput").ap()
    out = nc.dram_tensor("out_0", (B, C, T), F32, kind="ExternalOutput").ap()
    program(nc, io, out)
    r = _run(nc, [arrays], core_ids=[0])
    return r.results[0]["out_0"]
```

```python
import numpy as np
import concourse.bass as bass
from concourse import mybir
from contextlib import ExitStack

F32 = mybir.dt.float32
BF16 = mybir.dt.bfloat16
I32 = mybir.dt.int32
U32 = mybir.dt.uint32
F32R = mybir.dt.float32r
ALU = mybir.AluOpType
ACT = mybir.ActivationFunctionType
AX = mybir.AxisListType

P = 128
B, C, T = 8, 256, 512
CT = C // P
NT = B * CT
NTOK = B * C
HC = T // P
NH = 16


class Chain:

    def __init__(self, eng, sem, base=0):
        self.eng, self.sem, self.base, self.n = eng, sem, base, 0

    def __call__(self, ins):
        self.n += 1
        ins.then_inc(self.sem, 1)
        self.eng.wait_ge(self.sem, self.base + self.n)


class Room:

    def __init__(self, nc, ctx, tag):
        self.nc, self.ctx, self.tag, self.sems = nc, ctx, tag, []
        ctx.callback(self.clear)

    def clear(self):
        if self.sems:
            self.nc.clear_and_free_semaphores(self.sems)
            self.nc.all_engine_barrier()

    def sb(self, name, shape, dt=F32):
        return self.ctx.enter_context(self.nc.sbuf_tensor(f"{self.tag}_{name}", shape, dt))

    def ps(self, name, shape, dt=F32):
        return self.ctx.enter_context(self.nc.psum_tensor(f"{self.tag}_{name}", shape, dt))

    def sem(self, name):
        self.sems.append(self.nc.alloc_semaphore(f"{self.tag}_{name}"))
        return self.sems[-1]

    def block(self):
        return self.ctx.enter_context(self.nc.Block())


def row_of(vector):
    n = vector.shape[0]
    return vector.rearrange("(a n) -> a n", a=1).broadcast_to([P, n])


def start(nc, x_dram, mask, X, K, S):
    with ExitStack() as ctx:
        r = Room(nc, ctx, "in")
        graw = r.sb("graw", [P, 4])
        loaded = [r.sem(f"loaded{i}") for i in range(NT)]
        filled = r.sem("filled")
        gload = r.sem("gload")
        m = r.sb("m", [B, T])
        a = r.sb("a", [B, T])
        rest = r.sb("rest", [B, T])
        mp = r.sb("mp", [B, 3, T], BF16)
        ap = r.sb("ap", [B, 3, T], BF16)
        one = r.sb("one", [B, 3, T], BF16)
        mload = r.sem("mload")
        dv = r.sem("dv")
        split = r.sem("split")
        stored = r.sem("stored")
        block = r.block()

        @block.sync
        def _(sp):
            sp.dma_start(m[:], mask).then_inc(mload, 16)
            sp.dma_start(graw[:, 0:2], row_of(K["g_xattn"])).then_inc(gload, 16)
            sp.dma_start(graw[:, 2:4], row_of(K["g_ffn"])).then_inc(gload, 16)
            for i in range(NT):
                sp.dma_start(X[:, i, :], x_dram[i]).then_inc(loaded[i], 16)
            sp.wait_ge(split, 1)
            n = 0
            part = {"h": 0, "m": 1, "l": 2}
            for rows, dst, src in ((QROWS, S["mq"], ap), (KROWS, S["mk"], mp)):
                for k, w in enumerate(rows):
                    sp.dma_start(dst[:, k, :], src[:, part[w], :]).then_inc(stored, 16)
                tail = one if dst is S["mq"] else ap
                sp.dma_start(dst[:, 6:9, :], tail[:]).then_inc(stored, 16)
                n += len(rows) + 1
            sp.dma_start(S["mk"][:, 9:12, :], one[:]).then_inc(stored, 16)
            sp.wait_ge(stored, 16 * (n + 1))

        @block.gpsimd
        def _(pool):
            nc.gpsimd.memset(K["ident"][:], 0.0).then_inc(filled, 1)
            pool.wait_ge(filled, 1)
            nc.gpsimd.affine_select(out=K["ident"][:], in_=K["ident"][:], compare_op=ALU.not_equal, fill=1.0,
                                    base=0, pattern=[[-1, P]], channel_multiplier=1).then_inc(filled, 1)

        @block.scalar
        def _(act):
            act.wait_ge(gload, 32)
            nc.scalar.activation(K["gate"][:], graw[:], ACT.Tanh)

        @block.vector
        def _(dve):
            c = Chain(dve, dv)
            nc.vector.memset(one[:], 1.0)
            dve.wait_ge(mload, 16)
            c(nc.vector.tensor_scalar(a[:], m[:], -1.0, NEG, ALU.add, ALU.mult))
            split3(nc.vector, c, [mp[:, j, :] for j in range(3)], rest[:], m[:])
            split3(nc.vector, c, [ap[:, j, :] for j in range(3)], rest[:], a[:])
            dve.sem_inc(split, 1)
            for i in range(NT):
                dve.wait_ge(loaded[i], 16)
                nc.vector.bn_stats(K["bn"][:, i, :], X[:, i, :])


def row_stats(nc, K, tag, eps, mean, rstd, second=None):
    with ExitStack() as ctx:
        r = Room(nc, ctx, tag)
        ag = r.sb("ag", [P, NT, 2])
        v = r.sb("v", [P, NT])
        dv = r.sem("dv")
        root = r.sem("root")
        ready = r.sem("ready")
        block = r.block()

        @block.vector
        def _(dve):
            c = Chain(dve, dv)
            for i in range(NT):
                ins = nc.vector.bn_aggr(ag[:, i, :], K["bn"][:, i, :])
            c(ins)
            if second is not None:
                c(nc.vector.tensor_scalar(v[:], ag[:, :, 1], 1.0 + second, eps * second, ALU.mult, ALU.add))
            else:
                c(nc.vector.tensor_scalar(v[:], ag[:, :, 1], eps, None, ALU.add))
            dve.sem_inc(ready, 1)
            c(nc.vector.tensor_copy(mean[:], ag[:, :, 0]))
            dve.wait_ge(root, 1)
            c(nc.vector.reciprocal(rstd[:], v[:]))

        @block.scalar
        def _(act):
            act.wait_ge(ready, 1)
            nc.scalar.activation(v[:], v[:], ACT.Sqrt).then_inc(root, 1)



HD = 16
GH = 4
NG = NH // GH
NN = B * NG
QROWS = ("h", "h", "m", "h", "l", "m")
KROWS = ("h", "m", "h", "l", "h", "m")
NEG = 1000000.0
MROW = 6 * HD
MAXROW = MROW + 9
NROW = MAXROW + 3
VW = HD + 1


HIGH = -4096


def split3(engine, chain, parts, rest, src):
    chain(engine.tensor_copy(parts[0], src))
    chain(engine.tensor_tensor(rest, src, parts[0], ALU.subtract))
    chain(engine.tensor_copy(parts[1], rest))
    chain(engine.tensor_tensor(parts[2], rest, parts[1], ALU.subtract))


def attention(nc, io, X, K, S):
    with ExitStack() as outer:
        o = Room(nc, outer, "at")
        mean = o.sb("mean", [P, NT])
        rstd = o.sb("rstd", [P, NT])
        V = o.sb("V", [P, NN, HC * GH * VW])
        row_stats(nc, K, "at_st", 1e-5, mean, rstd)

        project(nc, io, X, K, S, mean, rstd, V)
        attend(nc, io, X, K, S, V)


def project(nc, io, X, K, S, mean, rstd, V):
    ident = K["ident"]
    mask8 = io["mask"].rearrange("b a t -> (b a) t")
    with ExitStack() as ctx:
        r = Room(nc, ctx, "pj")
        wraw = r.sb("wraw", [P, 3, CT, C])
        wT = r.sb("wT", [P, 3, CT, C])
        bcol = r.sb("bcol", [P, 2, CT])
        bvb = r.sb("bvb", [P, C])
        smc = r.sb("smc", [P, B * HC])
        tmb = r.sb("tmb", [P, 2, T])
        src = r.sb("src", [P, 2, CT, T])
        xn = r.sb("xn", [P, 2, CT, T])
        full = r.sb("full", [P, CT, 2, T])
        rest = r.sb("rest", [P, 2, T])
        parts = r.sb("parts", [P, CT, 2, 3, T], BF16)
        vt = r.sb("vt", [P, 4, C])
        pt = r.ps("pt", [P, 2, 512])
        pq = r.ps("pq", [P, 2, 512])
        pv = r.ps("pv", [P, 4, 512])
        wload = r.sem("wload")
        bload = r.sem("bload")
        transposed = r.sem("transposed")
        evacuated = r.sem("evacuated")
        in_loaded = [r.sem(f"in_loaded{u}") for u in range(2)]
        normed = r.sem("normed")
        projected = r.sem("projected")
        proj_read = r.sem("proj_read")
        vproj = r.sem("vproj")
        vread = r.sem("vread")
        v_done = r.sem("v_done")
        made = r.sem("made")
        dv = r.sem("dv")
        k_high = r.sem("k_high")
        k_rest = r.sem("k_rest")
        k_middle = r.sem("k_middle")
        full_ready = [r.sem("full_q"), r.sem("full_k")]
        q_split = r.sem("q_split")
        k_split = r.sem("k_split")
        kept = [[r.sem(f"kept_{k}{ct}") for ct in range(CT)] for k in "qk"]
        block = r.block()
        ctx_v = io["ctx"].rearrange("b (c p) t -> b p c t", p=P)

        def past(b, k):
            return not isinstance(b, int) or b >= k

        def batches(eng, batch):
            for b in range(2):
                batch(b, 0, b)
            with eng.Fori(1, B // 2) as g:
                for u in range(2):
                    batch(2 * g + u, g, u)

        @block.sync
        def _(sp):
            for k, w in enumerate(("Wq", "Wk", "Wv")):
                sp.dma_start(wraw[:, k, :, :], io[w].rearrange("(c p) n -> p c n", p=P)).then_inc(wload, 16)

            def load(b, g, u):
                if past(b, 2):
                    sp.wait_ge(proj_read, 4 * b - 4)
                    sp.wait_ge(vproj, HC * b - HC)
                sp.dma_start(src[:, u, :, :], ctx_v[b]).then_inc(in_loaded[u], 16)
                sp.dma_start(tmb[:, u, :], mask8[bass.ds(b, 1)].broadcast_to([P, T])).then_inc(in_loaded[u], 16)
                if isinstance(b, int) and b == 0:
                    for k, w in enumerate(("bq", "bk")):
                        sp.dma_start(bcol[:, k, :], io[w].rearrange("(c p) -> p c", p=P),
                                     allow_slow_non_contiguous=True).then_inc(bload, 16)
                    sp.dma_start(bvb[:], row_of(io["bv"])).then_inc(bload, 16)
                    sp.dma_start(smc[:], io["mask"].rearrange("b a (c p) -> p (b a c)", p=P),
                                 allow_slow_non_contiguous=True).then_inc(bload, 16)

            batches(sp, load)

        @block.scalar
        def _(act):
            def batch(b, g, u):
                for ct in range(CT):
                    n = CT * b + ct
                    p = [parts[:, ct, 1, j, :] for j in range(3)]
                    act.wait_ge(full_ready[1], n + 1)
                    if past(b, 1):
                        act.wait_ge(kept[1][ct], 16 * b)
                    nc.scalar.activation(p[0], full[:, ct, 1, :], ACT.Copy).then_inc(k_high, 1)
                    act.wait_ge(k_rest, n + 1)
                    nc.scalar.activation(p[1], rest[:, 1, :], ACT.Copy).then_inc(k_middle, 1)
                    for k, name, done in ((0, "qs", q_split), (1, "ks", k_split)):
                        act.wait_ge(done, n + 1)
                        act.dma_start(S[name][n].rearrange("j p t -> p j t"), parts[:, ct, k, :, :])\
                           .then_inc(kept[k][ct], 16)

            batches(act, batch)
            for k in range(2):
                for ct in range(CT):
                    act.wait_ge(kept[k][ct], 16 * B)

        @block.tensor
        def _(pe):
            pe.wait_ge(wload, 16 * 3)
            n = 0
            for k in range(3):
                for co in range(CT):
                    if n >= 2:
                        pe.wait_ge(evacuated, n - 1)
                    for ci in range(CT):
                        last = nc.tensor.transpose(pt[:, n % 2, ci * P:ci * P + P],
                                                   wraw[:, k, co, ci * P:ci * P + P], ident[:])
                    last.then_inc(transposed, 1)
                    n += 1
            pe.wait_ge(evacuated, n)

            def batch(b, g, u):
                pe.wait_ge(in_loaded[u], 32 * g + 32)
                pe.wait_ge(normed, b + 1)
                for ct in range(CT):
                    for k, rhs in enumerate((xn, src)):
                        j = 2 * ct + k
                        if past(b, 1) or j >= 2:
                            pe.wait_ge(proj_read, 4 * b + j - 1)
                        for c in range(CT):
                            last = nc.tensor.matmul(pq[:, k, :], wT[:, k, c, ct * P:ct * P + P],
                                                    rhs[:, u, c, :], start=(c == 0), stop=(c == CT - 1))
                        last.then_inc(projected, 1)
                    for s in (2 * ct, 2 * ct + 1):
                        if past(b, 1):
                            pe.wait_ge(vread, HC * b + s - 3)
                        for c in range(CT):
                            last = nc.tensor.matmul(pv[:, s, 0:C], src[:, u, c, s * P:s * P + P],
                                                    wT[:, 2, c, :], start=(c == 0), stop=(c == CT - 1))
                        last.then_inc(vproj, 1)

            batches(pe, batch)

        @block.gpsimd
        def _(pool):
            nc.gpsimd.memset(V[:], 1.0).then_inc(made, 1)

            def batch(b, g, u):
                for ct in range(CT):
                    n = CT * b + ct
                    pool.wait_ge(k_high, n + 1)
                    if past(b, 1) or ct >= 1:
                        pool.wait_ge(k_split, n)
                    nc.gpsimd.tensor_tensor(rest[:, 1, :], full[:, ct, 1, :], parts[:, ct, 1, 0, :], ALU.subtract)\
                        .then_inc(k_rest, 1)
                    pool.wait_ge(k_middle, n + 1)
                    nc.gpsimd.tensor_tensor(parts[:, ct, 1, 2, :], rest[:, 1, :], parts[:, ct, 1, 1, :], ALU.subtract)\
                        .then_inc(k_split, 1)

            batches(pool, batch)

        @block.vector
        def _(dve):
            n = 0
            for k in range(3):
                for co in range(CT):
                    dve.wait_ge(transposed, n + 1)
                    nc.vector.tensor_scalar(wT[:, k, :, co * P:co * P + P],
                                            pt[:, n % 2, 0:CT * P].rearrange("p (c n) -> p c n", c=CT),
                                            HD ** -0.5 if k == 0 else 1.0, None, ALU.mult).then_inc(evacuated, 1)
                    n += 1
            dve.wait_ge(bload, 16 * 4)
            first = Chain(dve, dv)
            first(nc.vector.tensor_scalar(bcol[:, 0, :], bcol[:, 0, :], HD ** -0.5, None, ALU.mult))
            dve.wait_ge(made, 1)

            def norm(b, g, u):
                if past(b, 2):
                    dve.wait_ge(proj_read, 4 * b - 4)
                for ct in range(CT):
                    ins = nc.vector.tensor_scalar(xn[:, u, ct, :],
                                                  X[:, bass.ds(CT * b + ct, 1), :].rearrange("p a t -> p (a t)"),
                                                  mean[:, bass.ds(CT * b + ct, 1)], rstd[:, bass.ds(CT * b + ct, 1)],
                                                  ALU.subtract, ALU.mult)
                ins.then_inc(normed, 1)

            def batch(b, g, u):
                if isinstance(b, int) and b == 0:
                    norm(0, 0, 0)
                dve.wait_ge(in_loaded[u], 32 * g + 32)
                for ct in range(CT):
                    for k in range(2):
                        j = 2 * ct + k
                        dve.wait_ge(projected, 4 * b + j + 1)
                        if past(b, 1):
                            dve.wait_ge((q_split, k_split)[k], CT * (b - 1) + ct + 1)
                        nc.vector.scalar_tensor_tensor(out=full[:, ct, k, :], in0=pq[:, k, :],
                                                       scalar=bcol[:, k, ct:ct + 1], in1=tmb[:, u, :],
                                                       op0=ALU.add, op1=ALU.mult).then_inc(proj_read, 1)
                        dve.wait_ge(proj_read, 4 * b + j + 1)
                        dve.sem_inc(full_ready[k], 1)
                    if past(b, 1):
                        dve.wait_ge(kept[0][ct], 16 * b)
                    f, p = full[:, ct, 0, :], [parts[:, ct, 0, j, :] for j in range(3)]
                    q = Chain(dve, dv, 1 + 4 * (CT * b + ct))
                    a, z = 2 * ct, 2 * ct + 1

                    def add_bias(s):
                        dve.wait_ge(vproj, HC * b + s + 1)
                        nc.vector.tensor_tensor(vt[:, s, :], pv[:, s, 0:C], bvb[:], ALU.add).then_inc(vread, 1)

                    def times_mask(s):
                        dve.wait_ge(vread, HC * b + s + 1)
                        dst = V[:, bass.ds(NG * b, NG), s * GH * VW:(s + 1) * GH * VW]\
                            .rearrange("p g (h w) -> p g h w", h=GH)[:, :, :, 0:HD]
                        nc.vector.tensor_scalar(dst, vt[:, s, :].rearrange("p (g h w) -> p g h w", g=NG, h=GH),
                                                smc[:, bass.ds(HC * b + s, 1)], None, ALU.mult).then_inc(v_done, 1)

                    def start(ins):
                        ins.then_inc(dv, 1)
                        q.n += 1

                    def ended():
                        dve.wait_ge(dv, q.base + q.n)

                    start(nc.vector.tensor_copy(p[0], f))
                    add_bias(a)
                    ended()
                    start(nc.vector.tensor_tensor(rest[:, 0, :], f, p[0], ALU.subtract))
                    add_bias(z)
                    ended()
                    start(nc.vector.tensor_copy(p[1], rest[:, 0, :]))
                    times_mask(a)
                    ended()
                    start(nc.vector.tensor_tensor(p[2], rest[:, 0, :], p[1], ALU.subtract))
                    times_mask(z)
                    ended()
                    dve.sem_inc(q_split, 1)
                    if ct == 0 and not (isinstance(b, int) and b == B - 1):
                        norm(b + 1, g + u, 1 - u)

            for b in range(2):
                batch(b, 0, b)
            with dve.Fori(1, B // 2 - 1) as g:
                for u in range(2):
                    batch(2 * g + u, g, u)
            for b in range(B - 2, B):
                batch(b, b // 2, b % 2)


def attend(nc, io, X, K, S, V):
    ident, gate = K["ident"], K["gate"]
    mask8 = io["mask"].rearrange("b a t -> (b a) t")
    RING = 4
    NI = NN // 2
    with ExitStack() as ctx:
        r = Room(nc, ctx, "sm")
        Q = r.sb("Q", [P, RING, GH, T], BF16)
        Kk = r.sb("K", [P, RING, GH, T], BF16)
        negm = r.sb("negm", [P, 2, GH * HC])
        mrow = r.sb("mrow", [GH * HC, 2, P])
        mrest = r.sb("mrest", [GH * HC, P])
        mparts = r.sb("mparts", [GH * HC, 2, 3, P], BF16)
        Pe = r.sb("P", [P, 4, 2, T])
        Vg = r.sb("Vg", [P, 2, HC, GH, 32])
        O = r.sb("O", [P, 4, T])
        rden = r.sb("rden", [P, T])
        tmb = r.sb("tmb", [P, 2, T])
        res = r.sb("res", [P, 2, T])
        dsel = r.sb("dsel", [P, 2, P])
        sel = r.sb("sel", [P, 2, P])
        ps_m = r.ps("ps_m", [P, 2, 512])
        ps_s = r.ps("ps_s", [P, 2, 2, 512])
        ps_o = r.ps("ps_o", [P, 512])
        ps_x = r.ps("ps_x", [P, 512])
        made = r.sem("made")
        stacked = [r.sem(f"stacked{u}") for u in range(RING)]
        m_scored = r.sem("m_scored")
        m_read = r.sem("m_read")
        m_turned = r.sem("m_turned")
        m_copied = r.sem("m_copied")
        cut = r.sem("cut")
        m_split = r.sem("m_split")
        m_stored = r.sem("m_stored")
        m_rows = [r.sem(f"m_rows{u}") for u in range(RING)]
        scored = r.sem("scored")
        exped = r.sem("exped")
        v_ready = r.sem("v_ready")
        valued = r.sem("valued")
        o_copied = r.sem("o_copied")
        den_out = r.sem("den_out")
        reciped = r.sem("reciped")
        picked = r.sem("picked")
        num_read = r.sem("num_read")
        tm_loaded = [r.sem(f"tm_loaded{u}") for u in range(2)]
        masked = r.sem("masked")
        finished = r.sem("finished")
        apart = r.sem("apart")
        block = r.block()

        def steps(eng, step):
            for j in range(2 * RING):
                step(j, j // RING, j % RING)
            with eng.Fori(2, NN // RING) as g:
                for u in range(RING):
                    step(RING * g + u, g, u)
            for j in range(NN, NN + 4):
                step(j, j // RING, j % RING)

        def within(n, lo, hi):
            return not isinstance(n, int) or lo <= n < hi

        @block.gpsimd
        def _(pool):
            nc.gpsimd.memset(dsel[:], 0.0).then_inc(made, 1)
            nc.gpsimd.memset(sel[:], 0.0).then_inc(made, 1)
            nc.gpsimd.memset(Vg[:], 0.0).then_inc(made, 1)
            pool.wait_ge(made, 3)
            for q in range(2):
                v = dsel[:, q, 64 * q:64 * q + 64].rearrange("p (j d) -> p j d", j=GH)
                nc.gpsimd.affine_select(out=v, in_=v, compare_op=ALU.not_equal, fill=1.0, base=-HD,
                                        pattern=[[-32, GH], [0, HD]], channel_multiplier=1).then_inc(made, 1)
                v = sel[:, q, 64 * q:64 * q + 64].rearrange("p (j d) -> p j d", j=GH)
                nc.gpsimd.affine_select(out=v, in_=v, compare_op=ALU.not_equal, fill=1.0, base=0,
                                        pattern=[[-32, GH], [-1, HD]], channel_multiplier=1).then_inc(made, 1)
            pool.wait_ge(made, 7)

            def step(j, g, u):
                q = j - 1
                if within(q, 0, NN):
                    pool.wait_ge(m_copied, q + 1)
                    c = Chain(pool, cut, 4 * q)
                    w = (u - 1) % RING
                    m, mp = mrow[:, w % 2, :], [mparts[:, w % 2, k, :] for k in range(3)]
                    pool.sem_inc(apart, 1)
                    c(nc.gpsimd.tensor_copy(mp[0], m))
                    c(nc.gpsimd.tensor_tensor(mrest[:], m, mp[0], ALU.subtract))
                    pool.sem_inc(apart, 1)
                    c(nc.gpsimd.tensor_copy(mp[1], mrest[:]))
                    c(nc.gpsimd.tensor_tensor(mp[2], mrest[:], mp[1], ALU.subtract))
                    pool.sem_inc(m_split, 1)
                    turn = g + (u - 1) // RING
                    if within(q, RING, NN):
                        pool.wait_ge(m_rows[w], 16 * turn)
                    pool.sem_inc(apart, 1)
                    pool.dma_start(S["mx"][w].rearrange("j k p -> k j p"), mparts[:, w % 2, :, :])\
                        .then_inc(m_stored, 16)
                    pool.wait_ge(m_stored, 16 * q + 16)
                    pool.sem_inc(apart, 1)
                    pool.dma_start(Q[MAXROW:NROW, w, :, :].rearrange("p h t -> p (h t)"),
                                   S["mx"][w].rearrange("j k p -> j (k p)")).then_inc(m_rows[w], 16)
                    if within(q, 2, NN):
                        pool.wait_ge(valued, 8 * q - 8)
                    pool.sem_inc(apart, 1)
                    nc.gpsimd.tensor_copy(Vg[:, w % 2, :, :, 0:VW],
                                          V[:, bass.ds(q, 1), :].rearrange("p a (s h w) -> p (a s) h w", s=HC, h=GH))\
                      .then_inc(v_ready, 1)
                if u % 2 == 1 and within(j, 5, NN + 4):
                    i, b = 2 * g + u // 2 - 2, (u // 2) % 2
                    pool.wait_ge(num_read, i + 1)
                    pool.wait_ge(tm_loaded[b], 16 * g)
                    nc.gpsimd.tensor_tensor(res[:, b, :], res[:, b, :], tmb[:, b, :], ALU.mult).then_inc(masked, 1)
                    pool.wait_ge(masked, i + 1)
                    x = X[:, bass.ds(i, 1), :].rearrange("p a t -> p (a t)")
                    nc.gpsimd.tensor_tensor(x, x, res[:, b, :], ALU.add).then_inc(finished, 1)

            steps(pool, step)
            pool.wait_ge(finished, NI)

        @block.sync
        def _(sp):
            def load(q, w, tile, b):
                half = slice(w % 2 * GH * HD, (w % 2 + 1) * GH * HD)
                for k in range(6):
                    for dst, name, rows in ((Q, "qs", QROWS), (Kk, "ks", KROWS)):
                        part = {"h": 0, "m": 1, "l": 2}[rows[k]]
                        sp.dma_start(dst[HD * k:HD * k + HD, w, :, :],
                                     S[name][tile, part, half, :].rearrange("(h d) t -> d h t", d=HD))\
                          .then_inc(stacked[w], 16)
                for dst, name, rows in ((Q, "mq", 9), (Kk, "mk", 12)):
                    sp.dma_start(dst[MROW:MROW + rows, w, :, :],
                                 S[name][b].unsqueeze(1).broadcast_to([rows, GH, T])).then_inc(stacked[w], 16)

            for q in range(RING):
                load(q, q, q // 2, 0)

            def step(j, g, u):
                if u % 2 == 0 and within(j, 4, NN + 4):
                    i, b = 2 * g + u // 2 - 2, (u // 2) % 2
                    if within(i, 2, NI):
                        sp.wait_ge(finished, i - 1)
                    sp.dma_start(tmb[:, b, :], mask8[bass.ds(g - 1, 1)].broadcast_to([P, T]))\
                      .then_inc(tm_loaded[b], 16)
                q = j + 2
                if within(q, RING, NN):
                    sp.wait_ge(scored, 8 * q - 24)
                    load(q, (u + 2) % RING, 2 * g + u // 2 + 1, g + (u + 2) // RING)

            for j in range(2 * RING):
                step(j, j // RING, j % RING)
            with sp.Fori(2, NN // RING - 1) as g:
                for u in range(RING):
                    step(RING * g + u, g, u)
            for j in range(NN - RING, NN + 4):
                step(j, j // RING, j % RING)

        STACK = 16 * (12 + 2)

        @block.tensor
        def _(pe):
            pe.wait_ge(made, 7)

            def maxima(n, g, u, half):
                for k in (2 * half, 2 * half + 1):
                    h, t = k // HC, k % HC
                    if k == 0:
                        pe.wait_ge(stacked[u], STACK * g + STACK)
                    if not isinstance(n, int) or n > 0 or k >= 2:
                        pe.wait_ge(m_read, GH * HC * n + k - 1)
                    nc.tensor.matmul(ps_m[:, k % 2, :], Q[0:MAXROW, u, h, t * P:t * P + P],
                                     Kk[0:MAXROW, u, h, :], start=True, stop=True).then_inc(m_scored, 1)

            def values(n, w, s, hp):
                pe.wait_ge(exped, 8 * n + 2 * s + hp + 1)
                if s == 0 and hp == 0:
                    pe.wait_ge(v_ready, n + 1)
                    if within(n, 1, NN):
                        pe.wait_ge(o_copied, n)
                for h in (2 * hp, 2 * hp + 1):
                    last = nc.tensor.matmul(ps_o[32 * h:32 * h + 32, :], Vg[:, w % 2, s, h, :],
                                            Pe[:, 2 * (s % 2) + hp, h % 2, :],
                                            start=(s == 0), stop=(s == HC - 1), skip_group_check=True)
                last.then_inc(valued, 1)

            def step(j, g, u):
                n, w = j - 2, (u - 2) % RING
                i = 2 * g + u // 2 - 2
                for half in range(8):
                    s, hp = half // 2, half % 2
                    if within(j, 0, NN):
                        maxima(j, g, u, half)
                    if within(n, 0, NN):
                        if half == 0:
                            pe.wait_ge(m_rows[w], 16 * (g + (u - 2) // RING) + 16)
                        if not isinstance(n, int) or n > 0 or half >= 2:
                            pe.wait_ge(exped, 8 * n + half - 1)
                        for h in range(2):
                            last = nc.tensor.matmul(ps_s[:, hp, h, :],
                                                    Kk[0:NROW, w, 2 * hp + h, s * P:s * P + P],
                                                    Q[0:NROW, w, 2 * hp + h, :], start=True, stop=True)
                        last.then_inc(scored, 1)
                    if s == 0 and within(j - 3, 0, NN):
                        values(j - 3, (u - 3) % RING, HC - 1, hp)
                    elif s > 0 and within(n, 0, NN):
                        values(n, w, s - 1, hp)
                    if half == 1 and within(j - 1, 0, NN):
                        pe.wait_ge(m_read, GH * HC * j)
                        if u % 2 == 0 and within(j, 6, NN + 4):
                            pe.wait_ge(num_read, i)
                        elif u % 2 == 1 and within(j, 5, NN + 4):
                            pe.wait_ge(reciped, 4 * i + 4)
                        elif j >= 2:
                            pe.wait_ge(m_copied, j - 1)
                        nc.tensor.transpose(ps_x[0:GH * HC, 0:P], negm[:, (u - 1) % 2, :], ident[:]).then_inc(m_turned, 1)
                    if half == 3 and within(j, 4, NN + 4):
                        if within(j - 1, 0, NN):
                            pe.wait_ge(m_copied, j)
                        elif u % 2 == 0:
                            pe.wait_ge(num_read, i)
                        if u % 2 == 0:
                            pe.wait_ge(o_copied, 2 * i + 2)
                            for q in range(2):
                                last = nc.tensor.matmul(ps_x[:], dsel[:, q, :], O[:, 2 * (u // 2 % 2) + q, :],
                                                        start=(q == 0), stop=(q == 1))
                            last.then_inc(den_out, 1)
                        elif within(j, 5, NN + 4):
                            pe.wait_ge(reciped, 4 * i + 4)
                            for q in range(2):
                                last = nc.tensor.matmul(ps_x[:], sel[:, q, :], O[:, 2 * (u // 2 % 2) + q, :],
                                                        start=(q == 0), stop=(q == 1))
                            last.then_inc(picked, 1)

            steps(pe, step)

        @block.scalar
        def _(act):
            def step(j, g, u):
                n = j - 2
                for half in range(8):
                    s, hp = half // 2, half % 2
                    if within(n, 0, NN):
                        if not isinstance(n, int) or n > 0 or s >= 2:
                            act.wait_ge(valued, 8 * n + half - 3)
                        act.wait_ge(scored, 8 * n + half + 1)
                        nc.scalar.activation(Pe[:, 2 * (s % 2) + hp, :, :], ps_s[:, hp, :, :], ACT.Exp)\
                          .then_inc(exped, 1)
                    if half == 1 and within(j - 3, 0, NN):
                        act.wait_ge(valued, 8 * (j - 3) + 8)
                        if within(j - 3, 4, NN):
                            act.wait_ge(picked, 2 * g + (u - 3) // 2 - 1)
                        nc.scalar.activation(O[:, (u - 3) % 4, :], ps_o[:], ACT.Copy).then_inc(o_copied, 1)
                    if half == 1 and within(j - 1, 0, NN):
                        act.wait_ge(m_turned, j)
                        if within(j - 1, 2, NN):
                            act.wait_ge(m_split, j - 2)
                        nc.scalar.activation(mrow[:, (u - 1) % 2, :], ps_x[0:GH * HC, 0:P], ACT.Copy)\
                          .then_inc(m_copied, 1)

            steps(act, step)

        @block.vector
        def _(dve):
            def step(j, g, u):
                i, b = 2 * g + u // 2 - 2, (u // 2) % 2
                for half in range(8):
                    if within(j, 0, NN):
                        if half == 0 and within(j, 2, NN):
                            dve.wait_ge(m_turned, j - 1)
                        for k in (2 * half, 2 * half + 1):
                            dve.wait_ge(m_scored, GH * HC * j + k + 1)
                            nc.vector.tensor_reduce(negm[:, u % 2, k:k + 1], ps_m[:, k % 2, :], AX.X, ALU.max,
                                                    negate=True).then_inc(m_read, 1)
                    if u % 2 == 0 and half == 3 and within(j, 6, NN + 4):
                        dve.wait_ge(finished, i)
                        nc.vector.bn_stats(K["bn"][:, bass.ds(i - 1, 1), :].rearrange("p a s -> p (a s)"),
                                           X[:, bass.ds(i - 1, 1), :].rearrange("p a t -> p (a t)"))
                    if u % 2 == 0 and half >= 4 and within(j, 4, NN + 4):
                        dve.wait_ge(den_out, i + 1)
                        if within(i, 1, NI):
                            dve.wait_ge(num_read, i)
                        q = slice((half - 4) * P, (half - 3) * P)
                        nc.vector.reciprocal(rden[:, q], ps_x[:, q]).then_inc(reciped, 1)
                    if u % 2 == 1 and half == 5 and within(j, 5, NN + 4):
                        dve.wait_ge(picked, i + 1)
                        dve.wait_ge(reciped, 4 * i + 4)
                        if within(i, 2, NI):
                            dve.wait_ge(finished, i - 1)
                        nc.vector.scalar_tensor_tensor(out=res[:, b, :], in0=ps_x[:], scalar=gate[:, 0:1],
                                                       in1=rden[:], op0=ALU.mult, op1=ALU.mult).then_inc(num_read, 1)

            steps(dve, step)
            dve.wait_ge(finished, NI)
            nc.vector.bn_stats(K["bn"][:, NI - 1, :], X[:, NI - 1, :])



BIG = 1048576.0
MAGIC = 12582912.0


def route0(nc, io, X, K, S, mean, rstd):
    ident = K["ident"]
    E = io["m0_gate_w"].shape[0]
    TOP = 8
    with ExitStack() as ctx:
        r = Room(nc, ctx, "r0")
        wraw = r.sb("wraw", [P, HC, E])
        grow = r.sb("grow", [E, T])
        xn = r.sb("xn", [P, 4, T])
        xnT = r.sb("xnT", [P, 2, T])
        lg = r.sb("lg", [P, 2, E])
        m8 = r.sb("m8", [P, 2, 8])
        i8 = r.sb("i8", [P, 2, 8], U32)
        if8 = r.sb("if8", [P, 2, 8])
        nm = r.sb("nm", [P, 2, 1])
        e8 = r.sb("e8", [P, 2, TOP])
        esum = r.sb("esum", [P, 2])
        eq = r.sb("eq", [P, 2, TOP, E])
        eqs = r.sb("eqs", [P, 2, TOP, E])
        pos = r.sb("pos", [P, E])
        t1 = r.sb("t1", [P, E])
        row = r.sb("row", [P, E])
        rowf = r.sb("rowf", [P, TOP])
        rowi = r.sb("rowi", [P, 2, TOP], I32)
        pair = r.sb("pair", [P, 2, TOP, 2], I32)
        sel = r.sb("sel", [P, 2, E], BF16)
        ssum = r.sb("ssum", [P, 2, E], BF16)
        upper = r.sb("upper", [P, P], BF16)
        ones = r.sb("ones", [P, P], BF16)
        ioe = r.sb("ioe", [P, E])
        tok = r.sb("tok", [P, NT], I32)
        first = r.sb("first", [P, E, 2], I32)
        zeros = r.sb("zeros", [P, T])
        ps_t = r.ps("ps_t", [P, 2, 512])
        ps_l = r.ps("ps_l", [P, 2, 512])
        ps_p = r.ps("ps_p", [P, 2, 512])
        made = r.sem("made")
        loaded = r.sem("loaded")
        inited = r.sem("inited")
        cleared = r.sem("cleared")
        wready = r.sem("wready")
        wturned = r.sem("wturned")
        normed = r.sem("normed")
        stored = [r.sem(f"stored{u}") for u in range(4)]
        turned = r.sem("turned")
        xT_ready = r.sem("xT_ready")
        logits = r.sem("logits")
        chosen = r.sem("chosen")
        placed = r.sem("placed")
        top_ready = r.sem("top_ready")
        e_ready = r.sem("e_ready")
        sel_ready = r.sem("sel_ready")
        pos_ready = r.sem("pos_ready")
        pair_ready = r.sem("pair_ready")
        scattered = [r.sem(f"scattered{u}") for u in range(2)]
        dv = r.sem("dv")
        apart = r.sem("apart")
        block = r.block()

        def past(i, k):
            return not isinstance(i, int) or i >= k

        def tiles(eng, *stages):
            def turn(i, g, u):
                for s, stage in enumerate(stages):
                    if not isinstance(i, int) or 0 <= i - s < NT:
                        stage(i - s, g + (u - s) // 4, (u - s) % 4)
            for i in range(4):
                turn(i, 0, i)
            with eng.Fori(1, NT // 4) as g:
                for u in range(4):
                    turn(4 * g + u, g, u)
            for i in range(NT, NT + len(stages) - 1):
                turn(i, i // 4, i % 4)

        def nothing(i, g, u):
            return

        @block.gpsimd
        def _(pool):
            nc.gpsimd.memset(ones[:], 1.0).then_inc(made, 1)
            nc.gpsimd.memset(upper[:], 1.0).then_inc(made, 1)
            nc.gpsimd.memset(ssum[:], 0.0).then_inc(made, 1)
            nc.gpsimd.memset(zeros[:], 0.0).then_inc(made, 1)
            nc.gpsimd.memset(first[:], 0).then_inc(made, 1)
            pool.wait_ge(made, 5)
            nc.gpsimd.affine_select(out=upper[:], in_=upper[:], compare_op=ALU.is_gt, fill=0.0, base=0,
                                    pattern=[[1, P]], channel_multiplier=-1).then_inc(made, 1)
            nc.gpsimd.iota(ioe[:], [[1, E]], base=0, channel_multiplier=0,
                           allow_small_or_imprecise_dtypes=True).then_inc(made, 1)
            nc.gpsimd.iota(tok[:], [[P, NT]], base=0, channel_multiplier=1).then_inc(made, 1)
            nc.gpsimd.iota(first[:, :, 0], [[0, E]], base=NTOK, channel_multiplier=1).then_inc(made, 1)
            pool.wait_ge(inited, 16)

            def scatter(i, g, u):
                pool.wait_ge(pair_ready, i + 1)
                pool.sem_inc(apart, 1)
                for k in range(TOP):
                    pool.indirect_dma_start(
                        out=S["table0"].rearrange("c b w -> (c b) w"),
                        out_offset=bass.IndirectOffsetOnAxis(ap=rowi[:, u % 2, k:k + 1], axis=0),
                        in_=pair[:, u % 2, k, :], in_offset=None, bounds_check=P * E - 1, oob_is_err=False)\
                        .then_inc(scattered[u % 2], 16)

            tiles(pool, scatter)
            for u in range(2):
                pool.wait_ge(scattered[u], 16 * TOP * NT // 2)

        @block.sync
        def _(sp):
            sp.dma_start(grow[:], io["m0_gate_w"]).then_inc(loaded, 16)
            sp.wait_ge(made, 9)
            sp.dma_start(S["table0"], first[:]).then_inc(inited, 16)

            def store(i, g, u):
                sp.wait_ge(normed, i + 1)
                sp.dma_start(S["xg"][bass.ds(P * i, P)], xn[:, u, :]).then_inc(stored[u], 16)

            tiles(sp, store)
            clear_sums(sp, S, zeros, cleared)
            sp.wait_ge(cleared, 48)
            for u in range(4):
                sp.wait_ge(stored[u], 16 * NT // 4)

        @block.tensor
        def _(pe):
            pe.wait_ge(loaded, 16)
            gv = grow[:].rearrange("e (p c) -> e c p", c=HC)
            for c in range(HC):
                last = nc.tensor.transpose(ps_t[:, 0, c * E:c * E + E], gv[:, c, :], ident[0:E, 0:E])
            last.then_inc(wturned, 1)
            pe.wait_ge(made, 9)
            pe.wait_ge(wready, 1)

            def logit(i, g, u):
                pe.wait_ge(normed, i + 1)
                xv = xn[:, u, :].rearrange("q (p c) -> q c p", c=HC)
                if past(i, 2):
                    pe.wait_ge(xT_ready, i - 1)
                for c in range(HC):
                    last = nc.tensor.transpose(ps_t[:, u % 2, c * P:c * P + P], xv[:, c, :], ident[:])
                last.then_inc(turned, 1)
                pe.wait_ge(xT_ready, i + 1)
                if past(i, 2):
                    pe.wait_ge(chosen, CHOICES * (i - 2) + 1)
                for c in range(HC):
                    last = nc.tensor.matmul(ps_l[:, u % 2, 0:E], xnT[:, u % 2, c * P:c * P + P], wraw[:, c, :],
                                            start=(c == 0), stop=(c == HC - 1))
                last.then_inc(logits, 1)

            def place(i, g, u):
                pe.wait_ge(sel_ready, i + 1)
                if past(i, 2):
                    pe.wait_ge(placed, PLACES * (i - 2) + 1)
                nc.tensor.matmul(ps_p[:, u % 2, 0:E], ones[:], ssum[:, u % 2, :], start=True, stop=False)
                nc.tensor.matmul(ps_p[:, u % 2, 0:E], upper[:], sel[:, u % 2, :], start=False, stop=True)\
                    .then_inc(pos_ready, 1)

            tiles(pe, logit, place)

        @block.scalar
        def _(act):
            def copy(i, g, u):
                act.wait_ge(turned, i + 1)
                if past(i, 2):
                    act.wait_ge(logits, i - 1)
                nc.scalar.activation(xnT[:, u % 2, :], ps_t[:, u % 2, :], ACT.Copy).then_inc(xT_ready, 1)

            def weigh(i, g, u):
                act.wait_ge(top_ready, i + 1)
                if past(i, 2):
                    act.wait_ge(pair_ready, i - 1)
                nc.scalar.activation(e8[:, u % 2, :], m8[:, u % 2, :], ACT.Exp, bias=nm[:, u % 2, :]).then_inc(e_ready, 1)

            tiles(act, copy, weigh)

        @block.vector
        def _(dve):
            setup = Chain(dve, dv)
            dve.wait_ge(made, 9)
            dve.wait_ge(wturned, 1)
            setup(nc.vector.tensor_copy(wraw[:], ps_t[:, 0, 0:HC * E].rearrange("p (c e) -> p c e", c=HC)))
            dve.sem_inc(wready, 1)
            shape = [P, TOP, E]

            def norm(i, g, u):
                if past(i, 4):
                    dve.wait_ge(turned, i - 3)
                    dve.wait_ge(stored[u], 16 * g)
                nc.vector.tensor_scalar(xn[:, u, :], X[:, bass.ds(i, 1), :].rearrange("p a t -> p (a t)"),
                                        mean[:, bass.ds(i, 1)], rstd[:, bass.ds(i, 1)],
                                        ALU.subtract, ALU.mult).then_inc(normed, 1)

            def choose(i, u, k):
                v = u % 2
                if k > 0:
                    dve.wait_ge(chosen, CHOICES * i + k)
                if k == 0:
                    dve.wait_ge(logits, i + 1)
                    ins = nc.vector.tensor_copy(lg[:, v, :], ps_l[:, v, 0:E])
                elif k == 1:
                    dve.sem_inc(apart, 1)
                    ins = nc.vector.max(m8[:, v, :], lg[:, v, :])
                elif k == 2:
                    ins = nc.vector.tensor_scalar(nm[:, v, :], m8[:, v, 0:1], -1.0, None, ALU.mult)
                elif k == 3:
                    dve.sem_inc(top_ready, 1)
                    ins = nc.vector.max_index(i8[:, v, :], m8[:, v, :], lg[:, v, :])
                elif k == 4:
                    ins = nc.vector.tensor_copy(if8[:, v, :], i8[:, v, :])
                elif k == 5:
                    ins = nc.vector.tensor_tensor(eq[:, v], ioe[:].unsqueeze(1).broadcast_to(shape),
                                                  if8[:, v, :].unsqueeze(2).broadcast_to(shape), ALU.is_equal)
                elif k == 6:
                    if past(i, 2):
                        dve.wait_ge(pos_ready, i - 1)
                    dve.sem_inc(apart, 1)
                    with nc.allow_low_precision(reason="counts of zero or one"):
                        ins = nc.vector.tensor_reduce(sel[:, v, :], eq[:, v].rearrange("p k e -> p e k"), AX.X, ALU.add)
                else:
                    dve.sem_inc(sel_ready, 1)
                    if past(i, 1):
                        dve.wait_ge(pos_ready, i)
                    ins = nc.vector.tensor_tensor(ssum[:, 1 - v, :], ssum[:, v, :], sel[:, v, :], ALU.add)
                ins.then_inc(chosen, 1)

            def place(i, g, u, k):
                v = u % 2
                if k > 0:
                    dve.wait_ge(placed, PLACES * i + k)
                w = pair[:, v, :, 1].bitcast(F32)
                if k == 0:
                    dve.wait_ge(pos_ready, i + 1)
                    ins = nc.vector.tensor_copy(pos[:], ps_p[:, v, 0:E])
                elif k == 1:
                    ins = nc.vector.tensor_scalar(t1[:], pos[:], float(P), BIG, ALU.is_ge, ALU.mult)
                elif k == 2:
                    ins = nc.vector.scalar_tensor_tensor(out=row[:], in0=pos[:], scalar=float(E), in1=t1[:],
                                                         op0=ALU.mult, op1=ALU.add)
                elif k == 3:
                    ins = nc.vector.tensor_tensor(row[:], row[:], ioe[:], ALU.add)
                elif k == 4:
                    ins = nc.vector.tensor_tensor(eqs[:, v], eq[:, v], row[:].unsqueeze(1).broadcast_to(shape), ALU.mult)
                elif k == 5:
                    dve.wait_ge(e_ready, i + 1)
                    ins = nc.vector.tensor_reduce(esum[:, v:v + 1], e8[:, v, :], AX.X, ALU.add)
                elif k == 6:
                    dve.sem_inc(apart, 1)
                    ins = nc.vector.tensor_reduce(rowf[:], eqs[:, v], AX.X, ALU.add)
                elif k == 7:
                    if past(i, 2):
                        half = 2 * g + u // 2
                        dve.wait_ge(scattered[v], 16 * TOP * half)
                    ins = nc.vector.tensor_copy(rowi[:, v, :], rowf[:])
                elif k == 8:
                    ins = nc.vector.reciprocal(esum[:, v:v + 1], esum[:, v:v + 1])
                elif k == 9:
                    ins = nc.vector.tensor_scalar(w, e8[:, v, :], esum[:, v:v + 1], None, ALU.mult)
                else:
                    ins = nc.vector.tensor_copy(pair[:, v, :, 0], tok[:, bass.ds(i, 1)].broadcast_to([P, TOP]))
                ins.then_inc(placed, 1)
                if k == PLACES - 1:
                    dve.wait_ge(placed, PLACES * i + PLACES)
                    dve.sem_inc(pair_ready, 1)

            def turn(i, g, u):
                if not isinstance(i, int) or i < NT:
                    norm(i, g, u)
                for k in range(max(CHOICES, PLACES)):
                    if k < PLACES and (not isinstance(i, int) or 0 <= i - 2 < NT):
                        place(i - 2, g + (u - 2) // 4, (u - 2) % 4, k)
                    if k < CHOICES and (not isinstance(i, int) or 0 <= i - 1 < NT):
                        choose(i - 1, (u - 1) % 4, k)

            for i in range(4):
                turn(i, 0, i)
            with dve.Fori(1, NT // 4) as g:
                for u in range(4):
                    turn(4 * g + u, g, u)
            for i in range(NT, NT + 2):
                turn(i, i // 4, i % 4)


CHOICES, PLACES = 8, 11


def clear_sums(eng, S, zeros, done):
    for k in range(2):
        eng.dma_start(S[f"y{k}"].rearrange("(n p) t -> p n t", p=P),
                      zeros[:].unsqueeze(1).broadcast_to([P, NTOK // P + 1, T])).then_inc(done, 16)
    eng.dma_start(S["xg"][NTOK:NTOK + P], zeros[:]).then_inc(done, 16)


def route1(nc, io, X, K, S, mean, rstd, rowi, pair):
    ident = K["ident"]
    E = io["f1_router_w"].shape[1]
    TOP = 2
    slots = BLOCKS1
    RING = 2
    with ExitStack() as ctx:
        r = Room(nc, ctx, "r1")
        wraw = r.sb("wraw", [P, HC, E])
        rsc = r.sb("rsc", [P, HC])
        pre = r.sb("pre", [P, HC])
        psb = r.sb("psb", [P, E])
        xn = r.sb("xn", [P, RING, T])
        xnT = r.sb("xnT", [P, RING, T])
        dd = r.sb("dd", [P, RING, T])
        dh = r.sb("dh", [P, RING, T])
        dl = r.sb("dl", [P, RING, T])
        lg = r.sb("lg", [P, NT, E])
        m8 = r.sb("m8", [P, NT, 8])
        i8 = r.sb("i8", [P, NT, 8], U32)
        if8 = r.sb("if8", [P, NT, TOP])
        e2 = r.sb("e2", [P, NT, TOP])
        esum = r.sb("esum", [P, NT])
        eq = r.sb("eq", [P, NT, TOP, E])
        eqs = r.sb("eqs", [P, NT, TOP, E])
        before = r.sb("before", [P, 2, NT, E])
        pos = r.sb("pos", [P, NT, E])
        t1 = r.sb("t1", [P, NT, E])
        row = r.sb("row", [P, NT, E])
        rowf = r.sb("rowf", [P, NT, TOP])
        sel = r.sb("sel", [P, NT, E], BF16)
        upper = r.sb("upper", [P, P], BF16)
        ones = r.sb("ones", [P, P], BF16)
        ioe = r.sb("ioe", [P, E])
        tok = r.sb("tok", [P, NT], I32)
        first = r.sb("first", [P, slots, 2], I32)
        counts = r.sb("counts", [P, 4, E])
        iob = r.sb("iob", [P, slots, E])
        own = r.sb("own", [P, slots])
        owni = r.sb("owni", [P, slots], I32)
        ps_t = r.ps("ps_t", [P, 2, 512])
        ps_l = r.ps("ps_l", [P, 512])
        ps_p = r.ps("ps_p", [P, 512])
        ps_c = r.ps("ps_c", [P, 512])
        made = r.sem("made")
        loaded = r.sem("loaded")
        wready = r.sem("wready")
        normed = r.sem("normed")
        stored = [r.sem(f"stored{u}") for u in range(RING)]
        turned = r.sem("turned")
        xT_ready = r.sem("xT_ready")
        dense_ready = r.sem("dense_ready")
        high = r.sem("high")
        low = r.sem("low")
        kept = [r.sem(f"kept{u}") for u in range(RING)]
        spilled = r.sem("spilled")
        logits = r.sem("logits")
        shifted = r.sem("shifted")
        e_ready = r.sem("e_ready")
        sel_ready = r.sem("sel_ready")
        pos_ready = r.sem("pos_ready")
        own_ready = r.sem("own_ready")
        cleared = r.sem("cleared")
        dv = r.sem("dv")
        block = r.block()

        def past(i, k):
            return not isinstance(i, int) or i >= k

        def tiles(eng, *stages):
            def turn(i, g, u):
                for s, stage in enumerate(stages):
                    if not isinstance(i, int) or 0 <= i - s < NT:
                        stage(i - s, g + (u - s) // RING, (u - s) % RING)
            for i in range(2 * RING):
                turn(i, i // RING, i % RING)
            with eng.Fori(2, NT // RING) as g:
                for u in range(RING):
                    turn(RING * g + u, g, u)
            for i in range(NT, NT + len(stages) - 1):
                turn(i, i // RING, i % RING)

        def nothing(i, g, u):
            return

        @block.gpsimd
        def _(pool):
            nc.gpsimd.memset(ones[:], 1.0).then_inc(made, 1)
            nc.gpsimd.memset(upper[:], 1.0).then_inc(made, 1)
            nc.gpsimd.memset(first[:], 0).then_inc(made, 1)
            pool.wait_ge(made, 3)
            nc.gpsimd.affine_select(out=upper[:], in_=upper[:], compare_op=ALU.is_gt, fill=0.0, base=0,
                                    pattern=[[1, P]], channel_multiplier=-1).then_inc(made, 1)
            nc.gpsimd.iota(ioe[:], [[1, E]], base=0, channel_multiplier=0,
                           allow_small_or_imprecise_dtypes=True).then_inc(made, 1)
            nc.gpsimd.iota(tok[:], [[P, NT]], base=0, channel_multiplier=1).then_inc(made, 1)
            nc.gpsimd.iota(first[:, :, 0], [[0, slots]], base=NTOK, channel_multiplier=1).then_inc(made, 1)
            nc.gpsimd.iota(iob[:], [[1, slots], [0, E]], base=0, channel_multiplier=0,
                           allow_small_or_imprecise_dtypes=True).then_inc(made, 1)
            pool.wait_ge(loaded, 64)

            def dense(i, g, u):
                pool.wait_ge(xT_ready, i + 1)
                if past(i, 2):
                    pool.wait_ge(low, i - 1)
                nc.gpsimd.tensor_tensor(dd[:, u, :].rearrange("p (c n) -> p c n", c=HC),
                                        xnT[:, u, :].rearrange("p (c n) -> p c n", c=HC),
                                        pre[:].unsqueeze(2).broadcast_to([P, HC, P]), ALU.mult)\
                    .then_inc(dense_ready, 1)

            tiles(pool, nothing, dense)

        @block.sync
        def _(sp):
            sp.dma_start(wraw[:], io["f1_router_w"].rearrange("(p c) e -> p c e", c=HC)).then_inc(loaded, 16)
            sp.dma_start(rsc[:], io["f1_router_scale"].rearrange("(p c) -> p c", c=HC)).then_inc(loaded, 16)
            sp.dma_start(pre[:], io["f1_rn_pre1"].rearrange("(p c) -> p c", c=HC)).then_inc(loaded, 16)
            sp.dma_start(psb[:], row_of(io["f1_per_expert_scale"])).then_inc(loaded, 16)

            def store(i, g, u):
                sp.wait_ge(normed, i + 1)
                sp.dma_start(S["xg"][bass.ds(P * i, P)], xn[:, u, :]).then_inc(stored[u], 16)

            def keep(i, g, u):
                for k, (done, x) in enumerate(((high, dh), (low, dl))):
                    sp.wait_ge(done, i + 1)
                    sp.dma_start(S["dT"][k][:, :, bass.ds(P * i, P)], x[:, u, :].rearrange("p (c n) -> p c n", c=HC))\
                      .then_inc(kept[u], 16)

            tiles(sp, store, nothing, keep)
            sp.dma_start(S["res"].rearrange("n p t -> p n t"), X[:]).then_inc(spilled, 16)
            sp.wait_ge(made, 8)
            sp.dma_start(S["table1"], first[:]).then_inc(cleared, 16)
            sp.wait_ge(own_ready, 1)
            sp.dma_start(S["owner"], owni[0:1, :]).then_inc(cleared, 16)
            sp.wait_ge(cleared, 32)
            for u in range(RING):
                sp.wait_ge(stored[u], 16 * NT // RING)
                sp.wait_ge(kept[u], 32 * NT // RING)
            sp.wait_ge(spilled, 16)

        @block.tensor
        def _(pe):
            def turn(i, g, u):
                pe.wait_ge(normed, i + 1)
                if past(i, 2):
                    pe.wait_ge(xT_ready, i - 1)
                xv = xn[:, u, :].rearrange("q (p c) -> q c p", c=HC)
                for c in range(HC):
                    last = nc.tensor.transpose(ps_t[:, u, c * P:c * P + P], xv[:, c, :], ident[:])
                last.then_inc(turned, 1)

            def logit(i, g, u):
                if isinstance(i, int) and i == 0:
                    pe.wait_ge(wready, 1)
                pe.wait_ge(xT_ready, i + 1)
                for c in range(HC):
                    last = nc.tensor.matmul(ps_l[:, bass.ds(E * i, E)], xnT[:, u, c * P:c * P + P], wraw[:, c, :],
                                            start=(c == 0), stop=(c == HC - 1))
                last.then_inc(logits, 1)

            tiles(pe, turn, logit)
            pe.wait_ge(made, 8)
            pe.wait_ge(sel_ready, 1)
            s = sel[:].rearrange("p n e -> p (n e)")
            nc.tensor.matmul(ps_p[:, 0:NT * E], upper[:], s, start=True, stop=True)
            nc.tensor.matmul(ps_c[:, 0:NT * E], ones[:], s, start=True, stop=True).then_inc(pos_ready, 1)

        @block.scalar
        def _(act):
            def copy(i, g, u):
                act.wait_ge(turned, i + 1)
                if past(i, 2):
                    act.wait_ge(logits, i - 1)
                    act.wait_ge(dense_ready, i - 1)
                nc.scalar.activation(xnT[:, u, :], ps_t[:, u, :], ACT.Copy).then_inc(xT_ready, 1)

            tiles(act, copy, nothing)
            act.wait_ge(shifted, 1)
            nc.scalar.activation(e2[:], e2[:], ACT.Exp).then_inc(e_ready, 1)

        @block.vector
        def _(dve):
            c = Chain(dve, dv)
            dve.wait_ge(loaded, 64)
            for k in range(HC):
                ins = nc.vector.tensor_scalar(wraw[:, k, :], wraw[:, k, :], rsc[:, k:k + 1], T ** -0.5,
                                              ALU.mult, ALU.mult)
            c(ins)
            dve.sem_inc(wready, 1)

            def norm(i, g, u):
                if past(i, 2):
                    dve.wait_ge(turned, i - 1)
                    dve.wait_ge(stored[u], 16 * g)
                nc.vector.tensor_scalar(xn[:, u, :], X[:, bass.ds(i, 1), :].rearrange("p a t -> p (a t)"),
                                        mean[:, bass.ds(i, 1)], rstd[:, bass.ds(i, 1)],
                                        ALU.subtract, ALU.mult).then_inc(normed, 1)

            def parts(i, g, u):
                dve.wait_ge(dense_ready, i + 1)
                if past(i, 2):
                    dve.wait_ge(kept[u], 32 * g)
                nc.vector.tensor_scalar(dh[:, u, :].bitcast(I32), dd[:, u, :].bitcast(I32), HIGH, None,
                                        ALU.bitwise_and).then_inc(high, 1)
                dve.wait_ge(high, i + 1)
                nc.vector.tensor_tensor(dl[:, u, :], dd[:, u, :], dh[:, u, :], ALU.subtract).then_inc(low, 1)

            tiles(dve, norm, nothing, parts)
            dve.wait_ge(made, 8)
            dve.wait_ge(logits, NT)
            c(nc.vector.tensor_copy(lg[:].rearrange("p n e -> p (n e)"), ps_l[:, 0:NT * E]))
            for i in range(NT):
                ins = nc.vector.max(m8[:, i, :], lg[:, i, :])
            c(ins)
            for i in range(NT):
                ins = nc.vector.max_index(i8[:, i, :], m8[:, i, :], lg[:, i, :])
            c(nc.vector.tensor_tensor(e2[:], m8[:, :, 0:TOP], m8[:, :, 0:1].broadcast_to([P, NT, TOP]), ALU.subtract))
            dve.sem_inc(shifted, 1)
            c(nc.vector.tensor_copy(if8[:], i8[:, :, 0:TOP]))
            shape = [P, NT, TOP, E]
            c(nc.vector.tensor_tensor(eq[:], ioe[:].unsqueeze(1).unsqueeze(1).broadcast_to(shape),
                                      if8[:].unsqueeze(3).broadcast_to(shape), ALU.is_equal))
            c(nc.vector.tensor_tensor(sel[:], eq[:, :, 0, :], eq[:, :, 1, :], ALU.add))
            dve.sem_inc(sel_ready, 1)
            dve.wait_ge(e_ready, 1)
            c(nc.vector.tensor_tensor(esum[:], e2[:, :, 0], e2[:, :, 1], ALU.add))
            c(nc.vector.reciprocal(esum[:], esum[:]))
            wgt = pair[:, :, :, 1].bitcast(F32)
            c(nc.vector.tensor_tensor(eqs[:], eq[:], psb[:].unsqueeze(1).unsqueeze(1).broadcast_to(shape), ALU.mult))
            c(nc.vector.tensor_reduce(rowf[:], eqs[:], AX.X, ALU.add))
            c(nc.vector.tensor_tensor(e2[:], e2[:], esum[:].unsqueeze(2).broadcast_to([P, NT, TOP]), ALU.mult))
            c(nc.vector.tensor_tensor(wgt, e2[:], rowf[:], ALU.mult))
            c(nc.vector.tensor_copy(pair[:, :, :, 0], tok[:].unsqueeze(2).broadcast_to([P, NT, TOP])))
            dve.wait_ge(pos_ready, 1)
            cnt = ps_c[:, 0:NT * E].rearrange("p (n e) -> p n e", e=E)
            c(nc.vector.tensor_copy(before[:, 0], cnt))
            step, k = 1, 0
            while step < NT:
                a, z = before[:, k], before[:, 1 - k]
                nc.vector.tensor_copy(z[:, 0:step], a[:, 0:step])
                c(nc.vector.tensor_tensor(z[:, step:], a[:, step:], a[:, 0:NT - step], ALU.add))
                step, k = 2 * step, 1 - k
            incl_t = before[:, k]
            total, nblk, incl, ob = (counts[:, j, :] for j in range(4))
            c(nc.vector.tensor_scalar(total, incl_t[:, NT - 1, :], P / 2 - 0.5, 1.0 / P, ALU.add, ALU.mult))
            c(nc.vector.tensor_tensor(pos[:], incl_t, cnt, ALU.subtract))
            c(nc.vector.tensor_tensor(pos[:], pos[:], ps_p[:, 0:NT * E].rearrange("p (n e) -> p n e", e=E), ALU.add))
            c(nc.vector.tensor_scalar(nblk, total, MAGIC, None, ALU.add))
            c(nc.vector.tensor_scalar(nblk, nblk, -MAGIC, None, ALU.add))
            c(nc.vector.memset(total, 1.0))
            c(nc.vector.tensor_tensor_scan(incl, total, nblk, 0.0, ALU.mult, ALU.add))
            c(nc.vector.tensor_tensor(ob, incl, nblk, ALU.subtract))
            c(nc.vector.tensor_tensor(iob[:], iob[:], incl.unsqueeze(1).broadcast_to([P, slots, E]), ALU.is_ge))
            c(nc.vector.tensor_reduce(own[:], iob[:], AX.X, ALU.add))
            c(nc.vector.tensor_scalar(own[:], own[:], float(E - 1), None, ALU.min))
            c(nc.vector.tensor_copy(owni[:], own[:]))
            dve.sem_inc(own_ready, 1)
            c(nc.vector.tensor_scalar(t1[:], pos[:], -(P / 2 - 0.5), 1.0 / P, ALU.add, ALU.mult))
            c(nc.vector.tensor_scalar(t1[:], t1[:], MAGIC, None, ALU.add))
            c(nc.vector.tensor_scalar(t1[:], t1[:], -MAGIC, 1.0 - P * slots, ALU.add, ALU.mult))
            c(nc.vector.scalar_tensor_tensor(out=row[:], in0=pos[:], scalar=float(slots), in1=t1[:],
                                             op0=ALU.mult, op1=ALU.add))
            c(nc.vector.tensor_tensor(row[:], row[:], ob.unsqueeze(1).broadcast_to([P, NT, E]), ALU.add))
            for k in range(TOP):
                ins = nc.vector.tensor_tensor(eqs[:, :, k, :], eq[:, :, k, :], row[:], ALU.mult)
            c(ins)
            c(nc.vector.tensor_reduce(rowf[:], eqs[:], AX.X, ALU.add))
            c(nc.vector.tensor_copy(rowi[:], rowf[:]))


def experts(nc, io, S, tag, I, blocks, table, wg, wu, wd, func, pre, owner=None):
    IC = I // 2
    RING = 4
    AHEAD = 6
    RI = 8
    with ExitStack() as ctx:
        r = Room(nc, ctx, tag)
        tab = r.sb("tab", [P, blocks, 2], I32)
        ow = r.sb("ow", [1, blocks], I32)
        prec = r.sb("prec", [P, HC])
        idx = r.sb("idx", [P, RI, 1], I32)
        xe = r.sb("xe", [P, RING, T])
        xeT = r.sb("xeT", [P, 2, T])
        wgu = r.sb("wgu", [P, RING, HC, 2 * I])
        wdn = r.sb("wdn", [IC, RING, 2, T])
        sg = r.sb("sg", [P, 2, I])
        h = r.sb("h", [P, 2, I])
        hT = r.sb("hT", [IC, 2, 2 * P])
        oe = r.sb("oe", [P, RING, T])
        ident = r.sb("id", [P, P])
        ps_t = r.ps("ps_t", [P, 2, 512])
        ps_g = r.ps("ps_g", [P, 2, 512])
        ps_h = r.ps("ps_h", [P, 2, 512])
        ps_d = r.ps("ps_d", [P, 2, 512])
        made = r.sem("made")
        tabbed = r.sem("tabbed")
        indexed = r.sem("indexed")
        gathered = [r.sem(f"gathered{u}") for u in range(RING)]
        turned = r.sem("turned")
        xT_ready = r.sem("xT_ready")
        w_in = [r.sem(f"w_in{u}") for u in range(RING)]
        d_in = [r.sem(f"d_in{u}") for u in range(RING)]
        gated = r.sem("gated")
        acted = r.sem("acted")
        h_ready = r.sem("h_ready")
        h_turned = r.sem("h_turned")
        hT_ready = r.sem("hT_ready")
        downed = r.sem("downed")
        o_ready = r.sem("o_ready")
        added = [r.sem(f"added{u}") for u in range(2)]
        apart = r.sem("apart")
        block = r.block()
        TABBED = 48 if owner is not None else 32

        def schedule(eng, *stages):
            def turn(g, u):
                for s, stage in enumerate(stages):
                    n, past = RING * g + u - s, (u - s) // RING
                    if not isinstance(n, int) or 0 <= n < blocks:
                        stage(n, g + past, (u - s) % RING)

            for j in range(2 * RING):
                turn(j // RING, j % RING)
            with eng.Fori(2, blocks // RING) as g:
                for u in range(RING):
                    turn(g, u)
            for j in range(blocks // RING * RING, blocks + len(stages) - 1):
                turn(j // RING, j % RING)

        @block.gpsimd
        def _(pool):
            nc.gpsimd.memset(ident[:], 0.0).then_inc(made, 1)
            pool.wait_ge(made, 1)
            nc.gpsimd.affine_select(out=ident[:], in_=ident[:], compare_op=ALU.not_equal, fill=1.0,
                                    base=0, pattern=[[-1, P]], channel_multiplier=1).then_inc(made, 1)
            pool.wait_ge(tabbed, TABBED)

            def gather(n, u):
                nc.gpsimd.tensor_copy(idx[:, u, :], tab[:, bass.ds(n, 1), 0]).then_inc(indexed, 1)
                pool.wait_ge(indexed, n + 1)
                if not isinstance(n, int) or n >= RING:
                    pool.wait_ge(turned, n - RING + 1)
                pool.sem_inc(apart, 1)
                pool.indirect_dma_start(out=xe[:, u % RING, :], out_offset=None, in_=S["xg"],
                                        in_offset=bass.IndirectOffsetOnAxis(ap=idx[:, u, 0:1], axis=0))\
                    .then_inc(gathered[u % RING], 16)

            def scatter(n, g, u):
                if not isinstance(n, int) or n >= 2:
                    pool.wait_ge(added[u % 2], 16 * (RI // 2 * g + u // 2))
                pool.wait_ge(o_ready, n + 1)
                pool.sem_inc(apart, 1)
                pool.indirect_dma_start(out=S[f"y{u % 2}"],
                                        out_offset=bass.IndirectOffsetOnAxis(ap=idx[:, u, 0:1], axis=0),
                                        in_=oe[:, u % RING, :], in_offset=None, compute_op=ALU.add)\
                    .then_inc(added[u % 2], 16)

            for n in range(AHEAD):
                gather(n, n)
            for n in range(RI):
                scatter(n, 0, n)
                gather(n + AHEAD, (n + AHEAD) % RI)
            groups = (blocks - AHEAD) // RI
            with pool.Fori(1, groups) as g:
                for u in range(RI):
                    scatter(RI * g + u, g, u)
                    gather(RI * g + u + AHEAD, (u + AHEAD) % RI)
            for n in range(RI * groups, blocks):
                scatter(n, n // RI, n % RI)
                if n + AHEAD < blocks:
                    gather(n + AHEAD, (n + AHEAD) % RI)
            for k in range(2):
                pool.wait_ge(added[k], 16 * ((blocks + 1 - k) // 2))

        @block.sync
        def _(sp):
            sp.dma_start(tab[:], table).then_inc(tabbed, 16)
            if pre is not None:
                sp.dma_start(prec[:], pre.rearrange("(p c) -> p c", c=HC)).then_inc(tabbed, 16)
            else:
                sp.sem_inc(tabbed, 16)
            if owner is not None:
                sp.dma_start(ow[:], owner).then_inc(tabbed, 16)
                sp.wait_ge(tabbed, TABBED)

            def weights(n, g, u):
                e = n
                if owner is not None:
                    e = sp.value_load(ow[0:1, bass.ds(n, 1)], min_val=0, max_val=wg.shape[0] - 1)
                e = bass.ds(e, 1)
                old = not isinstance(n, int) or n >= RING
                if old:
                    sp.wait_ge(gated, n - RING + 1)
                for k, w in enumerate((wg, wu)):
                    sp.dma_start(wgu[:, u, :, k * I:k * I + I],
                                 w[e].rearrange("a (p c) i -> p (a c) i", c=HC)).then_inc(w_in[u], 16)
                if old:
                    sp.wait_ge(downed, n - RING + 1)
                sp.dma_start(wdn[:, u, :, :], wd[e].rearrange("a (p c) n -> p (a c) n", c=2)).then_inc(d_in[u], 16)

            schedule(sp, weights)

        @block.tensor
        def _(pe):
            pe.wait_ge(made, 2)

            def turn_rows(n, g, u):
                pe.wait_ge(gathered[u], 16 * g + 16)
                if not isinstance(n, int) or n >= 2:
                    pe.wait_ge(xT_ready, n - 1)
                xv = xe[:, u, :].rearrange("q (p c) -> q c p", c=HC)
                for c in range(HC):
                    last = nc.tensor.transpose(ps_t[:, u % 2, c * P:c * P + P], xv[:, c, :], ident[:])
                last.then_inc(turned, 1)

            def gate_up(n, g, u):
                pe.wait_ge(xT_ready, n + 1)
                pe.wait_ge(w_in[u], 32 * g + 32)
                if not isinstance(n, int) or n >= 2:
                    pe.wait_ge(h_ready, n - 1)
                for c in range(HC):
                    last = nc.tensor.matmul(ps_g[:, u % 2, 0:2 * I], xeT[:, u % 2, c * P:c * P + P],
                                            wgu[:, u, c, :], start=(c == 0), stop=(c == HC - 1))
                last.then_inc(gated, 1)

            def turn_hidden(n, g, u):
                pe.wait_ge(h_ready, n + 1)
                if not isinstance(n, int) or n >= 2:
                    pe.wait_ge(hT_ready, n - 1)
                hv = h[:, u % 2, :].rearrange("q (p c) -> q c p", c=2)
                for c in range(2):
                    last = nc.tensor.transpose(ps_h[0:IC, u % 2, c * P:c * P + P], hv[:, c, :], ident[:])
                last.then_inc(h_turned, 1)

            def down(n, g, u):
                pe.wait_ge(hT_ready, n + 1)
                pe.wait_ge(d_in[u], 16 * g + 16)
                if not isinstance(n, int) or n >= 2:
                    pe.wait_ge(o_ready, n - 1)
                for c in range(2):
                    last = nc.tensor.matmul(ps_d[:, u % 2, :], hT[:, u % 2, c * P:c * P + P], wdn[:, u, c, :],
                                            start=(c == 0), stop=(c == 1))
                last.then_inc(downed, 1)

            schedule(pe, turn_rows, gate_up, turn_hidden, down)

        @block.scalar
        def _(act):
            act.wait_ge(tabbed, TABBED)

            def copy_rows(n, g, u):
                act.wait_ge(turned, n + 1)
                if not isinstance(n, int) or n >= 2:
                    act.wait_ge(gated, n - 1)
                if pre is None:
                    nc.scalar.activation(xeT[:, u % 2, :], ps_t[:, u % 2, :], ACT.Copy).then_inc(xT_ready, 1)
                else:
                    for c in range(HC):
                        ins = nc.scalar.activation(xeT[:, u % 2, c * P:c * P + P], ps_t[:, u % 2, c * P:c * P + P],
                                                   ACT.Copy, scale=prec[:, c:c + 1])
                    ins.then_inc(xT_ready, 1)

            def gate(n, g, u):
                act.wait_ge(gated, n + 1)
                if not isinstance(n, int) or n >= 2:
                    act.wait_ge(h_ready, n - 1)
                nc.scalar.activation(sg[:, u % 2, :], ps_g[:, u % 2, 0:I], func).then_inc(acted, 1)

            def copy_hidden(n, g, u):
                act.wait_ge(h_turned, n + 1)
                if not isinstance(n, int) or n >= 2:
                    act.wait_ge(downed, n - 1)
                nc.scalar.activation(hT[:, u % 2, :], ps_h[0:IC, u % 2, 0:2 * P], ACT.Copy).then_inc(hT_ready, 1)

            schedule(act, copy_rows, gate, copy_hidden)

        @block.vector
        def _(dve):
            dve.wait_ge(tabbed, TABBED)
            wcol = tab[:].bitcast(F32)

            def rows_alone(n, g, u):
                return

            def hidden(n, g, u):
                dve.wait_ge(acted, n + 1)
                if not isinstance(n, int) or n >= 2:
                    dve.wait_ge(h_turned, n - 1)
                nc.vector.scalar_tensor_tensor(out=h[:, u % 2, :], in0=ps_g[:, u % 2, I:2 * I],
                                               scalar=wcol[:, bass.ds(n, 1), 1],
                                               in1=sg[:, u % 2, :], op0=ALU.mult, op1=ALU.mult).then_inc(h_ready, 1)

            def results(n, g, u):
                dve.wait_ge(downed, n + 1)
                if not isinstance(n, int) or n >= RING:
                    dve.wait_ge(added[u % 2], 16 * (RING // 2 * (g - 1) + u // 2 + 1))
                nc.vector.tensor_copy(oe[:, u, :], ps_d[:, u % 2, :]).then_inc(o_ready, 1)

            schedule(dve, rows_alone, hidden, rows_alone, results)


def moe0(nc, io, X, K, S):
    gate = K["gate"]
    E = io["m0_gate_w"].shape[0]
    with ExitStack() as outer:
        o = Room(nc, outer, "m0")
        mean = o.sb("mean", [P, NT])
        rstd = o.sb("rstd", [P, NT])
        row_stats(nc, K, "m0_st", 1e-5, mean, rstd)
        route0(nc, io, X, K, S, mean, rstd)
    experts(nc, io, S, "m0e", io["m0_wg"].shape[2], E, S["table0"], io["m0_wg"], io["m0_wu"], io["m0_wd"],
            ACT.Silu, None)
    with ExitStack() as ctx:
        r = Room(nc, ctx, "m0a")
        y = r.sb("y", [P, 8, T])
        loaded = [r.sem(f"loaded{k}") for k in range(8)]
        summed = r.sem("summed")
        added = r.sem("added")
        block = r.block()

        @block.sync
        def _(sp):
            for i in range(2 * NT):
                if i >= 8:
                    sp.wait_ge(added, i // 2 - 3)
                sp.dma_start(y[:, i % 8, :], S[f"y{i % 2}"][i // 2 * P:i // 2 * P + P]).then_inc(loaded[i % 8], 16)

        @block.gpsimd
        def _(pool):
            for i in range(NT):
                a, b = 2 * i % 8, 2 * i % 8 + 1
                for k in (a, b):
                    pool.wait_ge(loaded[k], 16 * (2 * i // 8) + 16)
                nc.gpsimd.tensor_tensor(y[:, a, :], y[:, a, :], y[:, b, :], ALU.add).then_inc(summed, 1)

        @block.vector
        def _(dve):
            for i in range(NT + 1):
                if i < NT:
                    dve.wait_ge(summed, i + 1)
                    nc.vector.scalar_tensor_tensor(out=X[:, i, :], in0=y[:, 2 * i % 8, :], scalar=gate[:, 2:3],
                                                   in1=X[:, i, :], op0=ALU.mult, op1=ALU.add).then_inc(added, 1)
                if i > 0:
                    dve.wait_ge(added, i)
                    nc.vector.bn_stats(K["bn"][:, i - 1, :], X[:, i - 1, :])



DH = T // NH
SW = C + P
HW = DH + 1
MASKED = -1.0e30
LN_EPS = 1e-6


def mlstm(nc, io, X, K, S):
    with ExitStack() as outer:
        o = Room(nc, outer, "ml")
        mean = o.sb("mean", [P, NT])
        rstd = o.sb("rstd", [P, NT])
        acol = o.sb("acol", [P, 2, CT, B * NH])
        en = o.sb("en", [P, CT, B * NH])
        row_stats(nc, K, "ml_st", 1e-5, mean, rstd)
        gates(nc, io, X, K, S, mean, rstd, acol, en)
        mix(nc, io, X, K, S, acol, en)


def gates(nc, io, X, K, S, mean, rstd, acol, en):
    ident = K["ident"]
    G2 = 2 * NH
    with ExitStack() as ctx:
        r = Room(nc, ctx, "mg")
        wq = r.sb("wq", [P, HC, G2])
        wkv = r.sb("wkv", [P, HC, G2])
        wraw = r.sb("wraw", [P, 2, HC, G2])
        brow = r.sb("brow", [P, G2])
        ones = r.sb("ones", [P, C])
        xn = r.sb("xn", [P, 2, T])
        cx = r.sb("cx", [P, 4, T])
        xT = r.sb("xT", [P, 4, 2, T])
        xh = r.sb("xh", [P, 4, 2, T])
        xl = r.sb("xl", [P, 4, 2, T])
        gi = r.sb("gi", [P, CT, B * NH])
        gf = r.sb("gf", [P, CT, B * NH])
        ga = r.sb("ga", [P, CT, B * NH])
        gl = r.sb("gl", [P, CT, B * NH])
        Fc = r.sb("F", [P, C])
        a = r.sb("a", [P, C])
        M = r.sb("M", [P, C])
        mx = r.sb("mx", [P, C])
        nM = r.sb("nM", [P, C])
        ps_q = r.ps("ps_q", [P, 2, 512])
        ps_c = r.ps("ps_c", [P, 2, 512])
        ps_g = r.ps("ps_g", [P, 512])
        ps_r = r.ps("ps_r", [P, 512])
        ps_b = r.ps("ps_b", [P, 512])
        made = r.sem("made")
        wload = r.sem("wload")
        summed = r.sem("summed")
        c_in = [r.sem(f"c_in{u}") for u in range(4)]
        normed = r.sem("normed")
        q_turned = r.sem("q_turned")
        c_turned = r.sem("c_turned")
        q_copied = r.sem("q_copied")
        c_copied = r.sem("c_copied")
        high = r.sem("high")
        low = r.sem("low")
        kept = [r.sem(f"kept{u}") for u in range(4)]
        gated = r.sem("gated")
        abs_ready = r.sem("abs_ready")
        ln_ready = r.sem("ln_ready")
        l_ready = r.sem("l_ready")
        rows_turned = r.sem("rows_turned")
        rows_ready = r.sem("rows_ready")
        cols = r.sem("cols")
        cols_ready = r.sem("cols_ready")
        nM_stored = r.sem("nM_stored")
        av = r.sem("av")
        dv = r.sem("dv")
        block = r.block()

        def tiles(eng, front, back):
            def turn(i, g, u):
                if not isinstance(i, int) or i < NT:
                    front(i, g, u)
                if not isinstance(i, int) or i >= 1:
                    back(i - 1, g + (u - 1) // 4, (u - 1) % 4)
            for i in range(4):
                turn(i, 0, i)
            with eng.Fori(1, NT // 4) as g:
                for u in range(4):
                    turn(4 * g + u, g, u)
            turn(NT, NT // 4, 0)

        def nothing(i, g, u):
            return

        @block.gpsimd
        def _(pool):
            nc.gpsimd.memset(ones[:], 1.0).then_inc(made, 1)

            def lows(i, g, u):
                pool.wait_ge(high, i + 1)
                if not isinstance(i, int) or i >= 4:
                    pool.wait_ge(kept[u], 32 * g)
                nc.gpsimd.tensor_tensor(xl[:, u], xT[:, u], xh[:, u], ALU.subtract).then_inc(low, 1)

            tiles(pool, nothing, lows)

        @block.sync
        def _(sp):
            for half, (w, b) in enumerate((("l1_Wi", "l1_bi"), ("l1_Wf", "l1_bf"))):
                v = io[w].rearrange("(k c p) n -> k p c n", k=3, p=P)
                at = slice(NH * half, NH * half + NH)
                sp.dma_start(wq[:, :, at], v[0]).then_inc(wload, 16)
                for k in range(2):
                    sp.dma_start(wraw[:, k, :, at], v[1 + k]).then_inc(wload, 16)
                sp.dma_start(brow[:, at], row_of(io[b])).then_inc(wload, 16)
            ctx_t = io["ctx"].rearrange("b (c p) t -> (b c) p t", p=P)

            def load(i, g, u):
                if not isinstance(i, int) or i >= 4:
                    sp.wait_ge(c_turned, i - 3)
                sp.dma_start(cx[:, u, :], ctx_t[i]).then_inc(c_in[u], 16)

            def keep(i, g, u):
                b, ct = 2 * g + u // 2, u % 2
                for k, (done, x) in enumerate(((high, xh), (low, xl))):
                    sp.wait_ge(done, i + 1)
                    sp.dma_start(S["xT"][b, k, :, :, ct * P:ct * P + P].rearrange("k p n -> p k n"),
                                 x[:, u].rearrange("p j (c n) -> p (j c) n", c=HC)).then_inc(kept[u], 16)

            tiles(sp, load, keep)
            sp.wait_ge(rows_ready, 1)
            sp.dma_start(S["nm"], nM[:]).then_inc(nM_stored, 16)
            for u in range(4):
                sp.wait_ge(kept[u], 32 * NT // 4)
            sp.wait_ge(nM_stored, 16)

        @block.tensor
        def _(pe):
            def turn(i, g, u):
                for src, ready, count, ps, copied, turned in (
                        (xn[:, u % 2, :], normed, i + 1, ps_q, q_copied, q_turned),
                        (cx[:, u, :], c_in[u], 16 * g + 16, ps_c, c_copied, c_turned)):
                    pe.wait_ge(ready, count)
                    if not isinstance(i, int) or i >= 2:
                        pe.wait_ge(copied, i - 1)
                    for c in range(HC):
                        last = nc.tensor.transpose(ps[:, u % 2, c * P:c * P + P], src[:, c * P:c * P + P], ident[:])
                    last.then_inc(turned, 1)

            def gate(i, g, u):
                if isinstance(i, int) and i == 0:
                    pe.wait_ge(wload, 16 * 8)
                    pe.wait_ge(summed, 1)
                pe.wait_ge(q_copied, i + 1)
                pe.wait_ge(c_copied, i + 1)
                for k, w in enumerate((wq, wkv)):
                    for c in range(HC):
                        last = nc.tensor.matmul(ps_g[:, bass.ds(G2 * i, G2)], xT[:, u, k, c * P:c * P + P], w[:, c, :],
                                                start=(k == 0 and c == 0), stop=(k == 1 and c == HC - 1))
                last.then_inc(gated, 1)

            tiles(pe, turn, gate)
            pe.wait_ge(l_ready, 1)
            for k, src in enumerate((gl, gi)):
                for ct in range(CT):
                    last = nc.tensor.transpose(ps_r[:, k * C + ct * P:k * C + ct * P + P], src[:, ct, :], ident[:])
            last.then_inc(rows_turned, 1)
            pe.wait_ge(rows_ready, 1)
            for k, src in enumerate((a, mx)):
                for ct in range(CT):
                    last = nc.tensor.transpose(ps_b[:, k * C + ct * P:k * C + ct * P + P],
                                               src[:, ct * P:ct * P + P], ident[:])
            last.then_inc(cols, 1)

        @block.scalar
        def _(act):
            def copy_q(i, g, u):
                act.wait_ge(q_turned, i + 1)
                if not isinstance(i, int) or i >= 4:
                    act.wait_ge(gated, i - 3)
                    act.wait_ge(low, i - 3)
                nc.scalar.activation(xT[:, u, 0, :], ps_q[:, u % 2, :], ACT.Copy).then_inc(q_copied, 1)

            tiles(act, copy_q, nothing)
            act.wait_ge(abs_ready, 1)
            nc.scalar.activation(gl[:], ga[:], ACT.Exp, scale=-1.0).then_inc(av, 1)
            act.wait_ge(av, 1)
            nc.scalar.activation(gl[:], gl[:], ACT.Ln, bias=1.0).then_inc(ln_ready, 1)
            act.wait_ge(cols_ready, 1)
            nc.scalar.activation(en[:], acol[:, 1], ACT.Exp, scale=-1.0)

        @block.vector
        def _(dve):
            dve.wait_ge(made, 1)
            dve.wait_ge(wload, 16 * 8)
            nc.vector.tensor_tensor(wkv[:], wraw[:, 0], wraw[:, 1], ALU.add).then_inc(summed, 1)

            def norm(i, g, u):
                if not isinstance(i, int) or i >= 2:
                    dve.wait_ge(q_turned, i - 1)
                nc.vector.tensor_scalar(xn[:, u % 2, :], X[:, bass.ds(i, 1), :].rearrange("p a t -> p (a t)"),
                                        mean[:, bass.ds(i, 1)], rstd[:, bass.ds(i, 1)],
                                        ALU.subtract, ALU.mult).then_inc(normed, 1)

            def copy_c(i, g, u):
                dve.wait_ge(c_turned, i + 1)
                if not isinstance(i, int) or i >= 4:
                    dve.wait_ge(gated, i - 3)
                    dve.wait_ge(low, i - 3)
                    dve.wait_ge(kept[u], 32 * g)
                nc.vector.tensor_copy(xT[:, u, 1, :], ps_c[:, u % 2, :]).then_inc(c_copied, 1)
                dve.wait_ge(c_copied, i + 1)
                dve.wait_ge(q_copied, i + 1)
                nc.vector.tensor_scalar(xh[:, u].bitcast(I32), xT[:, u].bitcast(I32), HIGH, None, ALU.bitwise_and)\
                  .then_inc(high, 1)

            tiles(dve, norm, copy_c)
            dve.wait_ge(gated, NT)
            c = Chain(dve, dv)
            v = ps_g[:].rearrange("p (b c k h) -> p k c b h", b=B, c=CT, k=2)
            for k, dst in enumerate((gi, gf)):
                for ct in range(CT):
                    ins = nc.vector.tensor_tensor(dst[:, ct, :].rearrange("p (b h) -> p b h", b=B), v[:, k, ct],
                                                  brow[:, k * NH:k * NH + NH].unsqueeze(1).broadcast_to([P, B, NH]),
                                                  ALU.add)
            c(ins)
            nc.vector.scalar_tensor_tensor(out=ga[:], in0=gf[:], scalar=-1.0, in1=gf[:],
                                           op0=ALU.mult, op1=ALU.max).then_inc(abs_ready, 1)
            c(nc.vector.tensor_scalar(gf[:], gf[:], 0.0, None, ALU.min))
            dve.wait_ge(ln_ready, 1)
            c(nc.vector.tensor_tensor(gl[:], gf[:], gl[:], ALU.subtract))
            dve.sem_inc(l_ready, 1)
            dve.wait_ge(rows_turned, 1)
            c(nc.vector.tensor_tensor_scan(Fc[:], ones[:], ps_r[:, 0:C], 0.0, ALU.mult, ALU.add))
            c(nc.vector.tensor_tensor(a[:], ps_r[:, C:2 * C], Fc[:], ALU.subtract))
            c(nc.vector.tensor_tensor_scan(M[:], ones[:], a[:], -3.0e38, ALU.mult, ALU.max))
            c(nc.vector.tensor_tensor(mx[:], Fc[:], M[:], ALU.add))
            c(nc.vector.tensor_scalar(nM[:], M[:], -1.0, None, ALU.mult))
            dve.sem_inc(rows_ready, 1)
            dve.wait_ge(cols, 1)
            nc.vector.tensor_copy(acol[:].rearrange("p j c h -> p (j c h)"), ps_b[:]).then_inc(cols_ready, 1)


def mix(nc, io, X, K, S, acol, en):
    gate = K["gate"]
    with ExitStack() as ctx:
        r = Room(nc, ctx, "mx")
        lnb = r.sb("lnb", [P, T])
        cx = r.sb("cx", [P, CT, T])
        qs = r.sb("qs", [3 * DH, 2, NH, C])
        ks = r.sb("ks", [3 * DH, 2, NH, C])
        va = r.sb("va", [P, 2, CT, NH * HW])
        D0 = r.sb("D0", [P, 2, NH, SW])
        D = r.sb("D", [P, 4, SW])
        Cm = r.sb("C", [P, 4, SW])
        hr = r.sb("hr", [P, 2, CT, NH, HW])
        nrm = r.sb("nrm", [P, CT * NH])
        hv = r.sb("hv", [P, CT * NH, DH])
        sq = r.sb("sq", [P, CT * NH, DH])
        st = r.sb("st", [P, CT * NH])
        rs = r.sb("rs", [P, CT * NH])
        ps_s = r.ps("ps_s", [P, 4, 512])
        ps_h = r.ps("ps_h", [P, 2, CT, 512])
        made = r.sem("made")
        ln_in = r.sem("ln_in")
        q_in = [r.sem(f"q_in{u}") for u in range(2)]
        c_in = r.sem("c_in")
        spread = [r.sem(f"spread{u}") for u in range(2)]
        masked = r.sem("masked")
        va_ready = r.sem("va_ready")
        scored = r.sem("scored")
        d_ready = r.sem("d_ready")
        c_ready = r.sem("c_ready")
        mixed = r.sem("mixed")
        h_copied = r.sem("h_copied")
        var_ready = r.sem("var_ready")
        root = r.sem("root")
        df = r.sem("df")
        apart = r.sem("apart")
        block = r.block()

        def batches(eng, batch):
            for n in range(2):
                batch(n, 0, n)
            with eng.Fori(1, B // 2 - 1) as g:
                for u in range(2):
                    batch(2 * g + u, g, u)
            for n in range(B - 2, B):
                batch(n, n // 2, n % 2)

        def past(n, k):
            return not isinstance(n, int) or n >= k

        @block.gpsimd
        def _(pool):
            nc.gpsimd.memset(va[:], 1.0).then_inc(made, 1)
            pool.wait_ge(made, 1)

            def batch(n, g, u):
                pool.wait_ge(c_in, 16 * n + 16)
                if past(n, 2):
                    pool.wait_ge(mixed, NH * n - NH)
                pool.sem_inc(apart, 1)
                nc.gpsimd.tensor_copy(va[:, u, :, :].rearrange("p c (h w) -> p c h w", w=HW)[:, :, :, 0:DH],
                                      cx[:].rearrange("p c (h d) -> p c h d", d=DH)).then_inc(va_ready, 1)
                pool.wait_ge(spread[u], 32 * g + 32)
                pool.sem_inc(apart, 1)
                for lo in (0, C):
                    v = D0[:, u, :, lo:lo + P]
                    last = nc.gpsimd.affine_select(out=v, in_=v, compare_op=ALU.is_ge, fill=MASKED, base=0,
                                                   pattern=[[0, NH], [1, P]], channel_multiplier=-1)
                last.then_inc(masked, 1)

            batches(pool, batch)

        @block.sync
        def _(sp):
            sp.dma_start(lnb[:], row_of(io["l1_ln_scale"])).then_inc(ln_in, 16)
            vc = io["ctx"].rearrange("b (c p) t -> b p c t", p=P)
            rows = S["nm"].rearrange("(b a h) s -> b a (h s)", b=B, a=1)

            def batch(n, g, u):
                if past(n, 2):
                    sp.wait_ge(scored, NH * n - NH)
                x = S["xT"][n]
                for k, (q, c) in enumerate(((0, 0), (1, 0), (0, 1))):
                    for j, (dst, part) in enumerate(((qs, q), (ks, c))):
                        v = x[part, HC * j:HC * j + HC].rearrange("c (h d) s -> d (c h) s", d=DH)
                        sp.dma_start(dst[DH * k:DH * k + DH, u, :, :], v).then_inc(q_in[u], 16)
                if past(n, 2):
                    sp.wait_ge(d_ready, NH * n - NH)
                    sp.sem_inc(apart, 1)
                v = rows[n].broadcast_to([P, NH * C]).rearrange("p (h s) -> p h s", h=NH)
                sp.dma_start(D0[:, u, :, 0:C], v).then_inc(spread[u], 16)
                sp.dma_start(D0[:, u, :, C:SW], v[:, :, P:C]).then_inc(spread[u], 16)
                if past(n, 1):
                    sp.wait_ge(va_ready, n)
                sp.dma_start(cx[:], vc[n]).then_inc(c_in, 16)

            batches(sp, batch)

        @block.tensor
        def _(pe):
            def scores(n, g, u, pair):
                if pair == 0:
                    pe.wait_ge(q_in[u], 96 * g + 96)
                heads = (2 * pair, 2 * pair + 1)
                if past(n, 1) or pair >= 2:
                    pe.wait_ge(c_ready, NH * n + 2 * pair - 2)
                for h in heads:
                    for lo, t in ((P, P), (0, 0)):
                        last = nc.tensor.matmul(ps_s[:, h % 4, lo:lo + C], ks[:, u, h, t:t + P].bitcast(F32R),
                                                qs[:, u, h, :].bitcast(F32R), start=True, stop=True)
                last.then_inc(scored, 2)

            def values(n, g, u, pair):
                if pair == 0:
                    pe.wait_ge(va_ready, n + 1)
                if pair % 4 == 0 and past(n, 1):
                    pe.wait_ge(h_copied, 2 * n - 1 + pair // 4)
                for h in (2 * pair, 2 * pair + 1):
                    pe.wait_ge(c_ready, NH * n + h + 1)
                    at = slice((h % 8) * HW, (h % 8) * HW + HW)
                    v = [va[:, u, ct, h * HW:h * HW + HW] for ct in range(CT)]
                    out, c = ps_h[:, h // 8], Cm[:, h % 4, :]
                    nc.tensor.matmul(out[:, 0, at], c[:, 0:P], v[0], start=True, stop=True)
                    nc.tensor.matmul(out[:, 1, at], c[:, P:C], v[0], start=True, stop=False)
                    nc.tensor.matmul(out[:, 1, at], c[:, C:SW], v[1], start=False, stop=True).then_inc(mixed, 1)

            def batch(n, g, u):
                for pair in range(NH // 2):
                    if pair + 1 < NH // 2:
                        scores(n, g, u, pair + 1)
                    elif not (isinstance(n, int) and n == B - 1):
                        scores(n + 1, g + u, 1 - u, 0)
                    values(n, g, u, pair)

            scores(0, 0, 0, 0)
            batches(pe, batch)

        @block.scalar
        def _(act):
            def batch(n, g, u):
                act.wait_ge(masked, n + 1)
                for h in range(NH):
                    if past(n, 1) or h >= 4:
                        act.wait_ge(c_ready, NH * n + h - 3)
                    bh = NH * n + h
                    nc.scalar.activation(D[:, h % 4, 0:C], D0[:, u, h, 0:C], ACT.Exp, bias=acol[:, 0, 0, bass.ds(bh, 1)])
                    nc.scalar.activation(D[:, h % 4, C:SW], D0[:, u, h, C:SW], ACT.Exp,
                                         bias=acol[:, 0, 1, bass.ds(bh, 1)]).then_inc(d_ready, 1)
                    if h == ROOT_AT and past(n, 1):
                        act.wait_ge(var_ready, n)
                        nc.scalar.activation(rs[:], st[:], ACT.Sqrt).then_inc(root, 1)

            batches(act, batch)
            act.wait_ge(var_ready, B)
            nc.scalar.activation(rs[:], st[:], ACT.Sqrt).then_inc(root, 1)

        @block.vector
        def _(dve):
            wide = [P, CT * NH, DH]

            def copy_half(n, g, u, half):
                dve.wait_ge(mixed, NH * n + 8 * half + 8)
                nc.vector.tensor_copy(hr[:, u, :, 8 * half:8 * half + 8, :].rearrange("p c h w -> p c (h w)"),
                                      ps_h[:, half, :, 0:8 * HW]).then_inc(h_copied, 1)

            def finish(n, g, u, k):
                hh = hr[:, u].rearrange("p c h w -> p (c h) w")
                h2 = hv[:].rearrange("p (c h) d -> p c (h d)", c=CT)
                x = X[:, bass.ds(CT * n, CT), :]
                if k == 0:
                    dve.wait_ge(h_copied, 2 * n + 2)
                if k > 0 or past(n, 1):
                    dve.wait_ge(df, FINISH * n + k)
                if k == 0:
                    ins = nc.vector.scalar_tensor_tensor(out=nrm[:], in0=hh[:, :, DH], scalar=-1.0, in1=hh[:, :, DH],
                                                         op0=ALU.mult, op1=ALU.max)
                elif k == 1:
                    ins = nc.vector.tensor_tensor(nrm[:].rearrange("p (c h) -> p c h", c=CT),
                                                  nrm[:].rearrange("p (c h) -> p c h", c=CT),
                                                  en[:, :, bass.ds(NH * n, NH)], ALU.max)
                elif k == 2:
                    ins = nc.vector.tensor_scalar(nrm[:], nrm[:], LN_EPS, None, ALU.add)
                elif k == 3:
                    ins = nc.vector.reciprocal(nrm[:], nrm[:])
                elif k == 4:
                    ins = nc.vector.tensor_tensor(hv[:], hh[:, :, 0:DH], nrm[:].unsqueeze(2).broadcast_to(wide), ALU.mult)
                elif k == 5:
                    ins = nc.vector.tensor_reduce(st[:], hv[:], AX.X, ALU.add)
                elif k == 6:
                    ins = nc.vector.tensor_scalar(st[:], st[:], 1.0 / DH, None, ALU.mult)
                elif k == 7:
                    ins = nc.vector.tensor_tensor(hv[:], hv[:], st[:].unsqueeze(2).broadcast_to(wide), ALU.subtract)
                elif k == 8:
                    ins = nc.vector.tensor_tensor(sq[:], hv[:], hv[:], ALU.mult)
                elif k == 9:
                    ins = nc.vector.tensor_reduce(st[:], sq[:], AX.X, ALU.add)
                elif k == 10:
                    ins = nc.vector.tensor_scalar(st[:], st[:], 1.0 / DH, LN_EPS, ALU.mult, ALU.add)
                elif k == 11:
                    dve.sem_inc(var_ready, 1)
                    ins = nc.vector.tensor_tensor(h2, h2, lnb[:].unsqueeze(1).broadcast_to([P, CT, T]), ALU.mult)
                elif k == 12:
                    dve.wait_ge(root, n + 1)
                    ins = nc.vector.reciprocal(rs[:], rs[:])
                elif k == 13:
                    ins = nc.vector.tensor_tensor(hv[:], hv[:], rs[:].unsqueeze(2).broadcast_to(wide), ALU.mult)
                elif k == 14:
                    ins = nc.vector.scalar_tensor_tensor(out=x, in0=h2, scalar=gate[:, 1:2], in1=x,
                                                         op0=ALU.mult, op1=ALU.add)
                else:
                    t = bass.ds(CT * n + k - 15, 1)
                    ins = nc.vector.bn_stats(K["bn"][:, t, :].rearrange("p a s -> p (a s)"),
                                             X[:, t, :].rearrange("p a t -> p (a t)"))
                ins.then_inc(df, 1)

            def batch(n, g, u):
                for h in range(NH):
                    dve.wait_ge(scored, NH * n + h // 2 * 2 + 2)
                    dve.wait_ge(d_ready, NH * n + h + 1)
                    if past(n, 1) or h >= 4:
                        dve.wait_ge(mixed, NH * n + h - 3)
                    nc.vector.scalar_tensor_tensor(out=Cm[:, h % 4, :], in0=ps_s[:, h % 4, 0:SW], scalar=DH ** -0.5,
                                                   in1=D[:, h % 4, :], op0=ALU.mult, op1=ALU.mult).then_inc(c_ready, 1)
                    if h == 3 and past(n, 1):
                        copy_half(n - 1, g + u - 1, 1 - u, 1)
                    if h == 11:
                        copy_half(n, g, u, 0)
                    if past(n, 1):
                        for k in FINISH_AT.get(h, ()):
                            finish(n - 1, g + u - 1, 1 - u, k)

            dve.wait_ge(ln_in, 16)
            batches(dve, batch)
            copy_half(B - 1, B // 2 - 1, 1, 1)
            for k in range(FINISH):
                finish(B - 1, B // 2 - 1, 1, k)
            dve.wait_ge(df, FINISH * B)


FINISH = 15 + CT
FINISH_AT = {4: (0,), 5: (1, 2), 6: (3,), 7: (4,), 8: (5,), 9: (6, 7), 10: (8,), 11: (9,), 12: (10, 11), 13: (12,),
             14: (13,), 15: (14, 15, 16)}
ROOT_AT = 14




def dense_ffn(nc, io, S, rowi, pair):
    I = io["f1_w_gate"].shape[1]
    IC = I // P
    TG = 512
    TT = TG // P
    NQ = NTOK // TG
    STEPS = NQ * IC
    PASSES = ((0, 0), (1, 0), (0, 1))
    with ExitStack() as ctx:
        r = Room(nc, ctx, "dn")
        w = r.sb("w", [P, 2, HC, I])
        wd = r.sb("wd", [P, IC, T])
        dT = r.sb("dT", [P, 2, 2, HC, TG])
        wm = r.sb("wm", [P, 2, HC, P])
        dm = r.sb("dm", [P, T])
        hm = r.sb("hm", [P, TG])
        wp = r.sb("wp", [P, 2, 2, 2, HC, P], F32R)
        wdp = r.sb("wdp", [P, 2, 2, T], F32R)
        g = r.sb("g", [P, 2, TG])
        h = r.sb("h", [P, TG])
        hp = r.sb("hp", [P, 2, 2, TG], F32R)
        out = r.sb("out", [P, 2, T])
        ps_g = r.ps("ps_g", [P, 2, 512])
        ps_u = r.ps("ps_u", [P, 2, 512])
        ps_o = r.ps("ps_o", [P, TT, 512])
        zeros = r.sb("zeros", [P, T])
        made = r.sem("made")
        cleared = r.sem("cleared")
        scattered = r.sem("scattered")
        x_in = [r.sem(f"x_in{k}") for k in range(2)]
        w_in = [r.sem(f"w_in{k}") for k in range(4)]
        d_in = [r.sem(f"d_in{k}") for k in range(4)]
        w_masked = r.sem("w_masked")
        d_masked = r.sem("d_masked")
        h_masked = r.sem("h_masked")
        w_high = r.sem("w_high")
        w_low = r.sem("w_low")
        d_high = r.sem("d_high")
        d_low = r.sem("d_low")
        up = r.sem("up")
        acted = r.sem("acted")
        multiplied = r.sem("multiplied")
        h_high = r.sem("h_high")
        h_low = r.sem("h_low")
        down = r.sem("down")
        copied = [r.sem("copied_a"), r.sem("copied_d")]
        stored = [r.sem("stored_a"), r.sem("stored_d")]
        block = r.block()

        def steps(eng, step, apart=0):
            for q in range(NQ):
                if q < apart:
                    for ic in range(IC):
                        step(IC * q + ic, q, ic, ic % 2)
                    continue
                for u in range(2):
                    step(IC * q + u, q, u, u)
                with eng.Fori(1, IC // 2) as i:
                    for u in range(2):
                        step(2 * i + (IC * q + u), q, 2 * i + u, u)

        def past(m, k):
            return not isinstance(m, int) or m >= k

        @block.sync
        def _(sp):
            def load(q):
                if q >= 2:
                    sp.wait_ge(up, IC * (q - 1))
                for k in range(2):
                    sp.dma_start(dT[:, q % 2, k], S["dT"][k][:, :, q * TG:q * TG + TG]).then_inc(x_in[q % 2], 16)

            def weights(k):
                cols = slice(k * I // 4, (k + 1) * I // 4)
                for j, name in enumerate(("f1_w_gate", "f1_w_up")):
                    sp.dma_start(w[:, j, :, cols], io[name].rearrange("(p c) i -> p c i", c=HC)[:, :, cols])\
                      .then_inc(w_in[k], 16)
                part = slice(k * IC // 4, (k + 1) * IC // 4)
                sp.dma_start(wd[:, part, :], io["f1_w_down"].rearrange("(c p) n -> p c n", p=P)[:, part, :])\
                  .then_inc(d_in[k], 16)

            load(0)
            for k in range(4):
                weights(k)
            load(1)
            sp.wait_ge(made, 1)
            clear_sums(sp, S, zeros, cleared)
            for q in range(NQ):
                for t in range(TT):
                    k, n = t % 2, TT // 2 * q + t // 2
                    sp.wait_ge(copied[k], n + 1)
                    sp.dma_start(S["dn"][TT * q + t], out[:, k, :]).then_inc(stored[k], 16)
                if q + 2 < NQ:
                    load(q + 2)
            for k in range(2):
                sp.wait_ge(stored[k], 16 * NQ * TT // 2)
            sp.wait_ge(cleared, 48)

        @block.tensor
        def _(pe):
            def downs(m, u, first, last):
                for part in (h_high, h_low, d_high, d_low):
                    pe.wait_ge(part, m + 1)
                for t in range(TT):
                    for j, (a, b) in enumerate(PASSES):
                        ins = nc.tensor.matmul(ps_o[:, t, :], hp[:, u, a, t * P:t * P + P], wdp[:, u, b, :],
                                               start=(first and j == 0), stop=(last and j == 2))
                ins.then_inc(down, 1)

            def step(m, q, ic, u):
                if isinstance(ic, int) and ic == 0:
                    pe.wait_ge(x_in[q % 2], 32 * (q // 2) + 32)
                pe.wait_ge(w_high, m + 1)
                pe.wait_ge(w_low, m + 1)
                if past(m, 2):
                    pe.wait_ge(multiplied, m - 1)
                for ps, j in ((ps_g, 0), (ps_u, 1)):
                    for c in range(HC):
                        for k, (a, b) in enumerate(PASSES):
                            ins = nc.tensor.matmul(ps[:, u, :], wp[:, u, a, j, c, :],
                                                   dT[:, q % 2, b, c, :].bitcast(F32R),
                                                   start=(c == 0 and k == 0), stop=(c == HC - 1 and k == 2))
                ins.then_inc(up, 1)
                if past(m, 1):
                    if isinstance(ic, int) and ic == 1 and q > 0:
                        for k in range(2):
                            pe.wait_ge(copied[k], TT // 2 * q)
                    downs(m - 1, 1 - u, isinstance(ic, int) and ic == 1, isinstance(ic, int) and ic == 0)

            steps(pe, step)
            downs(STEPS - 1, 1, False, True)

        def copy_out(eng, copy, k, q):
            eng.wait_ge(down, IC * q + IC)
            for j in range(TT // 2):
                n = TT // 2 * q + j
                if n > 0:
                    eng.wait_ge(stored[k], 16 * n)
                copy(out[:, k, :], ps_o[:, 2 * j + k, :]).then_inc(copied[k], 1)

        @block.scalar
        def _(act):
            def copy(dst, src):
                return nc.scalar.activation(dst, src, ACT.Copy)

            def hidden(m, u):
                act.wait_ge(up, m + 1)
                if past(m, 2):
                    act.wait_ge(multiplied, m - 1)
                nc.scalar.activation(g[:, u, :], ps_g[:, u, :], ACT.Gelu_apprx_tanh).then_inc(acted, 1)
                if past(m, 2):
                    act.wait_ge(down, m - 1)
                for masked, high, dst, part in ((d_masked, d_high, wdp, dm), (h_masked, h_high, hp, hm)):
                    act.wait_ge(masked, m + 1)
                    nc.scalar.activation(dst[:, u, 0, :], part[:], ACT.Copy).then_inc(high, 1)

            def step(m, q, ic, u):
                act.wait_ge(w_masked, m + 1)
                if past(m, 2):
                    act.wait_ge(up, m - 1)
                nc.scalar.activation(wp[:, u, 0], wm[:], ACT.Copy).then_inc(w_high, 1)
                if isinstance(ic, int) and ic == 1 and q > 0:
                    copy_out(act, copy, 0, q - 1)
                if past(m, 1):
                    hidden(m - 1, 1 - u)

            steps(act, step)
            hidden(STEPS - 1, 1)
            copy_out(act, copy, 0, NQ - 1)

        @block.vector
        def _(dve):
            def mask(out, src):
                return nc.vector.tensor_scalar(out.bitcast(I32), src.bitcast(I32), HIGH, None, ALU.bitwise_and)

            def hidden(m, u, ic):
                if past(m, 1):
                    dve.wait_ge(d_high, m)
                    dve.wait_ge(d_low, m)
                if isinstance(m, int) and m < IC and m % (IC // 4) == 0:
                    dve.wait_ge(d_in[m * 4 // IC], 16)
                mask(dm[:], wd[:, bass.ds(ic, 1), :].rearrange("p a t -> p (a t)")).then_inc(d_masked, 1)
                dve.wait_ge(acted, m + 1)
                if past(m, 1):
                    dve.wait_ge(h_low, m)
                    dve.wait_ge(h_high, m)
                nc.vector.tensor_tensor(h[:], g[:, u, :], ps_u[:, u, :], ALU.mult).then_inc(multiplied, 1)
                dve.wait_ge(multiplied, m + 1)
                mask(hm[:], h[:]).then_inc(h_masked, 1)
                if past(m, 2):
                    dve.wait_ge(down, m - 1)
                dve.wait_ge(h_masked, m + 1)
                nc.vector.tensor_tensor(hp[:, u, 1, :], h[:], hm[:], ALU.subtract).then_inc(h_low, 1)

            def step(m, q, ic, u):
                if q == 0 and ic % (IC // 4) == 0:
                    dve.wait_ge(w_in[ic * 4 // IC], 32)
                if past(m, 1):
                    dve.wait_ge(w_high, m)
                    dve.wait_ge(w_low, m)
                mask(wm[:], w[:, :, :, bass.ds(P * ic, P)]).then_inc(w_masked, 1)
                if isinstance(ic, int) and ic == 1 and q > 0:
                    copy_out(dve, nc.vector.tensor_copy, 1, q - 1)
                if past(m, 1):
                    hidden(m - 1, 1 - u, IC - 1 if isinstance(ic, int) and ic == 0 else ic - 1)

            steps(dve, step, apart=1)
            hidden(STEPS - 1, 1, IC - 1)
            copy_out(dve, nc.vector.tensor_copy, 1, NQ - 1)

        @block.gpsimd
        def _(pool):
            def scatter(t):
                for k in range(2):
                    pool.indirect_dma_start(
                        out=S["table1"].rearrange("c b w -> (c b) w"),
                        out_offset=bass.IndirectOffsetOnAxis(ap=rowi[:, t, k:k + 1], axis=0),
                        in_=pair[:, t, k, :], in_offset=None, bounds_check=P * BLOCKS1 - 1, oob_is_err=False)\
                        .then_inc(scattered, 16)

            def downs(m, u, ic):
                pool.wait_ge(d_masked, m + 1)
                if past(m, 2):
                    pool.wait_ge(down, m - 1)
                nc.gpsimd.tensor_tensor(wdp[:, u, 1, :], wd[:, bass.ds(ic, 1), :].rearrange("p a t -> p (a t)"),
                                        dm[:], ALU.subtract).then_inc(d_low, 1)

            def step(m, q, ic, u):
                pool.wait_ge(w_masked, m + 1)
                if past(m, 2):
                    pool.wait_ge(up, m - 1)
                nc.gpsimd.tensor_tensor(wp[:, u, 1], w[:, :, :, bass.ds(P * ic, P)], wm[:], ALU.subtract)\
                    .then_inc(w_low, 1)
                if isinstance(ic, int):
                    n = 2 * q + ic
                    for t in range(EARLY + (NT - EARLY) * n // (2 * NQ), EARLY + (NT - EARLY) * (n + 1) // (2 * NQ)):
                        scatter(t)
                if past(m, 1):
                    downs(m - 1, 1 - u, IC - 1 if isinstance(ic, int) and ic == 0 else ic - 1)

            EARLY = 5
            nc.gpsimd.memset(zeros[:], 0.0).then_inc(made, 1)
            for t in range(EARLY):
                scatter(t)
            steps(pool, step)
            downs(STEPS - 1, 1, IC - 1)
            pool.wait_ge(scattered, 16 * 2 * NT)


def ffn1_routes(nc, io, X, K, S, rowi, pair):
    with ExitStack() as outer:
        o = Room(nc, outer, "f1s")
        mean = o.sb("mean", [P, NT])
        rstd = o.sb("rstd", [P, NT])
        row_stats(nc, K, "f1_st", 1e-5, mean, rstd, second=1e-6)
        route1(nc, io, X, K, S, mean, rstd, rowi, pair)


def ffn1(nc, io, K, S, rowi, pair, out):
    gate = K["gate"]
    dense_ffn(nc, io, S, rowi, pair)
    experts(nc, io, S, "f1e", io["f1_we_gate"].shape[2], BLOCKS1, S["table1"], io["f1_we_gate"], io["f1_we_up"],
            io["f1_we_down"], ACT.Gelu_apprx_tanh, io["f1_rn_pre2"], owner=S["owner"])
    with ExitStack() as outer:
        r = Room(nc, outer, "fn")
        X = r.sb("X", [P, NT, T])
        d = r.sb("d", [P, NT, T])
        m = r.sb("m", [P, NT, T])
        m1 = r.sb("m1", [P, 4, T])
        junk = r.sb("junk", [P, 2, T])
        post = r.sb("post", [P, 3, T])
        sq = r.sb("sq", [P, 4, 2, 4])
        rt = r.sb("rt", [P, 4, 2, 4])
        sq2 = r.sb("sq2", [P, NT])
        rt2 = r.sb("rt2", [P, NT])
        d_in = [r.sem(f"d_in{k}") for k in range(4)]
        m_in = [r.sem(f"m_in{k}") for k in range(4)]
        post_in = r.sem("post_in")
        res_in = [r.sem(f"res_in{k}") for k in range(4)]
        m_summed = r.sem("m_summed")
        squared_in = r.sem("squared_in")
        squared_sum = r.sem("squared_sum")
        sized = r.sem("sized")
        sized_sum = r.sem("sized_sum")
        root = r.sem("root")
        root_sum = r.sem("root_sum")
        scaled = r.sem("scaled")
        summed = r.sem("summed")
        last_scaled = r.sem("last_scaled")
        finished = r.sem("finished")
        stored = r.sem("stored")
        dv = r.sem("dv")
        block = r.block()

        GT = 4
        NGR = NT // GT

        def groups(*stages):
            for k in range(NGR + len(stages) - 1):
                for s, stage in enumerate(stages):
                    if 0 <= k - s < NGR:
                        stage(k - s)

        def tiles(k):
            return range(GT * k, GT * k + GT)

        @block.sync
        def _(sp):
            def load(k):
                for i in tiles(k):
                    if k > 0:
                        sp.wait_ge(m_summed, i - 3)
                        sp.wait_ge(squared_in, 2 * i - 6)
                    for dst, src in ((m[:, i, :], S["y0"]), (m1[:, i % 4, :], S["y1"])):
                        sp.dma_start(dst, src[i * P:i * P + P]).then_inc(m_in[i % 4], 16)
                    sp.dma_start(d[:, i, :], S["dn"][i]).then_inc(d_in[i % 4], 16)
                if k == 0:
                    for j, w in enumerate(("f1_rn_post1", "f1_rn_post2", "f1_rn_post")):
                        sp.dma_start(post[:, j, :], row_of(io[w])).then_inc(post_in, 16)
                t = slice(GT * k, GT * k + GT)
                sp.dma_start(X[:, t, :], S["res"][t].rearrange("n p t -> p n t")).then_inc(res_in[k], 16)

            def store(k):
                for i in tiles(k):
                    sp.wait_ge(finished, i + 1)
                    sp.dma_start(out[i], X[:, i, :]).then_inc(stored, 16)

            groups(load)
            groups(store)
            sp.wait_ge(stored, 16 * NT)

        @block.gpsimd
        def _(pool):
            def sum_blocks(k):
                for i in tiles(k):
                    pool.wait_ge(m_in[i % 4], 32 * (i // 4) + 32)
                    nc.gpsimd.tensor_tensor(m[:, i, :], m[:, i, :], m1[:, i % 4, :], ALU.add).then_inc(m_summed, 1)

            def sum_branches(k):
                for i in tiles(k):
                    pool.wait_ge(scaled, 2 * i + 2)
                    nc.gpsimd.tensor_tensor(d[:, i, :], d[:, i, :], m[:, i, :], ALU.add).then_inc(summed, 1)

            groups(sum_blocks, sum_branches)

        @block.scalar
        def _(act):
            def square_in(k):
                for i in tiles(k):
                    act.wait_ge(m_summed, i + 1)
                    if i > 0:
                        act.wait_ge(squared_in, 2 * i)
                    nc.scalar.activation(junk[:, 0, :], m[:, i, :], ACT.Square, accum_out=sq[:, k, 1, i % GT:i % GT + 1])\
                      .then_inc(squared_in, 1)
                    act.wait_ge(d_in[i % 4], 16 * (i // 4) + 16)
                    act.wait_ge(squared_in, 2 * i + 1)
                    nc.scalar.activation(junk[:, 0, :], d[:, i, :], ACT.Square, accum_out=sq[:, k, 0, i % GT:i % GT + 1])\
                      .then_inc(squared_in, 1)
                act.wait_ge(sized, k + 1)
                nc.scalar.activation(rt[:, k], rt[:, k], ACT.Sqrt).then_inc(root, 1)

            def square_sum(k):
                for i in tiles(k):
                    act.wait_ge(summed, i + 1)
                    if i > 0:
                        act.wait_ge(squared_sum, i)
                    nc.scalar.activation(junk[:, 1, :], d[:, i, :], ACT.Square, accum_out=sq2[:, i:i + 1])\
                      .then_inc(squared_sum, 1)
                act.wait_ge(sized_sum, k + 1)
                t = slice(GT * k, GT * k + GT)
                nc.scalar.activation(rt2[:, t], rt2[:, t], ACT.Sqrt).then_inc(root_sum, 1)

            groups(square_in, square_sum)

        @block.vector
        def _(dve):
            c = Chain(dve, dv)
            dve.wait_ge(post_in, 48)
            c(nc.vector.tensor_scalar(post[:, 2, :], post[:, 2, :], gate[:, 3:4], None, ALU.mult))

            def norm_branches(k):
                dve.wait_ge(squared_in, 2 * GT * (k + 1))
                c(nc.vector.tensor_scalar(rt[:, k], sq[:, k], 1.0 / T, RMS_EPS, ALU.mult, ALU.add))
                dve.sem_inc(sized, 1)
                dve.wait_ge(root, k + 1)
                c(nc.vector.reciprocal(rt[:, k], rt[:, k]))
                for i in tiles(k):
                    for j, v in enumerate((d, m)):
                        nc.vector.scalar_tensor_tensor(out=v[:, i, :], in0=v[:, i, :],
                                                       scalar=rt[:, k, j, i % GT:i % GT + 1],
                                                       in1=post[:, j, :], op0=ALU.mult, op1=ALU.mult).then_inc(scaled, 1)

            def norm_sum(k):
                t = slice(GT * k, GT * k + GT)
                dve.wait_ge(squared_sum, GT * (k + 1))
                c(nc.vector.tensor_scalar(rt2[:, t], sq2[:, t], 1.0 / T, RMS_EPS, ALU.mult, ALU.add))
                dve.sem_inc(sized_sum, 1)
                dve.wait_ge(root_sum, k + 1)
                c(nc.vector.reciprocal(rt2[:, t], rt2[:, t]))
                dve.wait_ge(res_in[k], 16)
                for i in tiles(k):
                    nc.vector.scalar_tensor_tensor(out=d[:, i, :], in0=d[:, i, :], scalar=rt2[:, i:i + 1],
                                                   in1=post[:, 2, :], op0=ALU.mult, op1=ALU.mult).then_inc(last_scaled, 1)
                    dve.wait_ge(last_scaled, i + 1)
                    nc.vector.tensor_tensor(X[:, i, :], X[:, i, :], d[:, i, :], ALU.add).then_inc(finished, 1)

            groups(norm_branches, norm_sum)


RMS_EPS = 1e-6

BLOCKS1 = (2 * NTOK - 8) // P + 8


def scratch(nc):
    d = {}
    def dram(name, shape, dt=F32):
        d[name] = nc.dram_tensor(f"scr_{name}", shape, dt, kind="Internal").ap()
    dram("qs", [NT, 3, P, T], BF16)
    dram("ks", [NT, 3, P, T], BF16)
    dram("mq", [B, 9, T], BF16)
    dram("mk", [B, 12, T], BF16)
    dram("mx", [4, 3, GH * HC, P], BF16)
    dram("xg", [NTOK + P, T])
    dram("y0", [NTOK + P, T])
    dram("y1", [NTOK + P, T])
    dram("table0", [P, 64, 2], I32)
    dram("nm", [B * NH, C])
    dram("xT", [B, 2, 2 * HC, P, C])
    dram("table1", [P, BLOCKS1, 2], I32)
    dram("owner", [1, BLOCKS1], I32)
    dram("dT", [2, P, HC, NTOK])
    dram("res", [NT, P, T])
    dram("dn", [NT, P, T])
    return d


def program(nc, io, out):
    with ExitStack() as ctx:
        K = {"ident": ctx.enter_context(nc.sbuf_tensor("ident", [P, P], F32)),
             "gate": ctx.enter_context(nc.sbuf_tensor("gate", [P, 4], F32)),
             "bn": ctx.enter_context(nc.sbuf_tensor("bn", [P, NT, 6], F32)),
             "g_xattn": io["g_xattn"], "g_ffn": io["g_ffn"]}
        rowi = ctx.enter_context(nc.sbuf_tensor("rowi", [P, NT, 2], I32))
        pair = ctx.enter_context(nc.sbuf_tensor("pair", [P, NT, 2, 2], I32))
        S = scratch(nc)
        with ExitStack() as inner:
            X = inner.enter_context(nc.sbuf_tensor("residual", [P, NT, T], F32))
            start(nc, io["x"].rearrange("b (c p) t -> (b c) p t", p=P), io["mask"].rearrange("b a t -> (b a) t"), X, K, S)
            attention(nc, io, X, K, S)
            moe0(nc, io, X, K, S)
            mlstm(nc, io, X, K, S)
            ffn1_routes(nc, io, X, K, S, rowi, pair)
        ffn1(nc, io, K, S, rowi, pair, out.rearrange("b (c p) t -> (b c) p t", p=P))


_NAMES = {
    "x": "x", "ctx": "ctx_2048", "mask": "mask_Bx1x2048_fk1", "g_xattn": "g_xattn", "g_ffn": "g_ffn",
    "Wq": "L0_xattn_Wq", "bq": "L0_xattn_bq", "Wk": "L0_xattn_Wk", "bk": "L0_xattn_bk", "Wv": "L0_xattn_Wv",
    "bv": "L0_xattn_bv", "m0_gate_w": "L0_ffn_gate_w", "m0_wg": "L0_ffn_wg", "m0_wu": "L0_ffn_wu",
    "m0_wd": "L0_ffn_wd", "l1_Wi": "L1_xattn_Wi", "l1_bi": "L1_xattn_bi", "l1_Wf": "L1_xattn_Wf",
    "l1_bf": "L1_xattn_bf", "l1_ln_scale": "L1_xattn_ln_scale", "f1_rn_pre1": "L1_ffn_rn_pre1",
    "f1_rn_pre2": "L1_ffn_rn_pre2", "f1_rn_post1": "L1_ffn_rn_post1", "f1_rn_post2": "L1_ffn_rn_post2",
    "f1_rn_post": "L1_ffn_rn_post", "f1_w_gate": "L1_ffn_w_gate", "f1_w_up": "L1_ffn_w_up",
    "f1_w_down": "L1_ffn_w_down", "f1_router_w": "L1_ffn_router_w", "f1_router_scale": "L1_ffn_router_scale",
    "f1_per_expert_scale": "L1_ffn_per_expert_scale", "f1_we_gate": "L1_ffn_we_gate",
    "f1_we_up": "L1_ffn_we_up", "f1_we_down": "L1_ffn_we_down",
}


def kernel(**inputs):
    import numpy as _np
    import concourse.bacc as _bacc
    from concourse import mybir as _mybir
    from concourse.bass_utils import run_bass_kernel_spmd as _run

    nc = _bacc.Bacc("TRN2", target_bir_lowering=False, num_devices=1)
    arrays, io = {}, {}
    for short, name in _NAMES.items():
        a = _np.ascontiguousarray(inputs[name])
        arrays[f"in_{name}"] = a
        io[short] = nc.dram_tensor(f"in_{name}", a.shape, _mybir.dt.from_np(a.dtype), kind="ExternalInput").ap()
    out = nc.dram_tensor("out_0", (B, C, T), F32, kind="ExternalOutput").ap()
    program(nc, io, out)
    r = _run(nc, [arrays], core_ids=[0])
    return r.results[0]["out_0"]
```
